# Optimizing a Trainium2 kernel written in Bass

```python
import numpy as np
import jax
import jax.numpy as jnp

def _softmax(x, axis=-1):
    return jax.nn.softmax(x, axis=axis)

def _gelu(x):
    return jax.nn.gelu(x, approximate=True)

def _silu(x):
    return jax.nn.silu(x)

def _sigmoid(x):
    return jax.nn.sigmoid(x)

def _layernorm(x, axis=-1, eps=1e-05):
    m = jnp.mean(x, axis=axis, keepdims=True)
    v = jnp.var(x, axis=axis, keepdims=True)
    return (x - m) / jnp.sqrt(v + eps)

def _scatter_add(tgt, idx, src, axis=0):
    return tgt.at[idx].add(src)

def _segment_sum(src, seg, n):
    return jax.ops.segment_sum(src, seg, n)
kernel_name = 'mk_gnn_preln_d2_gnn_r32_8028fa'

def setup_inputs(seed: int=0):
    np.random.seed(seed)
    _w = jnp.asarray

    def _rec_inputs():
        import jax
        import jax.numpy as jnp
        _gk = jax.random.key(seed)
        x = -0.000202 + 1 * jax.random.normal(jax.random.fold_in(_gk, 1), (3125, 128), jnp.float32)
        src = jax.random.randint(jax.random.fold_in(_gk, 2), (50000,), 0, 3125, jnp.int32)
        dst = jnp.minimum((3125 * jax.random.uniform(jax.random.fold_in(_gk, 3), (50000,)) ** 2.0).astype(jnp.int32), 99999)
        _o = jnp.argsort(dst, stable=True)
        src = src[_o]
        dst = dst[_o]
        edge_attr_128 = -5.16925e-05 + 1.00005 * jax.random.normal(jax.random.fold_in(_gk, 12), (50000, 128), jnp.float32)
        edge_type_6 = jax.random.randint(jax.random.fold_in(_gk, 14), (50000,), 0, 6, jnp.int32)
        node_type_3 = jax.random.randint(jax.random.fold_in(_gk, 15), (3125,), 0, 3, jnp.int32)
        return (x, src, dst, edge_attr_128, edge_type_6, node_type_3)
    x, src, dst, edge_attr_128, edge_type_6, node_type_3 = _rec_inputs()

    def _L0_gnn_setup():
        import jax, jax.numpy as jnp
        import numpy as np
        N = 50000
        E = 12500
        D = 128
        H = 4
        DH = 32
        T = 3
        R = 6
        L = 2
        EPS = 1e-05

        def typed_linear(x, types, W):
            out = x @ W[0]
            for t in range(1, W.shape[0]):
                out = jnp.where((types == t)[:, None], x @ W[t], out)
            return out

        def edge_typed(x, etype, W):
            out = jnp.einsum('ehd,hdo->eho', x, W[:, 0])
            for r in range(1, W.shape[1]):
                out = jnp.where((etype == r)[:, None, None], jnp.einsum('ehd,hdo->eho', x, W[:, r]), out)
            return out

        def layer_norm(x, g, b):
            mu = x.mean(-1, keepdims=True)
            var = ((x - mu) ** 2).mean(-1, keepdims=True)
            return (x - mu) * jax.lax.rsqrt(var + EPS) * g + b

        def hgt_layer(x, src, dst, ntype, etype, Wk, Wq, Wv, Wa, W_att, W_msg, pri, skip):
            n = x.shape[0]
            k = typed_linear(x, ntype, Wk).reshape(n, H, DH)
            q = typed_linear(x, ntype, Wq).reshape(n, H, DH)
            v = typed_linear(x, ntype, Wv).reshape(n, H, DH)
            kw = edge_typed(k[src], etype, W_att)
            mv = edge_typed(v[src], etype, W_msg)
            a = (kw * q[dst]).sum(-1) * pri.T[etype] / np.sqrt(DH).astype(np.float32)
            mx = jax.lax.stop_gradient(jax.ops.segment_max(a, dst, num_segments=n))
            ex = jnp.exp(a - mx[dst])
            den = jax.ops.segment_sum(ex, dst, num_segments=n)
            att = ex / den[dst]
            agg = jax.ops.segment_sum(att[:, :, None] * mv, dst, num_segments=n)
            h_a = typed_linear(agg.reshape(n, H * DH), ntype, Wa)
            sk = jax.nn.sigmoid(skip)[ntype][:, None]
            return h_a * sk + x * (1.0 - sk)
        key = jax.random.key(seed)
        ks = jax.random.split(key, 12)
        s = D ** (-0.5)
        sh = DH ** (-0.5)
        return {'h': jax.random.normal(ks[0], (N, D), jnp.float32), 'src': jax.random.randint(ks[1], (E,), 0, N), 'dst': jax.random.randint(ks[2], (E,), 0, N), 'ntype': jnp.sort(jax.random.randint(ks[3], (N,), 0, T)), 'etype': jnp.sort(jax.random.randint(ks[4], (E,), 0, R)), 'Wk': jax.random.normal(ks[5], (L, T, D, D), jnp.float32) * s, 'Wq': jax.random.normal(ks[6], (L, T, D, D), jnp.float32) * s, 'Wv': jax.random.normal(ks[7], (L, T, D, D), jnp.float32) * s, 'Wa': jax.random.normal(ks[8], (L, T, D, D), jnp.float32) * s, 'W_att': jax.random.normal(ks[9], (L, H, R, DH, DH), jnp.float32) * sh, 'W_msg': jax.random.normal(ks[10], (L, H, R, DH, DH), jnp.float32) * sh, 'pri': jnp.ones((L, H, R), jnp.float32), 'skip': jnp.ones((L, T), jnp.float32), 'ln_g': jnp.ones((L, D), jnp.float32), 'ln_b': jnp.zeros((L, D), jnp.float32), 'agg_w': jnp.ones((L,), jnp.float32), 'agg_g': jnp.ones((D,), jnp.float32), 'agg_b': jnp.zeros((D,), jnp.float32)}
    _L0_gnn_all = _L0_gnn_setup()
    _L0_gnn_in = {k: v for k, v in _L0_gnn_all.items() if k in ('Wk', 'Wq', 'Wv', 'Wa', 'W_att', 'W_msg', 'pri', 'skip', 'ln_g', 'ln_b', 'agg_w', 'agg_g', 'agg_b')}
    del _L0_gnn_all

    def _L1_gnn_setup():
        import jax, jax.numpy as jnp
        import numpy as np
        N, E, H, NH, HD = (50000, 25000, 128, 8, 16)

        def _layernorm(x, g, b, eps=1e-05):
            mu = jnp.mean(x, axis=-1, keepdims=True)
            var = jnp.mean(jnp.square(x - mu), axis=-1, keepdims=True)
            return (x - mu) * jax.lax.rsqrt(var + eps) * g + b
        key = jax.random.key(seed)
        ks = jax.random.split(key, 24)
        w = lambda k, shape, s=0.05: jax.random.normal(k, shape, jnp.float32) * s
        return {'x': jax.random.normal(ks[0], (N, H), jnp.float32), 'edge_index': jax.random.randint(ks[1], (2, E), 0, N, dtype=jnp.int64), 'curv': jax.random.normal(ks[2], (E, H), jnp.float32), 'Wq': w(ks[3], (H, H)), 'bq': jnp.zeros((H,), jnp.float32), 'Wk': w(ks[4], (H, H)), 'bk': jnp.zeros((H,), jnp.float32), 'Wv': w(ks[5], (H, H)), 'bv': jnp.zeros((H,), jnp.float32), 'Wo': w(ks[6], (H, H)), 'bo': jnp.zeros((H,), jnp.float32), 'Wc': w(ks[7], (H, NH)), 'bc': jnp.zeros((NH,), jnp.float32), 'W1': w(ks[8], (H, 4 * H)), 'b1': jnp.zeros((4 * H,), jnp.float32), 'W2': w(ks[9], (4 * H, H)), 'b2': jnp.zeros((H,), jnp.float32), 'g1': jnp.ones((H,), jnp.float32), 'be1': jnp.zeros((H,), jnp.float32), 'g2': jnp.ones((H,), jnp.float32), 'be2': jnp.zeros((H,), jnp.float32)}
    _L1_gnn_all = _L1_gnn_setup()
    _L1_gnn_in = {k: v for k, v in _L1_gnn_all.items() if k in ('Wq', 'bq', 'Wk', 'bk', 'Wv', 'bv', 'Wo', 'bo', 'Wc', 'bc', 'W1', 'b1', 'W2', 'b2', 'g1', 'be1', 'g2', 'be2')}
    del _L1_gnn_all
    return {'x': x, 'src': src, 'dst': dst, 'edge_attr_128': edge_attr_128, 'edge_type_6': edge_type_6, 'node_type_3': node_type_3, 'L0_gnn_Wk': _L0_gnn_in['Wk'], 'L0_gnn_Wq': _L0_gnn_in['Wq'], 'L0_gnn_Wv': _L0_gnn_in['Wv'], 'L0_gnn_Wa': _L0_gnn_in['Wa'], 'L0_gnn_W_att': _L0_gnn_in['W_att'], 'L0_gnn_W_msg': _L0_gnn_in['W_msg'], 'L0_gnn_pri': _L0_gnn_in['pri'], 'L0_gnn_skip': _L0_gnn_in['skip'], 'L0_gnn_ln_g': _L0_gnn_in['ln_g'], 'L0_gnn_ln_b': _L0_gnn_in['ln_b'], 'L0_gnn_agg_w': _L0_gnn_in['agg_w'], 'L0_gnn_agg_g': _L0_gnn_in['agg_g'], 'L0_gnn_agg_b': _L0_gnn_in['agg_b'], 'L1_gnn_Wq': _L1_gnn_in['Wq'], 'L1_gnn_bq': _L1_gnn_in['bq'], 'L1_gnn_Wk': _L1_gnn_in['Wk'], 'L1_gnn_bk': _L1_gnn_in['bk'], 'L1_gnn_Wv': _L1_gnn_in['Wv'], 'L1_gnn_bv': _L1_gnn_in['bv'], 'L1_gnn_Wo': _L1_gnn_in['Wo'], 'L1_gnn_bo': _L1_gnn_in['bo'], 'L1_gnn_Wc': _L1_gnn_in['Wc'], 'L1_gnn_bc': _L1_gnn_in['bc'], 'L1_gnn_W1': _L1_gnn_in['W1'], 'L1_gnn_b1': _L1_gnn_in['b1'], 'L1_gnn_W2': _L1_gnn_in['W2'], 'L1_gnn_b2': _L1_gnn_in['b2'], 'L1_gnn_g1': _L1_gnn_in['g1'], 'L1_gnn_be1': _L1_gnn_in['be1'], 'L1_gnn_g2': _L1_gnn_in['g2'], 'L1_gnn_be2': _L1_gnn_in['be2']}

def reference(x, src, dst, edge_attr_128, edge_type_6, node_type_3, L0_gnn_Wk, L0_gnn_Wq, L0_gnn_Wv, L0_gnn_Wa, L0_gnn_W_att, L0_gnn_W_msg, L0_gnn_pri, L0_gnn_skip, L0_gnn_ln_g, L0_gnn_ln_b, L0_gnn_agg_w, L0_gnn_agg_g, L0_gnn_agg_b, L1_gnn_Wq, L1_gnn_bq, L1_gnn_Wk, L1_gnn_bk, L1_gnn_Wv, L1_gnn_bv, L1_gnn_Wo, L1_gnn_bo, L1_gnn_Wc, L1_gnn_bc, L1_gnn_W1, L1_gnn_b1, L1_gnn_W2, L1_gnn_b2, L1_gnn_g1, L1_gnn_be1, L1_gnn_g2, L1_gnn_be2):
    import jax
    import jax.numpy as jnp

    def _L0_gnn_ref(h, src, dst, ntype, etype, Wk, Wq, Wv, Wa, W_att, W_msg, pri, skip, ln_g, ln_b, agg_w, agg_g, agg_b):
        import jax, jax.numpy as jnp
        import numpy as np
        N = 50000
        E = 12500
        D = 128
        H = 4
        DH = 32
        T = 3
        R = 6
        L = 2
        EPS = 1e-05

        def typed_linear(x, types, W):
            out = x @ W[0]
            for t in range(1, W.shape[0]):
                out = jnp.where((types == t)[:, None], x @ W[t], out)
            return out

        def edge_typed(x, etype, W):
            out = jnp.einsum('ehd,hdo->eho', x, W[:, 0])
            for r in range(1, W.shape[1]):
                out = jnp.where((etype == r)[:, None, None], jnp.einsum('ehd,hdo->eho', x, W[:, r]), out)
            return out

        def layer_norm(x, g, b):
            mu = x.mean(-1, keepdims=True)
            var = ((x - mu) ** 2).mean(-1, keepdims=True)
            return (x - mu) * jax.lax.rsqrt(var + EPS) * g + b

        def hgt_layer(x, src, dst, ntype, etype, Wk, Wq, Wv, Wa, W_att, W_msg, pri, skip):
            n = x.shape[0]
            k = typed_linear(x, ntype, Wk).reshape(n, H, DH)
            q = typed_linear(x, ntype, Wq).reshape(n, H, DH)
            v = typed_linear(x, ntype, Wv).reshape(n, H, DH)
            kw = edge_typed(k[src], etype, W_att)
            mv = edge_typed(v[src], etype, W_msg)
            a = (kw * q[dst]).sum(-1) * pri.T[etype] / np.sqrt(DH).astype(np.float32)
            mx = jax.lax.stop_gradient(jax.ops.segment_max(a, dst, num_segments=n))
            ex = jnp.exp(a - mx[dst])
            den = jax.ops.segment_sum(ex, dst, num_segments=n)
            att = ex / den[dst]
            agg = jax.ops.segment_sum(att[:, :, None] * mv, dst, num_segments=n)
            h_a = typed_linear(agg.reshape(n, H * DH), ntype, Wa)
            sk = jax.nn.sigmoid(skip)[ntype][:, None]
            return h_a * sk + x * (1.0 - sk)
        x = h
        outs = []
        for l in range(L):
            ho = hgt_layer(x, src, dst, ntype, etype, Wk[l], Wq[l], Wv[l], Wa[l], W_att[l], W_msg[l], pri[l], skip[l])
            x = layer_norm(x + ho, ln_g[l], ln_b[l])
            outs.append(x)
        w = jax.nn.softmax(agg_w)
        mixed = sum((w[i] * outs[i] for i in range(L)))
        return layer_norm(mixed, agg_g, agg_b)

    def _L1_gnn_ref(x, edge_index, curv, Wq, bq, Wk, bk, Wv, bv, Wo, bo, Wc, bc, W1, b1, W2, b2, g1, be1, g2, be2):
        import jax, jax.numpy as jnp
        import numpy as np
        N, E, H, NH, HD = (50000, 25000, 128, 8, 16)

        def _layernorm(x, g, b, eps=1e-05):
            mu = jnp.mean(x, axis=-1, keepdims=True)
            var = jnp.mean(jnp.square(x - mu), axis=-1, keepdims=True)
            return (x - mu) * jax.lax.rsqrt(var + eps) * g + b
        num_nodes = x.shape[0]
        src, tgt = (edge_index[0], edge_index[1])
        x_norm = _layernorm(x, g1, be1)
        q = (x_norm @ Wq + bq).reshape(num_nodes, NH, HD)
        k = (x_norm @ Wk + bk).reshape(num_nodes, NH, HD)
        v = (x_norm @ Wv + bv).reshape(num_nodes, NH, HD)
        scores = jnp.einsum('ehd,ehd->eh', q[src], k[tgt]) / np.sqrt(HD).astype(np.float32)
        scores = scores + (curv @ Wc + bc)
        smax = jax.ops.segment_max(scores, tgt, num_segments=num_nodes)
        p = jnp.exp(scores - smax[tgt])
        ssum = jax.ops.segment_sum(p, tgt, num_segments=num_nodes)
        probs = p / ssum[tgt]
        messages = (probs[:, :, None] * v[tgt]).reshape(scores.shape[0], -1)
        out = jnp.zeros_like(x).at[src].add(messages)
        out = out @ Wo + bo
        x = x + out
        x_norm2 = _layernorm(x, g2, be2)
        ffn_out = jax.nn.relu(x_norm2 @ W1 + b1) @ W2 + b2
        return x + ffn_out
    edge_index = jnp.stack([src, dst])
    h = jnp.maximum(_layernorm(x, axis=-1), 0.0)
    x = x + _L0_gnn_ref(h, src, dst, node_type_3, edge_type_6, L0_gnn_Wk, L0_gnn_Wq, L0_gnn_Wv, L0_gnn_Wa, L0_gnn_W_att, L0_gnn_W_msg, L0_gnn_pri, L0_gnn_skip, L0_gnn_ln_g, L0_gnn_ln_b, L0_gnn_agg_w, L0_gnn_agg_g, L0_gnn_agg_b)
    h = jnp.maximum(_layernorm(x, axis=-1), 0.0)
    x = x + _L1_gnn_ref(h, edge_index, edge_attr_128, L1_gnn_Wq, L1_gnn_bq, L1_gnn_Wk, L1_gnn_bk, L1_gnn_Wv, L1_gnn_bv, L1_gnn_Wo, L1_gnn_bo, L1_gnn_Wc, L1_gnn_bc, L1_gnn_W1, L1_gnn_b1, L1_gnn_W2, L1_gnn_b2, L1_gnn_g1, L1_gnn_be1, L1_gnn_g2, L1_gnn_be2)
    return x

_drawn_inputs = setup_inputs


def setup_inputs(seed=0):
    import zlib

    import numpy as np

    out = dict(_drawn_inputs(seed))
    spreads = {'L0_gnn_pri': (1.0, 0.6),
     'L0_gnn_skip': (1.0, 0.6),
     'L0_gnn_ln_g': (1.0, 0.2),
     'L0_gnn_ln_b': (0.0, 0.1),
     'L0_gnn_agg_w': (1.0, 0.6),
     'L0_gnn_agg_g': (1.0, 0.2),
     'L0_gnn_agg_b': (0.0, 0.1),
     'L1_gnn_bq': (0.0, 0.8),
     'L1_gnn_bk': (0.0, 0.8),
     'L1_gnn_bv': (0.0, 0.277),
     'L1_gnn_bo': (0.0, 0.1),
     'L1_gnn_bc': (0.0, 0.8),
     'L1_gnn_b1': (0.0, 0.282),
     'L1_gnn_b2': (0.0, 0.1),
     'L1_gnn_g1': (1.0, 0.6),
     'L1_gnn_be1': (0.0, 0.586),
     'L1_gnn_g2': (1.0, 0.2),
     'L1_gnn_be2': (0.0, 0.45)}
    factors = {'L1_gnn_Wq': 3.255, 'L1_gnn_Wk': 3.277}
    for name, (base, spread) in spreads.items():
        noise = np.random.default_rng([zlib.crc32(name.encode()), seed]).standard_normal(out[name].shape)
        drawn = base * np.exp(spread * noise) if base else spread * noise
        out[name] = jnp.asarray(drawn.astype(out[name].dtype))
    for name, factor in factors.items():
        out[name] = (out[name] * factor).astype(out[name].dtype)
    return out
```

```python
from contextlib import ExitStack

import numpy as np

import concourse.bass as bass
from concourse import mybir
from concourse.alu_op_type import AluOpType as ALU

F32 = mybir.dt.float32
BF16 = mybir.dt.bfloat16
I32 = mybir.dt.int32
ACT = mybir.ActivationFunctionType
X = mybir.AxisListType.X

P = 128
D = 128
NODES, EDGES = 3125, 50000
BLOCKS = -(-NODES // P)
NP = BLOCKS * P
CH = 7
TILES = 392
EP = TILES * P
CHUNKS = TILES // CH
PAIRS = CHUNKS // 2
RING = 8
STEPS = TILES + BLOCKS - 1
REC = 12
TYPES, RELS, LAYERS = 3, 6, 2
HEADS0, HEADS1 = 4, 8
MSG = 132
LO, HI = 64, NP // 64
BIG = 1.0e30
EPS = 1e-5
HID = 4 * D
ROWS = ["ln_g0", "ln_g1", "ln_b0", "ln_b1", "agg_g", "agg_b", "bq", "bk", "bv", "bo", "b2", "g1", "be1", "g2", "be2"]
SCAN_LEN = 2 * CH
SCANS = TILES // SCAN_LEN
SCAN_ROWS = SCANS * HEADS0


def spread(ap, axis, n):
    shape = list(ap.shape)
    shape.insert(axis, n)
    return ap.unsqueeze(axis).to_broadcast(shape)


class Chain:

    def __init__(self, eng, done):
        self.eng, self.done, self.base, self.n = eng, done, 0, 0

    def __call__(self, ins):
        self.n += 1
        ins.then_inc(self.done, 1)
        self.eng.wait_ge(self.done, self.base + self.n)

    def enter(self, i, per):
        if self.n or not isinstance(self.base, int):
            self.start = self.base + self.n
        else:
            self.start = self.base
        self.base, self.n, self.per = self.start + i * per, 0, per

    def leave(self, trips):
        assert self.n == self.per
        self.base, self.n = self.start + trips * self.per, 0


class Phase:

    def __init__(self, nc, name):
        self.nc, self.name, self.stack, self.sems = nc, name, ExitStack(), []

    def __enter__(self):
        return self

    def __exit__(self, *a):
        self.stack.close()
        self.nc.clear_and_free_semaphores(self.sems)
        self.nc.all_engine_barrier()

    def sb(self, name, shape, dt=F32):
        return self.stack.enter_context(self.nc.sbuf_tensor(f"{self.name}_{name}", shape, dt))

    def ps(self, name, shape, dt=F32):
        return self.stack.enter_context(self.nc.psum_tensor(f"{self.name}_{name}", shape, dt))

    def sem(self, name):
        self.sems.append(self.nc.alloc_semaphore(f"{self.name}_{name}"))
        return self.sems[-1]

    def block(self):
        return self.nc.Block()


def load_inputs(nc, g):
    with Phase(nc, "load") as p:
        loaded, made, expd = p.sem("loaded"), p.sem("made"), p.sem("expd")
        ntype = p.sb("ntype", [P, BLOCKS], I32)
        ecols = p.sb("ecols", [P, 3, TILES], I32)
        skip = p.sb("skip", [P, LAYERS * TYPES])
        skipe = p.sb("skipe", [P, LAYERS * TYPES])
        aggw = p.sb("aggw", [P, 2])
        small = p.sb("small", [P, 8])
        ntf = p.sb("ntf", [P, BLOCKS])
        pri = p.sb("pri", [P, LAYERS * RELS])
        items = [
            (ntype[:], g.ins["ntype"]),
            (ecols[:], g.ins["edge_cols"].rearrange("p (a t) -> p a t", a=3)), (g.ident[:], g.ins["c_ident"]),
            (g.tri[:], g.ins["c_tri"]), (g.iota[:], g.ins["c_iota"]), (g.shift[:], g.ins["c_shift"]),
            (g.steprow[:], g.ins["c_step"]), (g.wtyped[:], g.ins["w_typed"]), (g.wrel[:], g.ins["w_rel"]), (g.wqkv[:], g.ins["w_qkv"]),
            (g.wo[:], g.ins["w_o"]), (g.w1[:], g.ins["w_1"]), (g.w2[:], g.ins["w_2"]), (g.wc[:], g.ins["w_c"]), (g.b1[:], g.ins["b_1"]),
            (g.rows[:], g.ins["b_rows"]), (g.bc[:], g.ins["b_c"]), (skip[:], g.ins["b_skip"]), (aggw[:], g.ins["b_aggw"]), (pri[:], g.ins["b_pri"]),
        ]
        with p.block() as block:
            @block.sync
            def _(sp):
                for dst, src in items:
                    sp.dma_start(dst, src).then_inc(loaded, 16)

            @block.scalar
            def _(act):
                act.wait_ge(loaded, 16 * len(items))
                nc.scalar.activation(skipe[:], skip[:], ACT.Exp, scale=-1.0).then_inc(expd, 1)
                act.wait_ge(made, 2)
                nc.scalar.activation(small[:, 4:6], small[:, 2:4], ACT.Exp, accum_out=small[:, 6:7]).then_inc(expd, 1)

            @block.vector
            def _(dve):
                ch = Chain(dve, made)
                dve.wait_ge(loaded, 16 * len(items))
                v = nc.vector
                ch(v.tensor_tensor(small[:, 0:1], aggw[:, 0:1], aggw[:, 1:2], ALU.max))
                ch(v.tensor_scalar(small[:, 2:4], aggw[:], small[:, 0:1], None, ALU.subtract))
                ch(v.memset(g.ones_bf[:], 1.0))
                ch(v.memset(g.ones[:], 1.0))
                ch(v.memset(g.rec[:, :, 3:4], 0.0))
                ch(v.tensor_copy(g.tri_bf[:], g.tri[:]))
                for a in range(3):
                    ch(v.tensor_copy(g.rec[:, :, a], ecols[:, a, :]))
                ch(v.tensor_copy(ntf[:], ntype[:]))
                for t in range(TYPES):
                    ch(v.tensor_single_scalar(g.mask[:, t, :], ntf[:], float(t), ALU.is_equal))
                dve.wait_ge(expd, 1)
                ch(v.tensor_scalar_add(skip[:], skipe[:], 1.0))
                ch(v.reciprocal(skipe[:], skip[:]))
                for l in range(LAYERS):
                    a = l * TYPES
                    ch(v.tensor_scalar(g.gate[:, l, :], g.mask[:, 0, :], skipe[:, a:a + 1], None, ALU.mult))
                    for t in range(1, TYPES):
                        ch(v.scalar_tensor_tensor(g.gate[:, l, :], g.mask[:, t, :], skipe[:, a + t:a + t + 1],
                                                  g.gate[:, l, :], ALU.mult, ALU.add))
                ch(v.tensor_scalar(pri[:], pri[:], float(D // HEADS0) ** -0.5, None, ALU.mult))
                for l in range(LAYERS):
                    for r in range(RELS):
                        w = g.wrel[:, ((2 * l) * RELS + r) * D:((2 * l) * RELS + r + 1) * D]
                        ch(v.tensor_scalar(w, w, pri[:, l * RELS + r:l * RELS + r + 1], None, ALU.mult))
                dve.wait_ge(expd, 2)
                ch(v.reciprocal(small[:, 7:8], small[:, 6:7]))
                ch(v.tensor_scalar(g.mixw[:], small[:, 4:6], small[:, 7:8], None, ALU.mult))


def load_nodes(nc, g):
    with Phase(nc, "nodes") as p:
        loaded = p.sem("loaded")
        with p.block() as block:
            @block.sync
            def _(sp):
                sp.dma_start(g.x0[:], g.ins["x"].rearrange("p (b d) -> p b d", d=D)).then_inc(loaded, 16)
                sp.dma_start(g.node_row[:], g.ins["c_node"]).then_inc(loaded, 16)
                sp.wait_ge(loaded, 32)


def edge_scores(nc, g):
    with Phase(nc, "attr") as p:
        ea = p.sb("ea", [P, 2, CH * P])
        sc = [p.ps(f"sc{h}", [P, 512]) for h in range(2)]
        landed = [p.sem(f"landed{h}") for h in range(2)]
        multiplied = [p.sem(f"multiplied{h}") for h in range(2)]
        kept = [p.sem(f"kept{h}") for h in range(2)]
        W = HEADS1
        with p.block() as block:
            @block.sync
            def _(sp):
                with sp.Fori(0, PAIRS) as i:
                    for h in range(2):
                        sp.wait_ge(multiplied[h], i)
                        sp.dma_start(ea[:, h, :], g.ins["edge_attr"][:, bass.ds((i * 2 + h) * (CH * P), CH * P)]).then_inc(landed[h], 16)

            @block.tensor
            def _(pe):
                with pe.Fori(0, PAIRS) as i:
                    for h in range(2):
                        pe.wait_ge(kept[h], i)
                        pe.wait_ge(landed[h], i * 16 + 16)
                        for k in range(CH):
                            mm = nc.tensor.matmul(sc[h][:, k * W:(k + 1) * W], ea[:, h, k * P:(k + 1) * P], g.wc[:],
                                                  start=True, stop=True)
                        mm.then_inc(multiplied[h], 1)

            @block.vector
            def _(dve):
                with dve.Fori(0, PAIRS) as i:
                    for h in range(2):
                        dve.wait_ge(multiplied[h], i + 1)
                        nc.vector.tensor_tensor(g.rec[:, bass.ds((i * 2 + h) * CH, CH), 4:4 + W],
                                                sc[h][:, 0:CH * W].rearrange("p (t w) -> p t w", w=W),
                                                spread(g.bc[:], 1, CH), ALU.add).then_inc(kept[h], 1)


def digits(nc, g, word, name, and_with=None, shift=None):
    with Phase(nc, name) as p:
        a, b, made = p.sb("a", [P, TILES], I32), p.sb("b", [P, TILES], I32), p.sem("made")
        with p.block() as block:
            @block.vector
            def _(dve):
                ch = Chain(dve, made)
                ch(nc.vector.tensor_copy(a[:], g.rec[:, :, word]))
                if shift:
                    ch(nc.vector.tensor_single_scalar(b[:], a[:], shift, ALU.arith_shift_right))
                else:
                    ch(nc.vector.tensor_single_scalar(b[:], a[:], and_with, ALU.bitwise_and))
                ch(nc.vector.tensor_copy(g.keys[:], b[:]))


def count_keys(nc, g, groups, before, name):
    G = groups
    with Phase(nc, name) as p:
        oh = p.sb("oh", [P, 2, CH, G], BF16)
        tot = [p.ps(f"tot{h}", [P, 512]) for h in range(2)]
        marked = [p.sem(f"marked{h}") for h in range(2)]
        summed = [p.sem(f"summed{h}") for h in range(2)]
        kept = [p.sem(f"kept{h}") for h in range(2)]
        done, zeroed, turn = p.sem("done"), p.sem("zeroed"), p.sem("turn")
        counts = before[:, 1:1 + G * TILES].rearrange("p (g t) -> p g t", t=TILES)
        with p.block() as block:
            @block.vector
            def _(dve):
                nc.vector.memset(before[:, 0:1], 0.0).then_inc(zeroed, 1)
                with dve.Fori(0, PAIRS) as i:
                    for h in range(2):
                        dve.wait_ge(summed[h], i)
                        nc.vector.tensor_tensor(oh[:, h], spread(g.keys[:, bass.ds((i * 2 + h) * CH, CH)], 2, G),
                                                spread(g.iota[:, 0:G], 1, CH), ALU.is_equal).then_inc(marked[h], 1)
                for h in range(2):
                    dve.wait_ge(kept[h], PAIRS)
                dve.wait_ge(zeroed, 1)
                flat = before[:, 1:1 + G * TILES]
                nc.vector.tensor_tensor_scan(out=flat, data0=flat, data1=flat, initial=0.0,
                                             op0=ALU.add, op1=ALU.max).then_inc(done, 1)
                dve.wait_ge(done, 1)

            @block.tensor
            def _(pe):
                with pe.Fori(0, PAIRS) as i:
                    for h in range(2):
                        pe.wait_ge(kept[h], i)
                        pe.wait_ge(marked[h], i + 1)
                        nc.tensor.matmul(tot[h][:, 0:CH * G], g.ones_bf[:], oh[:, h].rearrange("p t g -> p (t g)"),
                                         start=True, stop=True).then_inc(summed[h], 1)

            @block.scalar
            def _(act):
                with act.Fori(0, PAIRS) as i:
                    for h in range(2):
                        act.wait_ge(summed[h], i + 1)
                        act.sem_inc(turn, 1)
                        nc.scalar.copy(counts[:, :, bass.ds((i * 2 + h) * CH, CH)].rearrange("p g t -> p t g"),
                                       tot[h][:, 0:CH * G].rearrange("p (t g) -> p t g", g=G)).then_inc(kept[h], 1)


def place_keys(nc, g, groups, before, name, records_to=None, positions=None):
    G = groups
    with Phase(nc, name) as p:
        oh = p.sb("oh", [P, 2, CH, G], BF16)
        pos = p.sb("pos", [P, 2, CH, G])
        posf = p.sb("posf", [P, 2, CH])
        idx = p.sb("idx", [P, 2, CH], I32)
        rec = p.sb("rec", [P, 2, CH, REC])
        above = [p.ps(f"above{h}", [P, 512]) for h in range(2)]
        marked = [p.sem(f"marked{h}") for h in range(2)]
        counted = [p.sem(f"counted{h}") for h in range(2)]
        indexed = [p.sem(f"indexed{h}") for h in range(2)]
        copied = [p.sem(f"copied{h}") for h in range(2)]
        scattered = [p.sem(f"scattered{h}") for h in range(2)]
        chain, turn = p.sem("chain"), p.sem("turn")
        base = before[:, 0:G * TILES].rearrange("p (g t) -> p t g", t=TILES)
        with p.block() as block:
            @block.vector
            def _(dve):
                v, ch = nc.vector, Chain(dve, chain)
                with dve.Fori(0, PAIRS) as i:
                    ch.enter(i, 6)
                    for h in range(2):
                        v.tensor_tensor(oh[:, h], spread(g.keys[:, bass.ds((i * 2 + h) * CH, CH)], 2, G),
                                        spread(g.iota[:, 0:G], 1, CH), ALU.is_equal).then_inc(marked[h], 1)
                    for h in range(2):
                        dve.wait_ge(counted[h], i + 1)
                        ch(v.tensor_tensor(pos[:, h], above[h][:, 0:CH * G].rearrange("p (t g) -> p t g", g=G),
                                           base[:, bass.ds((i * 2 + h) * CH, CH), :], ALU.add))
                        ch(v.tensor_tensor(pos[:, h], pos[:, h], oh[:, h], ALU.mult))
                        if records_to is not None:
                            dve.wait_ge(scattered[h], i * (16 * CH))
                        ch(v.tensor_reduce(posf[:, h], pos[:, h], X, ALU.add))
                        out = idx[:, h] if records_to is not None else positions[:, bass.ds((i * 2 + h) * CH, CH)]
                        dve.sem_inc(turn, 1)
                        v.tensor_copy(out, posf[:, h]).then_inc(indexed[h], 1)
                    dve.wait_ge(indexed[0], i + 1)
                    dve.wait_ge(indexed[1], i + 1)
                ch.leave(PAIRS)

            @block.tensor
            def _(pe):
                with pe.Fori(0, PAIRS) as i:
                    for h in range(2):
                        pe.wait_ge(indexed[h], i)
                        pe.wait_ge(marked[h], i + 1)
                        nc.tensor.matmul(above[h][:, 0:CH * G], g.tri_bf[:], oh[:, h].rearrange("p t g -> p (t g)"),
                                         start=True, stop=True).then_inc(counted[h], 1)

            if records_to is not None:
                @block.scalar
                def _(act):
                    with act.Fori(0, PAIRS) as i:
                        for h in range(2):
                            act.wait_ge(scattered[h], i * (16 * CH))
                            act.sem_inc(turn, 1)
                            nc.scalar.copy(rec[:, h], g.rec[:, bass.ds((i * 2 + h) * CH, CH), :]).then_inc(copied[h], 1)

                @block.gpsimd
                def _(pool):
                    with pool.Fori(0, PAIRS) as i:
                        for h in range(2):
                            pool.wait_ge(copied[h], i + 1)
                            pool.wait_ge(indexed[h], i + 1)
                            pool.sem_inc(turn, 1)
                            for k in range(CH):
                                nc.gpsimd.indirect_dma_start(
                                    out=records_to, out_offset=bass.IndirectOffsetOnAxis(ap=idx[:, h, k:k + 1], axis=0),
                                    in_=rec[:, h, k, :], in_offset=None).then_inc(scattered[h], 16)
                    for h in range(2):
                        pool.wait_ge(scattered[h], PAIRS * 16 * CH)


def read_records(nc, g, source, name):
    with Phase(nc, name) as p:
        landed = p.sem("landed")
        with p.block() as block:
            @block.sync
            def _(sp):
                sp.dma_start(g.rec[:], source.rearrange("(t p) w -> p t w", p=P)).then_inc(landed, 16)
                sp.wait_ge(landed, 16)


def path_table(nc, g, before, table, name):
    with Phase(nc, name) as p:
        made = p.sem("made")
        B = BLOCKS
        f = p.sb("f", [1, 4, B])
        fi = p.sb("fi", [1, 2, B], I32)
        cmp = p.sb("cmp", [1, STEPS, max(B, SCANS) - 1])
        tf = p.sb("tf", [1, STEPS, 4])
        wraps = p.sb("wraps", [1, STEPS])
        bounds = p.sb("bounds", [1, SCANS])
        with p.block() as block:
            @block.vector
            def _(dve):
                v, ch = nc.vector, Chain(dve, made)
                starts = before[0:1, 0:B * TILES].rearrange("p (g t) -> p g t", t=TILES)[:, :, 0]
                ch(v.tensor_copy(fi[:, 0, :], starts))
                ch(v.tensor_single_scalar(fi[:, 1, :], fi[:, 0, :], 7, ALU.arith_shift_right))
                ch(v.tensor_copy(f[:, 0, :], fi[:, 1, :]))
                ch(v.tensor_scalar(f[:, 1, :], f[:, 0, :], float(TILES - 1), None, ALU.min))
                ch(v.tensor_tensor(f[:, 2, :], f[:, 1, :], g.iota[0:1, 0:B], ALU.add))
                ch(v.memset(tf[:], 0.0))
                s = g.steprow[0:1, 0:STEPS]
                ch(v.tensor_tensor(cmp[:, :, 0:B - 1], spread(s, 2, B - 1), spread(f[:, 2, 1:B], 1, STEPS), ALU.is_ge))
                ch(v.tensor_reduce(tf[:, :, 2], cmp[:, :, 0:B - 1], X, ALU.add))
                ch(v.tensor_tensor(tf[:, :, 0], s, tf[:, :, 2], ALU.subtract))
                for w in (RING * CH, SCAN_LEN):
                    n = TILES // w - 1
                    ch(v.tensor_scalar(bounds[:, 0:n], g.iota[0:1, 1:1 + n], float(w), None, ALU.mult))
                    ch(v.tensor_tensor(cmp[:, :, 0:n], spread(tf[:, :, 0], 2, n), spread(bounds[:, 0:n], 1, STEPS), ALU.is_ge))
                    ch(v.tensor_reduce(wraps[:], cmp[:, :, 0:n], X, ALU.add))
                    at = 1 if w == RING * CH else 3
                    ch(v.scalar_tensor_tensor(tf[:, :, at], wraps[:], -float(w), tf[:, :, 0], ALU.mult, ALU.add))
                ch(v.scalar_tensor_tensor(tf[:, :, 3], tf[:, :, 3], float(SCANS), wraps[:], ALU.mult, ALU.add))
                ch(v.tensor_copy(table[:], tf[:].rearrange("p s w -> p (s w)")))


def edge_indices(nc, g):
    with Phase(nc, "cols") as p:
        made = p.sem("made")
        f = p.sb("f", [P, TILES])
        with p.block() as block:
            @block.vector
            def _(dve):
                v, ch = nc.vector, Chain(dve, made)
                ch(v.scalar_tensor_tensor(f[:], g.rec[:, :, 0], float(RELS), g.rec[:, :, 2], ALU.mult, ALU.add))
                ch(v.tensor_copy(g.rel_idx[:], f[:]))
                ch(v.tensor_copy(g.src_idx[:], g.rec[:, :, 0]))
                ch(v.tensor_copy(g.dst_idx[:], g.rec[:, :, 1]))
                ch(v.tensor_copy(g.dst[:], g.rec[:, :, 1]))
                ch(v.tensor_copy(g.src[:], g.rec[:, :, 0]))
                for q in range(2):
                    ch(v.tensor_copy(g.edge_sc[:, q], g.rec[:, :, 4 + q * HEADS0:4 + (q + 1) * HEADS0]
                                     .rearrange("p (c j) h -> p j c h", j=SCAN_LEN)))


class Norms:

    def __init__(self, nc, p, g):
        self.nc, self.g, self.n = nc, g, 0
        self.var_ready, self.std_ready = p.sem("var_ready"), p.sem("std_ready")
        self.sq = p.sb("sq", [P, BLOCKS, D])
        self.st = p.sb("st", [P, 5, BLOCKS])

    def vector(self, dve, ch, out, src, gain=None, bias=None, relu=False):
        v, st, sq = self.nc.vector, self.st, self.sq
        self.n += 1
        ch(v.tensor_reduce(st[:, 0, :], src[:], X, ALU.add))
        ch(v.tensor_scalar(st[:, 1, :], st[:, 0, :], 1.0 / D, None, ALU.mult))
        ch(v.tensor_tensor(out[:], src[:], spread(st[:, 1, :], 2, D), ALU.subtract))
        ch(v.tensor_tensor(sq[:], out[:], out[:], ALU.mult))
        ch(v.tensor_reduce(st[:, 2, :], sq[:], X, ALU.add))
        v.tensor_scalar(st[:, 3, :], st[:, 2, :], 1.0 / D, EPS, ALU.mult, ALU.add).then_inc(self.var_ready, 1)
        dve.wait_ge(self.std_ready, self.n)
        ch(v.reciprocal(st[:, 0, :], st[:, 4, :]))
        ch(v.tensor_tensor(out[:], out[:], spread(st[:, 0, :], 2, D), ALU.mult))
        if gain is not None:
            ch(v.tensor_tensor(out[:], out[:], spread(self.g.row(gain), 1, BLOCKS), ALU.mult))
            ch(v.tensor_tensor(out[:], out[:], spread(self.g.row(bias), 1, BLOCKS), ALU.add))
        if relu:
            ch(v.tensor_scalar_max(out[:], out[:], 0.0))

    def scalar(self, act, norms):
        for n in range(norms):
            act.wait_ge(self.var_ready, n + 1)
            self.nc.scalar.activation(self.st[:, 4, :], self.st[:, 3, :], ACT.Sqrt).then_inc(self.std_ready, 1)


def norm_phase(nc, g, name, work, norms):
    with Phase(nc, name) as p:
        made = p.sem("made")
        ln = Norms(nc, p, g)
        with p.block() as block:
            @block.vector
            def _(dve):
                work(dve, Chain(dve, made), ln)

            @block.scalar
            def _(act):
                ln.scalar(act, norms)


def typed_tables(nc, g, layer, x):
    with Phase(nc, f"tab{layer}") as p:
        xm = p.sb("xm", [P, TYPES, D])
        xt = p.sb("xt", [P, TYPES, D])
        kvq = p.sb("kvq", [P, 3, D])
        tab = p.sb("tab", [P, RELS, 2, D])
        pt, pk = p.ps("pt", [P, 512]), p.ps("pk", [P, 512])
        pr = [p.ps(f"pr{j}", [P, 512]) for j in range(4)]
        masked, turned, xt_ready, projected = p.sem("masked"), p.sem("turned"), p.sem("xt_ready"), p.sem("projected")
        kvq_ready, related, tab_ready = p.sem("kvq_ready"), p.sem("related"), p.sem("tab_ready")
        tab_out, q_out, turn = p.sem("tab_out"), p.sem("q_out"), p.sem("turn")
        half = RELS - 4
        with p.block() as block:
            @block.vector
            def _(dve):
                v = nc.vector
                with dve.Fori(0, BLOCKS) as b:
                    dve.wait_ge(turned, b)
                    for t in range(TYPES):
                        v.tensor_scalar(xm[:, t, :], x[:, bass.ds(b, 1), :].rearrange("p a d -> p (a d)"),
                                        g.mask[:, t, bass.ds(b, 1)], None, ALU.mult).then_inc(masked, 1)
                    dve.wait_ge(tab_out, b * 16)
                    dve.wait_ge(related, b + 1)
                    v.tensor_copy(tab[:, 0:4, 0, :], pr[0][:].rearrange("p (r d) -> p r d", d=D)).then_inc(tab_ready, 1)
                    v.tensor_copy(tab[:, 4:RELS, 0, :], pr[1][:, 0:half * D].rearrange("p (r d) -> p r d", d=D)).then_inc(tab_ready, 1)

            @block.tensor
            def _(pe):
                t_ = nc.tensor
                with pe.Fori(0, BLOCKS) as b:
                    pe.wait_ge(xt_ready, b)
                    pe.wait_ge(masked, b * TYPES + TYPES)
                    for t in range(TYPES):
                        mm = t_.transpose(pt[:, t * D:(t + 1) * D], xm[:, t, :], g.ident[:])
                    mm.then_inc(turned, 1)
                    pe.wait_ge(kvq_ready, b)
                    pe.wait_ge(xt_ready, b + 1)
                    for a in range(3):
                        for t in range(TYPES):
                            w = g.typed(a, layer, t)
                            lhs, rhs = (w, xt[:, t, :]) if a < 2 else (xt[:, t, :], w)
                            mm = t_.matmul(pk[:, a * D:(a + 1) * D], lhs, rhs, start=(t == 0), stop=(t == TYPES - 1))
                    mm.then_inc(projected, 1)
                    pe.wait_ge(tab_ready, b * 4)
                    pe.wait_ge(kvq_ready, b + 1)
                    for a in range(2):
                        w = g.relation(a, layer)
                        t_.matmul(pr[2 * a][:, 0:4 * D], kvq[:, a, :], w[:, 0:4 * D], start=True, stop=True)
                        mm = t_.matmul(pr[2 * a + 1][:, 0:half * D], kvq[:, a, :], w[:, 4 * D:RELS * D], start=True, stop=True)
                    mm.then_inc(related, 1)

            @block.scalar
            def _(act):
                s = nc.scalar
                with act.Fori(0, BLOCKS) as b:
                    act.wait_ge(projected, b)
                    act.wait_ge(turned, b + 1)
                    s.copy(xt[:].rearrange("p t d -> p (t d)"), pt[:, 0:TYPES * D]).then_inc(xt_ready, 1)
                    act.wait_ge(related, b)
                    act.wait_ge(q_out, b * 16)
                    act.wait_ge(projected, b + 1)
                    s.copy(kvq[:].rearrange("p a d -> p (a d)"), pk[:, 0:3 * D]).then_inc(kvq_ready, 1)
                    act.wait_ge(tab_out, b * 16)
                    act.wait_ge(related, b + 1)
                    s.copy(tab[:, 0:4, 1, :], pr[2][:].rearrange("p (r d) -> p r d", d=D)).then_inc(tab_ready, 1)
                    s.copy(tab[:, 4:RELS, 1, :], pr[3][:, 0:half * D].rearrange("p (r d) -> p r d", d=D)).then_inc(tab_ready, 1)

            @block.sync
            def _(sp):
                with sp.Fori(0, BLOCKS) as b:
                    sp.wait_ge(kvq_ready, b + 1)
                    sp.dma_start(g.q_tab[bass.ds(b * P, P), :], kvq[:, 2, :]).then_inc(q_out, 16)
                    sp.wait_ge(tab_ready, b * 4 + 4)
                    sp.dma_start(g.rel_tab.rearrange("(n r) w -> n (r w)", r=RELS)[bass.ds(b * P, P), :],
                                 tab[:].rearrange("p r a d -> p (r a d)")).then_inc(tab_out, 16)
                sp.wait_ge(q_out, BLOCKS * 16)
                sp.wait_ge(tab_out, BLOCKS * 16)


def gather_scores(nc, g, heads, kv_tab, kv_idx, q_tab, q_idx, name):
    H = heads
    with Phase(nc, name) as p:
        kv = p.sb("kv", [P, 2, CH, 2 * D])
        q = p.sb("q", [P, 2, CH, D])
        prod = p.sb("prod", [P, 2, CH, D])
        ikv, iq = p.sb("ikv", [P, 2, CH], I32), p.sb("iq", [P, 2, CH], I32)
        indexed = [p.sem(f"indexed{h}") for h in range(2)]
        gathered = [p.sem(f"gathered{h}") for h in range(2)]
        multiplied = [p.sem(f"multiplied{h}") for h in range(2)]
        scored = [p.sem(f"scored{h}") for h in range(2)]
        values_out = [p.sem(f"values_out{h}") for h in range(2)]
        turn = p.sem("turn")
        per = 16 * 2 * CH
        with p.block() as block:
            @block.scalar
            def _(act):
                with act.Fori(0, PAIRS) as i:
                    for h in range(2):
                        act.wait_ge(gathered[h], i * per)
                        act.sem_inc(turn, 1)
                        nc.scalar.copy(ikv[:, h, :], kv_idx[:, bass.ds((i * 2 + h) * CH, CH)]).then_inc(indexed[h], 1)
                        nc.scalar.copy(iq[:, h, :], q_idx[:, bass.ds((i * 2 + h) * CH, CH)]).then_inc(indexed[h], 1)

            @block.gpsimd
            def _(pool):
                with pool.Fori(0, PAIRS) as i:
                    for h in range(2):
                        pool.wait_ge(indexed[h], i * 2 + 2)
                        pool.wait_ge(multiplied[h], i)
                        pool.wait_ge(values_out[h], i * 16)
                        pool.sem_inc(turn, 1)
                        for k in range(CH):
                            nc.gpsimd.indirect_dma_start(
                                out=kv[:, h, k, :], out_offset=None, in_=kv_tab,
                                in_offset=bass.IndirectOffsetOnAxis(ap=ikv[:, h, k:k + 1], axis=0)).then_inc(gathered[h], 16)
                            nc.gpsimd.indirect_dma_start(
                                out=q[:, h, k, :], out_offset=None, in_=q_tab,
                                in_offset=bass.IndirectOffsetOnAxis(ap=iq[:, h, k:k + 1], axis=0)).then_inc(gathered[h], 16)

            @block.sync
            def _(sp):
                with sp.Fori(0, PAIRS) as i:
                    for h in range(2):
                        sp.wait_ge(gathered[h], i * per + per)
                        sp.dma_start(g.values[bass.ds(i * 2 + h, 1)].rearrange("c p (t d) -> (c p) t d", d=D),
                                     kv[:, h, :, D:2 * D]).then_inc(values_out[h], 16)
                for h in range(2):
                    sp.wait_ge(values_out[h], PAIRS * 16)

            @block.vector
            def _(dve):
                with dve.Fori(0, PAIRS) as i:
                    for h in range(2):
                        dve.wait_ge(gathered[h], i * per + per)
                        nc.vector.tensor_tensor(prod[:, h], kv[:, h, :, 0:D], q[:, h], ALU.mult).then_inc(multiplied[h], 1)
                        dve.wait_ge(multiplied[h], i + 1)
                        dve.sem_inc(turn, 1)
                        for u in range(H // HEADS0):
                            nc.vector.tensor_reduce(
                                g.score[:, u, h * CH:(h + 1) * CH, bass.ds(i, 1), :].rearrange("p k c h -> p k (c h)"),
                                prod[:, h].rearrange("p t (q h d) -> p q t h d", h=HEADS0, q=H // HEADS0)[:, u],
                                X, ALU.add).then_inc(scored[h], 1)


def segment_softmax(nc, g, group, name, scale=None):
    H = HEADS0
    J = SCAN_LEN
    G = 7
    JG = J // G
    L = J * P
    R = SCAN_ROWS
    with Phase(nc, name) as p:
        a = p.sb("a", [R, L])
        fw, bw = p.sb("fw", [R, L]), p.sb("bw", [R, L])
        seg = p.sb("seg", [R, L])
        cont = p.sb("cont", [R, L + 1])
        mark = p.sb("mark", [R, L + 1])
        dst1 = p.sb("dst1", [P, J, SCANS, H])
        ends = p.sb("ends", [R, 6])
        erow = p.sb("erow", [1, 4, R])
        crow = p.sb("crow", [1, 2, R])
        carry = p.sb("carry", [R, 2])
        bank = [p.ps(f"bank{j}", [P, 512]) for j in range(G)]
        small = p.ps("small", [P, 512])
        made, pe_done, act_done = p.sem("made"), p.sem("pe_done"), p.sem("act_done")
        dve_note, pe_note = p.sem("dve_note"), p.sem("pe_note")
        shift_f, shift_b = g.shift[0:R, 0:R], g.shift[0:R, P:P + R]
        score = g.score[:, group].rearrange("p j c h -> p j (c h)")
        dstc = dst1[:].rearrange("p j c h -> p j (c h)")

        with p.block() as block:
            @block.vector
            def _(dve):
                v, ch = nc.vector, Chain(dve, made)
                if scale is not None:
                    ch(v.scalar_tensor_tensor(g.score[:, group], g.score[:, group], scale, g.edge_sc[:, group],
                                              ALU.mult, ALU.add))
                v.tensor_scalar_add(dst1[:], spread(g.dst[:].rearrange("p (c j) -> p j c", j=J), 3, H), 1.0).then_inc(dve_note, 1)
                dve.wait_ge(pe_done, 1)
                for j in range(G):
                    ch(v.tensor_copy(seg[:, j * JG * P:(j + 1) * JG * P], bank[j][0:R, 0:JG * P]))
                v.tensor_tensor(cont[:, 1:L], seg[:, 1:L], seg[:, 0:L - 1], ALU.is_equal).then_inc(dve_note, 1)
                dve.wait_ge(pe_done, 3)
                ch(v.tensor_tensor(cont[:, 0:1], seg[:, 0:1], small[0:R, 0:1], ALU.is_equal))
                ch(v.tensor_tensor(cont[:, L:L + 1], seg[:, L - 1:L], small[0:R, 1:2], ALU.is_equal))
                ch(v.tensor_scalar(mark[:], cont[:], 1.0, BIG, ALU.subtract, ALU.mult))
                ch(v.tensor_reduce(ends[:, 2:3], cont[:, 0:L], X, ALU.min))
                ch(v.tensor_reduce(ends[:, 3:4], cont[:, 1:L + 1], X, ALU.min))
                dve.wait_ge(act_done, 1)

                def scans(data0, data1, starts, op0, op1):
                    v.tensor_tensor_scan(out=fw[:], data0=data0[:, 0:L], data1=data1[:], initial=starts[0],
                                         op0=op0, op1=op1).then_inc(dve_note, 1)
                    v.tensor_tensor_scan(out=bw[:, ::-1], data0=data0[:, L:0:-1], data1=data1[:, ::-1], initial=starts[1],
                                         op0=op0, op1=op1).then_inc(dve_note, 1)

                def carries(note, op0, op1, first, of_mask):
                    dve.wait_ge(dve_note, note)
                    ch(v.tensor_copy(ends[:, 0:1], fw[:, L - 1:L]))
                    v.tensor_copy(ends[:, 1:2], bw[:, 0:1]).then_inc(dve_note, 1)
                    dve.wait_ge(pe_done, 4 if of_mask else 6)
                    ch(v.tensor_copy(erow[:].rearrange("p a r -> p (a r)"), small[0:1, 0:4 * R]))
                    if of_mask:
                        ch(v.tensor_scalar(erow[:, 2:4, :], erow[:, 2:4, :], 1.0, BIG, ALU.subtract, ALU.mult))
                    ch(v.memset(crow[:, 0, 0:H], first))
                    ch(v.memset(crow[:, 1, R - H:R], first))
                    for h in range(H):
                        ch(v.tensor_tensor_scan(out=crow[:, 0, H + h:R:H], data0=erow[:, 2, h:R - H:H],
                                                data1=erow[:, 0, h:R - H:H], initial=first, op0=op0, op1=op1))
                        ch(v.tensor_tensor_scan(out=crow[:, 1, h:R - H:H][:, ::-1], data0=erow[:, 3, H + h:R:H][:, ::-1],
                                                data1=erow[:, 1, H + h:R:H][:, ::-1], initial=first, op0=op0, op1=op1))
                    dve.sem_inc(dve_note, 1)
                    dve.wait_ge(pe_done, 5 if of_mask else 7)
                    ch(v.tensor_copy(carry[:], small[0:R, 0:2]))

                scans(mark, a, (-BIG, -BIG), ALU.add, ALU.max)
                carries(4, ALU.add, ALU.max, -BIG, True)
                scans(mark, a, (carry[:, 0:1], carry[:, 1:2]), ALU.add, ALU.max)
                dve.wait_ge(dve_note, 8)
                ch(v.tensor_tensor(fw[:], fw[:], bw[:], ALU.max))
                v.tensor_tensor(a[:], a[:], fw[:], ALU.subtract).then_inc(dve_note, 1)
                dve.wait_ge(act_done, 2)
                scans(cont, seg, (0.0, 0.0), ALU.mult, ALU.add)
                carries(11, ALU.mult, ALU.add, 0.0, False)
                scans(cont, seg, (carry[:, 0:1], carry[:, 1:2]), ALU.mult, ALU.add)
                dve.wait_ge(dve_note, 15)
                ch(v.tensor_tensor(fw[:], fw[:], bw[:], ALU.add))
                ch(v.tensor_tensor(fw[:], fw[:], seg[:], ALU.subtract))
                ch(v.reciprocal(bw[:], fw[:]))
                v.tensor_tensor(a[:], seg[:], bw[:], ALU.mult).then_inc(dve_note, 1)
                dve.wait_ge(pe_done, 8)
                for j in range(G):
                    out = score[:, j * JG:(j + 1) * JG]
                    ch(v.tensor_copy(out, bank[j][:, 0:JG * R].rearrange("p (j r) -> p j r", j=JG)))

            @block.tensor
            def _(pe):
                t_ = nc.tensor
                pe.wait_ge(dve_note, 1)
                for j in range(J):
                    at = bank[j // JG][0:R, (j % JG) * P:(j % JG + 1) * P]
                    mm = t_.transpose(at, dstc[:, j], g.ident[:])
                mm.then_inc(pe_done, 1)
                pe.wait_ge(dve_note, 2)
                for j in range(J):
                    at = bank[j // JG][0:R, (j % JG) * P:(j % JG + 1) * P]
                    mm = t_.transpose(at, score[:, j], g.ident[:])
                mm.then_inc(pe_done, 1)
                t_.matmul(small[0:R, 0:1], shift_f, seg[:, L - 1:L], start=True, stop=True)
                t_.matmul(small[0:R, 1:2], shift_b, seg[:, 0:1], start=True, stop=True).then_inc(pe_done, 1)
                for note in (5, 12):
                    pe.wait_ge(dve_note, note)
                    for j in range(4):
                        mm = t_.matmul(small[0:1, j * R:(j + 1) * R], ends[:, j:j + 1], g.ident[0:R, 0:R], start=True, stop=True)
                    mm.then_inc(pe_done, 1)
                    pe.wait_ge(dve_note, note + 1)
                    for j in range(2):
                        mm = t_.matmul(small[0:R, j:j + 1], crow[:, j, :], g.ones[0:1, 0:1], start=True, stop=True)
                    mm.then_inc(pe_done, 1)
                pe.wait_ge(act_done, 1)
                pe.wait_ge(dve_note, 16)
                for j in range(J):
                    at = bank[j // JG][:, (j % JG) * R:(j % JG + 1) * R]
                    mm = t_.transpose(at, a[:, j * P:(j + 1) * P], g.ident[0:R, 0:R])
                mm.then_inc(pe_done, 1)

            @block.scalar
            def _(act):
                act.wait_ge(pe_done, 2)
                for j in range(G):
                    cp = nc.scalar.copy(a[:, j * JG * P:(j + 1) * JG * P], bank[j][0:R, 0:JG * P])
                cp.then_inc(act_done, 1)
                act.wait_ge(dve_note, 9)
                nc.scalar.activation(seg[:], a[:], ACT.Exp).then_inc(act_done, 1)


def aggregate(nc, g, table, name, weighted):
    with Phase(nc, name) as p:
        width = D if weighted else MSG
        ring = p.sb("ring", [P, RING, CH, width])
        tiles = ring[:].rearrange("p c t d -> p (c t) d")
        oh = p.sb("oh", [P, 2, P])
        rows = p.sb("rows", [P, 2, D])
        part = [p.ps(f"part{b}", [P, 512]) for b in range(2)]
        landed = [p.sem(f"landed{j}") for j in range(RING)]
        made, rows_ready, summed, added, zeroed = p.sem("made"), p.sem("rows_ready"), p.sem("summed"), p.sem("added"), p.sem("zeroed")
        turn = p.sem("turn")
        LAPS = CHUNKS // RING
        LAP = RING * CH
        TAIL = STEPS - LAPS * LAP

        def chunk_source(c):
            if weighted:
                return g.values[bass.ds(c, 1)].rearrange("c p (t d) -> (c p) t d", d=D)
            return g.messages.rearrange("(c t p) w -> c p t w", p=P, t=CH)[bass.ds(c, 1)].rearrange("c p t w -> (c p) t w")

        with p.block() as block:
            @block.sync
            def _(sp):
                for j in range(RING):
                    sp.dma_start(ring[:, j], chunk_source(j)).then_inc(landed[j], 16)
                with sp.Fori(1, LAPS) as i:
                    for j in range(RING):
                        sp.wait_ge(added, i * LAP + (CH * j - LAP + CH + BLOCKS - 1))
                        sp.dma_start(ring[:, j], chunk_source(i * RING + j)).then_inc(landed[j], 16)

            def step(dve, s, k, after):
                v, b = nc.vector, k % 2
                _, (tile, slot, node, weight) = nc.values_load_multi_w_load_instructions(
                    table[0:1, bass.ds(s * 4, 4)], engines=[dve.engine], min_val=0, max_val=TILES - 1,
                    skip_runtime_bounds_check_because="path_table builds the words within their ranges")
                slot, node = (nc.s_assert_within(w, 0, top - 1, skip_runtime_bounds_check_because="see path_table")
                              for w, top in ((slot, RING * CH), (node, BLOCKS)))
                node_ids = g.node_row[:].rearrange("p (b n) -> p b n", n=P)[:, bass.ds(node, 1), :].rearrange("p a n -> p (a n)")
                row = tiles[:, bass.ds(slot, 1), :].rearrange("p a d -> p (a d)")
                if weighted:
                    v.tensor_scalar(oh[:, b, :], node_ids, g.dst[:, bass.ds(tile, 1)], None, ALU.is_equal)
                    w = g.score[:, 0].rearrange("p j c h -> p (j c) h")[:, bass.ds(weight, 1), :].rearrange("p a h -> p (a h)")
                    v.tensor_tensor(rows[:, b, :].rearrange("p (h d) -> p h d", h=HEADS0),
                                    row.rearrange("p (h d) -> p h d", h=HEADS0),
                                    spread(w, 2, D // HEADS0), ALU.mult).then_inc(rows_ready, 1)
                else:
                    v.tensor_scalar(oh[:, b, :], node_ids, row[:, D:D + 1], None, ALU.is_equal)
                    v.tensor_copy(rows[:, b, :], row[:, 0:D]).then_inc(rows_ready, 1)
                if after is not None:
                    add(dve, *after)
                return s, b, node

            def add(dve, s, b, node):
                dve.wait_ge(summed, s + 1)
                dve.wait_ge(added, s)
                acc = g.agg[:, bass.ds(node, 1), :].rearrange("p a d -> p (a d)")
                nc.vector.tensor_tensor(acc, acc, part[b][:, 0:D], ALU.add).then_inc(added, 1)

            @block.vector
            def _(dve):
                nc.vector.memset(g.agg[:], 0.0).then_inc(zeroed, 1)
                dve.wait_ge(zeroed, 1)
                with dve.Fori(0, LAPS) as i:
                    after = None
                    for k in range(LAP):
                        if k % CH == 0:
                            dve.wait_ge(landed[k // CH], i * 16 + 16)
                            dve.sem_inc(turn, 1)
                        after = step(dve, i * LAP + k, k, after)
                    add(dve, *after)
                after = None
                for k in range(TAIL):
                    after = step(dve, LAPS * LAP + k, k, after)
                add(dve, *after)

            @block.tensor
            def _(pe):
                with pe.Fori(0, STEPS // 2) as i:
                    for b in range(2):
                        pe.wait_ge(rows_ready, i * 2 + b + 1)
                        nc.tensor.matmul(part[b][:, 0:D], oh[:, b, :], rows[:, b, :], start=True, stop=True).then_inc(summed, 1)


def typed_update(nc, g, layer, x, y):
    with Phase(nc, f"upd{layer}") as p:
        xm = p.sb("xm", [P, TYPES, D])
        xt = p.sb("xt", [P, TYPES, D])
        rest = p.sb("rest", [P, D])
        keep = p.sb("keep", [P, BLOCKS])
        pt, ph = p.ps("pt", [P, 512]), p.ps("ph", [P, 512])
        masked, turned, xt_ready, projected = p.sem("masked"), p.sem("turned"), p.sem("xt_ready"), p.sem("projected")
        chain, updated = p.sem("chain"), p.sem("updated")
        with p.block() as block:
            @block.vector
            def _(dve):
                v, ch = nc.vector, Chain(dve, chain)
                ch(v.tensor_scalar(keep[:], g.gate[:, layer, :], -1.0, 2.0, ALU.mult, ALU.add))
                with dve.Fori(0, BLOCKS) as b:
                    ch.enter(b, 1)
                    dve.wait_ge(turned, b)
                    for t in range(TYPES):
                        v.tensor_scalar(xm[:, t, :], g.agg[:, bass.ds(b, 1), :].rearrange("p a d -> p (a d)"),
                                        g.mask[:, t, bass.ds(b, 1)], None, ALU.mult).then_inc(masked, 1)
                    dve.wait_ge(updated, b)
                    ch(v.tensor_scalar(rest[:], x[:, bass.ds(b, 1), :].rearrange("p a d -> p (a d)"),
                                       keep[:, bass.ds(b, 1)], None, ALU.mult))
                    dve.wait_ge(projected, b + 1)
                    v.scalar_tensor_tensor(y[:, bass.ds(b, 1), :].rearrange("p a d -> p (a d)"), ph[:, 0:D],
                                           g.gate[:, layer, bass.ds(b, 1)], rest[:], ALU.mult, ALU.add).then_inc(updated, 1)
                ch.leave(BLOCKS)

            @block.tensor
            def _(pe):
                t_ = nc.tensor
                with pe.Fori(0, BLOCKS) as b:
                    pe.wait_ge(xt_ready, b)
                    pe.wait_ge(masked, b * TYPES + TYPES)
                    for t in range(TYPES):
                        mm = t_.transpose(pt[:, t * D:(t + 1) * D], xm[:, t, :], g.ident[:])
                    mm.then_inc(turned, 1)
                    pe.wait_ge(updated, b)
                    pe.wait_ge(xt_ready, b + 1)
                    for t in range(TYPES):
                        mm = t_.matmul(ph[:, 0:D], xt[:, t, :], g.typed(3, layer, t), start=(t == 0), stop=(t == TYPES - 1))
                    mm.then_inc(projected, 1)

            @block.scalar
            def _(act):
                with act.Fori(0, BLOCKS) as b:
                    act.wait_ge(projected, b)
                    act.wait_ge(turned, b + 1)
                    nc.scalar.copy(xt[:].rearrange("p t d -> p (t d)"), pt[:, 0:TYPES * D]).then_inc(xt_ready, 1)


def plain_tables(nc, g, x):
    with Phase(nc, "tab2") as p:
        xs, xt = p.sb("xs", [P, D]), p.sb("xt", [P, D])
        qkv = p.sb("qkv", [P, 3 * D])
        pt, pk = p.ps("pt", [P, 512]), p.ps("pk", [P, 512])
        copied, turned, xt_ready, projected = p.sem("copied"), p.sem("turned"), p.sem("xt_ready"), p.sem("projected")
        qkv_ready, out = p.sem("qkv_ready"), p.sem("out")
        bias = g.rows[:, ROWS.index("bq") * D:(ROWS.index("bq") + 3) * D]
        with p.block() as block:
            @block.vector
            def _(dve):
                with dve.Fori(0, BLOCKS) as b:
                    dve.wait_ge(turned, b)
                    nc.vector.tensor_scalar(xs[:], x[:, bass.ds(b, 1), :].rearrange("p a d -> p (a d)"), 1.0, None,
                                            ALU.mult).then_inc(copied, 1)
                    dve.wait_ge(out, b * 32)
                    dve.wait_ge(projected, b + 1)
                    nc.vector.tensor_tensor(qkv[:], pk[:, 0:3 * D], bias, ALU.add).then_inc(qkv_ready, 1)

            @block.tensor
            def _(pe):
                with pe.Fori(0, BLOCKS) as b:
                    pe.wait_ge(xt_ready, b)
                    pe.wait_ge(copied, b + 1)
                    nc.tensor.transpose(pt[:, 0:D], xs[:], g.ident[:]).then_inc(turned, 1)
                    pe.wait_ge(qkv_ready, b)
                    pe.wait_ge(xt_ready, b + 1)
                    nc.tensor.matmul(pk[:, 0:3 * D], xt[:], g.wqkv[:], start=True, stop=True).then_inc(projected, 1)

            @block.scalar
            def _(act):
                with act.Fori(0, BLOCKS) as b:
                    act.wait_ge(projected, b)
                    act.wait_ge(turned, b + 1)
                    nc.scalar.copy(xt[:], pt[:, 0:D]).then_inc(xt_ready, 1)

            @block.sync
            def _(sp):
                with sp.Fori(0, BLOCKS) as b:
                    sp.wait_ge(qkv_ready, b + 1)
                    sp.dma_start(g.q_tab[bass.ds(b * P, P), :], qkv[:, 0:D]).then_inc(out, 16)
                    sp.dma_start(g.kv_tab[bass.ds(b * P, P), :], qkv[:, D:3 * D]).then_inc(out, 16)
                sp.wait_ge(out, BLOCKS * 32)


def scatter_messages(nc, g):
    with Phase(nc, "msg") as p:
        val = p.sb("val", [P, 2, CH, D])
        msg = p.sb("msg", [P, 2, CH, MSG])
        idx = p.sb("idx", [P, 2, CH], I32)
        landed = [p.sem(f"landed{h}") for h in range(2)]
        multiplied = [p.sem(f"multiplied{h}") for h in range(2)]
        named = [p.sem(f"named{h}") for h in range(2)]
        scattered = [p.sem(f"scattered{h}") for h in range(2)]
        zeroed, turn = p.sem("zeroed"), p.sem("turn")
        with p.block() as block:
            @block.sync
            def _(sp):
                with sp.Fori(0, PAIRS) as i:
                    for h in range(2):
                        sp.wait_ge(multiplied[h], i * 2)
                        sp.dma_start(val[:, h], g.values[bass.ds(i * 2 + h, 1)].rearrange("c p (t d) -> (c p) t d", d=D)).then_inc(landed[h], 16)

            @block.vector
            def _(dve):
                nc.vector.memset(msg[:], 0.0).then_inc(zeroed, 1)
                dve.wait_ge(zeroed, 1)
                with dve.Fori(0, PAIRS) as i:
                    for h in range(2):
                        dve.wait_ge(scattered[h], i * (16 * CH))
                        dve.wait_ge(landed[h], i * 16 + 16)
                        for q in range(2):
                            nc.vector.tensor_tensor(
                                msg[:, h, :, q * D // 2:(q + 1) * D // 2].rearrange("p t (h d) -> p t h d", h=HEADS0),
                                val[:, h, :, q * D // 2:(q + 1) * D // 2].rearrange("p t (h d) -> p t h d", h=HEADS0),
                                spread(g.score[:, q, h * CH:(h + 1) * CH, bass.ds(i, 1), :].rearrange("p k c h -> p k (c h)"),
                                       3, D // HEADS1), ALU.mult).then_inc(multiplied[h], 1)

            @block.scalar
            def _(act):
                act.wait_ge(zeroed, 1)
                with act.Fori(0, PAIRS) as i:
                    for h in range(2):
                        act.wait_ge(scattered[h], i * (16 * CH))
                        act.sem_inc(turn, 1)
                        nc.scalar.copy(msg[:, h, :, D], g.src[:, bass.ds((i * 2 + h) * CH, CH)]).then_inc(named[h], 1)
                        nc.scalar.copy(idx[:, h, :], g.pos[:, bass.ds((i * 2 + h) * CH, CH)]).then_inc(named[h], 1)

            @block.gpsimd
            def _(pool):
                with pool.Fori(0, PAIRS) as i:
                    for h in range(2):
                        pool.wait_ge(multiplied[h], i * 2 + 2)
                        pool.wait_ge(named[h], i * 2 + 2)
                        pool.sem_inc(turn, 1)
                        for k in range(CH):
                            nc.gpsimd.indirect_dma_start(
                                out=g.messages, out_offset=bass.IndirectOffsetOnAxis(ap=idx[:, h, k:k + 1], axis=0),
                                in_=msg[:, h, k, :], in_offset=None).then_inc(scattered[h], 16)
                for h in range(2):
                    pool.wait_ge(scattered[h], PAIRS * 16 * CH)


def output_projection(nc, g, x, y):
    with Phase(nc, "proj") as p:
        xs, xt = p.sb("xs", [P, D]), p.sb("xt", [P, D])
        pt, ph = p.ps("pt", [P, 512]), p.ps("ph", [P, 512])
        copied, turned, xt_ready, projected, updated = (p.sem(n) for n in ("copied", "turned", "xt_ready", "projected", "updated"))
        made = p.sem("made")
        with p.block() as block:
            @block.vector
            def _(dve):
                with dve.Fori(0, BLOCKS) as b:
                    dve.wait_ge(turned, b)
                    nc.vector.tensor_scalar(xs[:], g.agg[:, bass.ds(b, 1), :].rearrange("p a d -> p (a d)"), 1.0, None,
                                            ALU.mult).then_inc(copied, 1)
                    dve.wait_ge(projected, b + 1)
                    nc.vector.tensor_tensor(y[:, bass.ds(b, 1), :].rearrange("p a d -> p (a d)"), ph[:, 0:D],
                                            x[:, bass.ds(b, 1), :].rearrange("p a d -> p (a d)"), ALU.add).then_inc(updated, 1)
                dve.wait_ge(updated, BLOCKS)
                nc.vector.tensor_tensor(y[:], y[:], spread(g.row("bo"), 1, BLOCKS), ALU.add).then_inc(made, 1)
                dve.wait_ge(made, 1)

            @block.tensor
            def _(pe):
                with pe.Fori(0, BLOCKS) as b:
                    pe.wait_ge(xt_ready, b)
                    pe.wait_ge(copied, b + 1)
                    nc.tensor.transpose(pt[:, 0:D], xs[:], g.ident[:]).then_inc(turned, 1)
                    pe.wait_ge(updated, b)
                    pe.wait_ge(xt_ready, b + 1)
                    nc.tensor.matmul(ph[:, 0:D], xt[:], g.wo[:], start=True, stop=True).then_inc(projected, 1)

            @block.scalar
            def _(act):
                with act.Fori(0, BLOCKS) as b:
                    act.wait_ge(projected, b)
                    act.wait_ge(turned, b + 1)
                    nc.scalar.copy(xt[:], pt[:, 0:D]).then_inc(xt_ready, 1)


def feed_forward(nc, g, xn, x2, x1, y, out):
    with Phase(nc, "ffn") as p:
        xs, xt = p.sb("xs", [P, D]), p.sb("xt", [P, D])
        hid = p.sb("hid", [P, 4, P])
        pt, p1, p2 = p.ps("pt", [P, 512]), p.ps("p1", [P, 512]), p.ps("p2", [P, 512])
        copied, turned, xt_ready, opened, hid_ready, closed, updated = (
            p.sem(n) for n in ("copied", "turned", "xt_ready", "opened", "hid_ready", "closed", "updated"))
        made, stored = p.sem("made"), p.sem("stored")
        with p.block() as block:
            @block.vector
            def _(dve):
                ch = Chain(dve, made)
                ch(nc.vector.tensor_tensor(x2[:], x2[:], x1[:], ALU.add))
                ch(nc.vector.tensor_tensor(x2[:], x2[:], spread(g.row("b2"), 1, BLOCKS), ALU.add))
                with dve.Fori(0, BLOCKS) as b:
                    dve.wait_ge(turned, b)
                    nc.vector.tensor_scalar(xs[:], xn[:, bass.ds(b, 1), :].rearrange("p a d -> p (a d)"), 1.0, None,
                                            ALU.mult).then_inc(copied, 1)
                    dve.wait_ge(closed, b + 1)
                    nc.vector.tensor_tensor(y[:, bass.ds(b, 1), :].rearrange("p a d -> p (a d)"), p2[:, 0:D],
                                            x2[:, bass.ds(b, 1), :].rearrange("p a d -> p (a d)"), ALU.add).then_inc(updated, 1)

            @block.tensor
            def _(pe):
                t_ = nc.tensor
                with pe.Fori(0, BLOCKS) as b:
                    pe.wait_ge(xt_ready, b)
                    pe.wait_ge(copied, b + 1)
                    t_.transpose(pt[:, 0:D], xs[:], g.ident[:]).then_inc(turned, 1)
                    pe.wait_ge(hid_ready, b * 4)
                    pe.wait_ge(xt_ready, b + 1)
                    for j in range(4):
                        mm = t_.matmul(p1[:, j * P:(j + 1) * P], g.w1[:, j * P:(j + 1) * P], xt[:], start=True, stop=True)
                    mm.then_inc(opened, 1)
                    pe.wait_ge(updated, b)
                    pe.wait_ge(hid_ready, b * 4 + 4)
                    for j in range(4):
                        mm = t_.matmul(p2[:, 0:D], hid[:, j, :], g.w2[:, j * D:(j + 1) * D], start=(j == 0), stop=(j == 3))
                    mm.then_inc(closed, 1)

            @block.scalar
            def _(act):
                with act.Fori(0, BLOCKS) as b:
                    act.wait_ge(opened, b)
                    act.wait_ge(turned, b + 1)
                    nc.scalar.copy(xt[:], pt[:, 0:D]).then_inc(xt_ready, 1)
                    act.wait_ge(closed, b)
                    act.wait_ge(opened, b + 1)
                    for j in range(4):
                        nc.scalar.activation(hid[:, j, :], p1[:, j * P:(j + 1) * P], ACT.Relu, bias=g.b1[:, j:j + 1]).then_inc(hid_ready, 1)

            @block.sync
            def _(sp):
                sp.wait_ge(updated, BLOCKS)
                sp.dma_start(out, y[:].rearrange("p b d -> p (b d)")).then_inc(stored, 16)
                sp.wait_ge(stored, 16)


class Graph:

    def __init__(self, nc, stack, ins):
        self.ins = ins

        def sb(name, shape, dt=F32):
            return stack.enter_context(nc.sbuf_tensor(name, shape, dt))

        self.ident, self.tri = sb("ident", [P, P]), sb("tri", [P, P])
        self.tri_bf, self.ones_bf = sb("tri_bf", [P, P], BF16), sb("ones_bf", [P, P], BF16)
        self.ones = sb("ones", [P, 2])
        self.iota = sb("iota", [P, LO])
        self.shift = sb("shift", [P, 2 * P])
        self.steprow = sb("steprow", [1, STEPS])
        self.wtyped = sb("wtyped", [P, 4 * LAYERS * TYPES * D])
        self.wrel = sb("wrel", [P, 2 * LAYERS * RELS * D])
        self.wqkv, self.wo = sb("wqkv", [P, 3 * D]), sb("wo", [P, D])
        self.w1, self.w2 = sb("w1", [P, HID]), sb("w2", [P, HID])
        self.wc, self.b1, self.bc = sb("wc", [P, HEADS1]), sb("b1", [P, 4]), sb("bc", [P, HEADS1])
        self.rows = sb("rows", [P, len(ROWS) * D])
        self.mask, self.gate = sb("mask", [P, TYPES, BLOCKS]), sb("gate", [P, LAYERS, BLOCKS])
        self.mixw = sb("mixw", [P, 2])
        self.tab_dst, self.tab_src = sb("tab_dst", [1, 4 * STEPS], I32), sb("tab_src", [1, 4 * STEPS], I32)
        self.rel_idx, self.src_idx, self.dst_idx = (sb(n, [P, TILES], I32) for n in ("rel_idx", "src_idx", "dst_idx"))
        self.pos = sb("pos", [P, TILES], I32)
        self.dst, self.src, self.keys = (sb(n, [P, TILES]) for n in ("dst", "src", "keys"))
        self.edge_sc = sb("edge_sc", [P, 2, SCAN_LEN, SCANS, HEADS0])

        def dram(name, shape):
            return nc.dram_tensor(name, shape, F32, kind="Internal").ap()

        self.rec_a, self.rec_b = dram("rec_a", [EP, REC]), dram("rec_b", [EP, REC])
        self.rel_tab, self.q_tab, self.kv_tab = dram("rel_tab", [NP * RELS, 2 * D]), dram("q_tab", [NP, D]), dram("kv_tab", [NP, 2 * D])
        self.values, self.messages = dram("values", [CHUNKS, P, CH * D]), dram("messages", [EP, MSG])

    def node_buffers(self, nc, stack):
        self.x0, self.agg, self.xa, self.xb = (
            stack.enter_context(nc.sbuf_tensor(n, [P, BLOCKS, D], F32)) for n in ("x0", "agg", "xa", "xb"))
        self.node_row = stack.enter_context(nc.sbuf_tensor("node_row", [P, NP], F32))
        self.score = stack.enter_context(nc.sbuf_tensor("score", [P, 2, SCAN_LEN, SCANS, HEADS0], F32))

    def row(self, name):
        at = ROWS.index(name)
        return self.rows[:, at * D:(at + 1) * D]

    def typed(self, which, layer, t):
        at = (which * LAYERS + layer) * TYPES + t
        return self.wtyped[:, at * D:(at + 1) * D]

    def relation(self, which, layer):
        at = (2 * layer + which) * RELS
        return self.wrel[:, at * D:(at + RELS) * D]


def build_program(nc, ins, out):
    with ExitStack() as stack:
        g = Graph(nc, stack, ins)
        with ExitStack() as sorting:
            g.rec = sorting.enter_context(nc.sbuf_tensor("rec", [P, TILES, REC], F32))
            load_inputs(nc, g)
            edge_scores(nc, g)
            with nc.sbuf_tensor("before", [P, 1 + LO * TILES], F32) as before:
                digits(nc, g, 1, "lo", and_with=LO - 1)
                count_keys(nc, g, LO, before, "count_lo")
                place_keys(nc, g, LO, before, "place_lo", records_to=g.rec_a)
                read_records(nc, g, g.rec_a, "read_a")
                digits(nc, g, 1, "hi", shift=6)
                count_keys(nc, g, HI, before, "count_hi")
                place_keys(nc, g, HI, before, "place_hi", records_to=g.rec_b)
                read_records(nc, g, g.rec_b, "read_b")
            with nc.sbuf_tensor("before_blocks", [P, 1 + BLOCKS * TILES], F32) as before:
                digits(nc, g, 1, "dst_block", shift=7)
                count_keys(nc, g, BLOCKS, before, "count_dst")
                path_table(nc, g, before, g.tab_dst, "path_dst")
                digits(nc, g, 0, "src_block", shift=7)
                count_keys(nc, g, BLOCKS, before, "count_src")
                place_keys(nc, g, BLOCKS, before, "place_src", positions=g.pos)
                path_table(nc, g, before, g.tab_src, "path_src")
            edge_indices(nc, g)
        g.node_buffers(nc, stack)
        load_nodes(nc, g)
        v = nc.vector

        norm_phase(nc, g, "norm_in", lambda dve, ch, ln: ln.vector(dve, ch, g.xa, g.x0, relu=True), 1)
        x, y = g.xa, g.xb
        for l in range(LAYERS):
            typed_tables(nc, g, l, x)
            gather_scores(nc, g, HEADS0, g.rel_tab, g.rel_idx, g.q_tab, g.dst_idx, f"scores{l}")
            segment_softmax(nc, g, 0, f"softmax{l}")
            aggregate(nc, g, g.tab_dst, f"agg{l}", True)
            typed_update(nc, g, l, x, y)
            norm_phase(nc, g, f"norm{l}",
                       lambda dve, ch, ln, y=y, l=l: ln.vector(dve, ch, y, y, f"ln_g{l}", f"ln_b{l}"), 1)
            x, y = y, x

        def mix(dve, ch, ln):
            ch(v.tensor_scalar(g.xa[:], g.xa[:], g.mixw[:, 1:2], None, ALU.mult))
            ch(v.scalar_tensor_tensor(g.xa[:], g.xb[:], g.mixw[:, 0:1], g.xa[:], ALU.mult, ALU.add))
            ln.vector(dve, ch, g.xa, g.xa, "agg_g", "agg_b")
            ch(v.tensor_tensor(g.x0[:], g.x0[:], g.xa[:], ALU.add))
            ln.vector(dve, ch, g.xb, g.x0, relu=True)
            ln.vector(dve, ch, g.xa, g.xb, "g1", "be1")

        norm_phase(nc, g, "mix", mix, 3)
        plain_tables(nc, g, g.xa)
        gather_scores(nc, g, HEADS1, g.kv_tab, g.dst_idx, g.q_tab, g.src_idx, "scores2")
        for group in range(2):
            segment_softmax(nc, g, group, f"softmax2_{group}", scale=float(D // HEADS1) ** -0.5)
        scatter_messages(nc, g)
        aggregate(nc, g, g.tab_src, "agg2", False)
        output_projection(nc, g, g.xb, g.xb)
        norm_phase(nc, g, "norm2", lambda dve, ch, ln: ln.vector(dve, ch, g.xa, g.xb, "g2", "be2"), 1)
        feed_forward(nc, g, g.xa, g.xb, g.x0, g.agg, out)



def constants():
    k = np.arange(P)
    h = HEADS0
    shift = np.zeros((P, 2 * P), np.float32)
    shift[:, 0:P] = k[None, :] == k[:, None] + h
    shift[:, P:] = k[None, :] == k[:, None] - h
    return {
        "c_ident": np.eye(P, dtype=np.float32),
        "c_tri": (k[:, None] < k[None, :]).astype(np.float32),
        "c_iota": np.tile(np.arange(LO, dtype=np.float32), (P, 1)),
        "c_shift": shift,
        "c_node": np.tile(np.arange(NP, dtype=np.float32), (P, 1)),
        "c_step": np.arange(STEPS, dtype=np.float32)[None],
    }


def lay_out(inp):
    f = np.float32
    a = {k: np.asarray(v) for k, v in inp.items()}
    arrays = constants()
    x = np.zeros((NP, D), f)
    x[:NODES] = a["x"]
    arrays["x"] = x.reshape(BLOCKS, P, D).transpose(1, 0, 2).reshape(P, BLOCKS * D)
    nt = np.zeros(NP, np.int32)
    nt[:NODES] = a["node_type_3"]
    arrays["ntype"] = nt.reshape(BLOCKS, P).T
    cols = np.zeros((3, EP), np.int32)
    cols[0:2] = NP - 1
    cols[0, :EDGES], cols[1, :EDGES], cols[2, :EDGES] = a["src"], a["dst"], a["edge_type_6"]
    arrays["edge_cols"] = cols.reshape(3, TILES, P).transpose(2, 0, 1).reshape(P, 3 * TILES)
    ea = np.zeros((D, EP), f)
    ea[:, :EDGES] = a["edge_attr_128"].T
    arrays["edge_attr"] = ea
    typed = np.stack([a["L0_gnn_Wk"], a["L0_gnn_Wv"], a["L0_gnn_Wq"], a["L0_gnn_Wa"]])
    arrays["w_typed"] = typed.reshape(4 * LAYERS * TYPES, D, D).transpose(1, 0, 2).reshape(D, -1)
    dh = D // HEADS0
    rel = np.zeros((LAYERS, 2, RELS, D, D), f)
    for which, name in enumerate(("L0_gnn_W_att", "L0_gnn_W_msg")):
        for h in range(HEADS0):
            rel[:, which, :, h * dh:(h + 1) * dh, h * dh:(h + 1) * dh] = a[name][:, h]
    arrays["w_rel"] = rel.reshape(LAYERS * 2 * RELS, D, D).transpose(1, 0, 2).reshape(D, -1)
    arrays["b_pri"] = np.repeat(a["L0_gnn_pri"].transpose(1, 0, 2).reshape(HEADS0, LAYERS * RELS), dh, 0)
    arrays["w_qkv"] = np.concatenate([a["L1_gnn_Wq"], a["L1_gnn_Wk"], a["L1_gnn_Wv"]], 1)
    arrays["w_o"], arrays["w_1"], arrays["w_c"] = a["L1_gnn_Wo"], a["L1_gnn_W1"], a["L1_gnn_Wc"]
    arrays["w_2"] = a["L1_gnn_W2"].reshape(4, D, D).transpose(1, 0, 2).reshape(D, 4 * D)
    arrays["b_1"] = a["L1_gnn_b1"].reshape(4, D).T
    rows = dict(ln_g0=a["L0_gnn_ln_g"][0], ln_g1=a["L0_gnn_ln_g"][1], ln_b0=a["L0_gnn_ln_b"][0],
                ln_b1=a["L0_gnn_ln_b"][1], agg_g=a["L0_gnn_agg_g"], agg_b=a["L0_gnn_agg_b"])
    for n in ("bq", "bk", "bv", "bo", "b2", "g1", "be1", "g2", "be2"):
        rows[n] = a["L1_gnn_" + n]
    arrays["b_rows"] = np.tile(np.concatenate([rows[n] for n in ROWS])[None], (P, 1))
    arrays["b_c"] = np.tile(a["L1_gnn_bc"][None], (P, 1))
    arrays["b_skip"] = np.tile(a["L0_gnn_skip"].reshape(1, -1), (P, 1))
    arrays["b_aggw"] = np.tile(a["L0_gnn_agg_w"][None], (P, 1))
    return {k: np.ascontiguousarray(v) for k, v in arrays.items()}


def kernel(**inputs):
    import concourse.bacc as _bacc
    from concourse.bass_utils import run_bass_kernel_spmd as _run

    nc = _bacc.Bacc("TRN2", target_bir_lowering=False, num_devices=1)
    arrays = lay_out(inputs)
    ins = {n: nc.dram_tensor(n, v.shape, mybir.dt.from_np(v.dtype), kind="ExternalInput").ap() for n, v in arrays.items()}
    out = nc.dram_tensor("out", (P, BLOCKS * D), F32, kind="ExternalOutput").ap()
    build_program(nc, ins, out)
    r = _run(nc, [arrays], core_ids=[0])
    got = np.asarray(r.results[0]["out"])
    return got.reshape(P, BLOCKS, D).transpose(1, 0, 2).reshape(NP, D)[:NODES]
```

```python
from contextlib import ExitStack

import numpy as np

import concourse.bass as bass
from concourse import mybir
from concourse.alu_op_type import AluOpType as ALU

F32 = mybir.dt.float32
BF16 = mybir.dt.bfloat16
I32 = mybir.dt.int32
ACT = mybir.ActivationFunctionType
X = mybir.AxisListType.X

P = 128
D = 128
NODES, EDGES = 3125, 50000
BLOCKS = -(-NODES // P)
NP = BLOCKS * P
CH = 7
TILES = 392
EP = TILES * P
CHUNKS = TILES // CH
PAIRS = CHUNKS // 2
RING = 8
LAPS = CHUNKS // RING
SLOTS = 4
STEPS = TILES + BLOCKS - 1
TAIL = -(-STEPS // CH) - CHUNKS
LAG = -(-(CH + BLOCKS - 1) // CH) - 1
GROUP = 5
GROUPS = BLOCKS // GROUP
REC = 12
TYPES, RELS, LAYERS = 3, 6, 2
HEADS0, HEADS1 = 4, 8
MSG = 132
LO, HI = 64, NP // 64
BIG = 1.0e30
EPS = 1e-5
HID = 4 * D
ROWS = ["ln_g0", "ln_g1", "ln_b0", "ln_b1", "agg_g", "agg_b", "bq", "bk", "bv", "bo", "b2", "g1", "be1", "g2", "be2"]
SCAN_LEN = 2 * CH
SCANS = TILES // SCAN_LEN
SCAN_ROWS = SCANS * HEADS0


def spread(ap, axis, n):
    shape = list(ap.shape)
    shape.insert(axis, n)
    return ap.unsqueeze(axis).to_broadcast(shape)


def wait(eng, sem, count):
    if not isinstance(count, int) or count > 0:
        eng.wait_ge(sem, count)


def laps(eng, chunk, tail=True, peel=True):
    if peel:
        for j in range(RING):
            chunk(0, j, CH)
    with eng.Fori(1 if peel else 0, LAPS) as i:
        for j in range(RING):
            chunk(i, j, CH)
    if tail:
        for j in range(TAIL):
            chunk(LAPS, j, min(CH, STEPS - (CHUNKS + j) * CH))


def path_words(nc, eng, table, c, steps):
    why = "path_table builds the words within their ranges"
    _, words = nc.values_load_multi_w_load_instructions(
        table[0:1, bass.ds(c * (4 * CH), 4 * steps)], engines=[eng.engine], min_val=0, max_val=TILES - 1,
        skip_runtime_bounds_check_because=why)
    tops = (TILES, RING * CH, BLOCKS, TILES)
    return [[nc.s_assert_within(w, 0, top - 1, skip_runtime_bounds_check_because=why)
             for w, top in zip(words[4 * k:4 * k + 4], tops)] for k in range(steps)]


def flat(ap):
    return ap.rearrange("p a d -> p (a d)")


class Chain:

    def __init__(self, eng, done):
        self.eng, self.done, self.base, self.n = eng, done, 0, 0

    def __call__(self, ins):
        self.n += 1
        ins.then_inc(self.done, 1)
        self.eng.wait_ge(self.done, self.base + self.n)

    def enter(self, i, per):
        if self.n or not isinstance(self.base, int):
            self.start = self.base + self.n
        else:
            self.start = self.base
        self.base, self.n, self.per = self.start + i * per, 0, per

    def leave(self, trips):
        assert self.n == self.per
        self.base, self.n = self.start + trips * self.per, 0


class Phase:

    def __init__(self, nc, name):
        self.nc, self.name, self.stack, self.sems = nc, name, ExitStack(), []

    def __enter__(self):
        return self

    def __exit__(self, *a):
        self.stack.close()
        self.nc.clear_and_free_semaphores(self.sems)
        self.nc.all_engine_barrier()

    def sb(self, name, shape, dt=F32):
        return self.stack.enter_context(self.nc.sbuf_tensor(f"{self.name}_{name}", shape, dt))

    def ps(self, name, shape, dt=F32):
        return self.stack.enter_context(self.nc.psum_tensor(f"{self.name}_{name}", shape, dt))

    def sem(self, name):
        self.sems.append(self.nc.alloc_semaphore(f"{self.name}_{name}"))
        return self.sems[-1]

    def block(self):
        return self.nc.Block()


def load_inputs(nc, g):
    with Phase(nc, "load") as p:
        loaded, made, expd = p.sem("loaded"), p.sem("made"), p.sem("expd")
        ntype = p.sb("ntype", [P, BLOCKS], I32)
        ecols = p.sb("ecols", [P, 3, TILES], I32)
        skip = p.sb("skip", [P, LAYERS * TYPES])
        skipe = p.sb("skipe", [P, LAYERS * TYPES])
        aggw = p.sb("aggw", [P, 2])
        small = p.sb("small", [P, 8])
        ntf = p.sb("ntf", [P, BLOCKS])
        pri = p.sb("pri", [P, LAYERS * RELS])
        items = [
            (ntype[:], g.ins["ntype"]),
            (ecols[:], g.ins["edge_cols"].rearrange("p (a t) -> p a t", a=3)), (g.ident[:], g.ins["c_ident"]),
            (g.tri[:], g.ins["c_tri"]), (g.iota[:], g.ins["c_iota"]), (g.shift[:], g.ins["c_shift"]),
            (g.steprow[:], g.ins["c_step"]), (g.wtyped[:], g.ins["w_typed"]), (g.wrel[:], g.ins["w_rel"]), (g.wqkv[:], g.ins["w_qkv"]),
            (g.wo[:], g.ins["w_o"]), (g.w1[:], g.ins["w_1"]), (g.w2[:], g.ins["w_2"]), (g.wc[:], g.ins["w_c"]), (g.b1[:], g.ins["b_1"]),
            (g.rows[:], g.ins["b_rows"]), (g.bc[:], g.ins["b_c"]), (skip[:], g.ins["b_skip"]), (aggw[:], g.ins["b_aggw"]), (pri[:], g.ins["b_pri"]),
        ]
        with p.block() as block:
            @block.sync
            def _(sp):
                for dst, src in items:
                    sp.dma_start(dst, src).then_inc(loaded, 16)

            @block.scalar
            def _(act):
                act.wait_ge(loaded, 16 * len(items))
                nc.scalar.activation(skipe[:], skip[:], ACT.Exp, scale=-1.0).then_inc(expd, 1)
                act.wait_ge(made, 2)
                nc.scalar.activation(small[:, 4:6], small[:, 2:4], ACT.Exp, accum_out=small[:, 6:7]).then_inc(expd, 1)

            @block.vector
            def _(dve):
                ch = Chain(dve, made)
                dve.wait_ge(loaded, 16 * len(items))
                v = nc.vector
                ch(v.tensor_tensor(small[:, 0:1], aggw[:, 0:1], aggw[:, 1:2], ALU.max))
                ch(v.tensor_scalar(small[:, 2:4], aggw[:], small[:, 0:1], None, ALU.subtract))
                ch(v.memset(g.ones_bf[:], 1.0))
                ch(v.memset(g.ones[:], 1.0))
                ch(v.memset(g.rec[:, :, 3:4], 0.0))
                ch(v.tensor_copy(g.tri_bf[:], g.tri[:]))
                ch(v.tensor_copy(g.ident_bf[:], g.ident[:]))
                for a in range(3):
                    ch(v.tensor_copy(g.rec[:, :, a], ecols[:, a, :]))
                ch(v.tensor_copy(ntf[:], ntype[:]))
                for t in range(TYPES):
                    ch(v.tensor_single_scalar(g.mask[:, t, :], ntf[:], float(t), ALU.is_equal))
                dve.wait_ge(expd, 1)
                ch(v.tensor_scalar_add(skip[:], skipe[:], 1.0))
                ch(v.reciprocal(skipe[:], skip[:]))
                for l in range(LAYERS):
                    a = l * TYPES
                    ch(v.tensor_scalar(g.gate[:, l, :], g.mask[:, 0, :], skipe[:, a:a + 1], None, ALU.mult))
                    for t in range(1, TYPES):
                        ch(v.scalar_tensor_tensor(g.gate[:, l, :], g.mask[:, t, :], skipe[:, a + t:a + t + 1],
                                                  g.gate[:, l, :], ALU.mult, ALU.add))
                ch(v.tensor_scalar(pri[:], pri[:], float(D // HEADS0) ** -0.5, None, ALU.mult))
                for l in range(LAYERS):
                    for r in range(RELS):
                        w = g.wrel[:, ((2 * l) * RELS + r) * D:((2 * l) * RELS + r + 1) * D]
                        ch(v.tensor_scalar(w, w, pri[:, l * RELS + r:l * RELS + r + 1], None, ALU.mult))
                dve.wait_ge(expd, 2)
                ch(v.reciprocal(small[:, 7:8], small[:, 6:7]))
                ch(v.tensor_scalar(g.mixw[:], small[:, 4:6], small[:, 7:8], None, ALU.mult))


def copy_over(nc, dst, src, name):
    with Phase(nc, name) as p:
        copied = p.sem("copied")
        with p.block() as block:
            @block.sync
            def _(sp):
                sp.dma_start(dst, src).then_inc(copied, 16)
                sp.wait_ge(copied, 16)


def edge_scores(nc, g):
    with Phase(nc, "attr") as p:
        ea = p.sb("ea", [P, RING, CH * P])
        sc = [p.ps(f"sc{h}", [P, 512]) for h in range(2)]
        landed = [p.sem(f"landed{j}") for j in range(RING)]
        multiplied, kept = p.sem("multiplied"), p.sem("kept")
        W = HEADS1
        with p.block() as block:
            @block.sync
            def _(sp):
                def chunk(i, j, steps):
                    c = i * RING + j
                    if not isinstance(i, int):
                        sp.wait_ge(multiplied, c - RING + 1)
                    sp.dma_start(ea[:, j, :], g.ins["edge_attr"][:, bass.ds(c * (CH * P), CH * P)]).then_inc(landed[j], 16)

                laps(sp, chunk, tail=False)

            @block.tensor
            def _(pe):
                def chunk(i, j, steps):
                    c, h = i * RING + j, j % 2
                    wait(pe, kept, c - 1)
                    pe.wait_ge(landed[j], i * 16 + 16)
                    for k in range(CH):
                        mm = nc.tensor.matmul(sc[h][:, k * W:(k + 1) * W], ea[:, j, k * P:(k + 1) * P], g.wc[:],
                                              start=True, stop=True)
                    mm.then_inc(multiplied, 1)

                laps(pe, chunk, tail=False)

            @block.vector
            def _(dve):
                def chunk(i, j, steps):
                    c = i * RING + j
                    dve.wait_ge(multiplied, c + 1)
                    nc.vector.tensor_tensor(g.rec[:, bass.ds(c * CH, CH), 4:4 + W],
                                            sc[j % 2][:, 0:CH * W].rearrange("p (t w) -> p t w", w=W),
                                            spread(g.bc[:], 1, CH), ALU.add).then_inc(kept, 1)

                laps(dve, chunk, tail=False)


def count_inversions(nc, g):
    with Phase(nc, "order") as p:
        loaded, made, summed = p.sem("loaded"), p.sem("made"), p.sem("summed")
        rows = p.sb("rows", [P, TILES + 1], I32)
        rows_f = p.sb("rows_f", [P, TILES + 1])
        above = p.sb("above", [P, TILES])
        per_row = p.sb("per_row", [P, 1])
        total = p.ps("total", [P, 512])
        with p.block() as block:
            @block.sync
            def _(sp):
                sp.dma_start(rows[:], g.ins["dst_rows"]).then_inc(loaded, 16)

            @block.vector
            def _(dve):
                v, ch = nc.vector, Chain(dve, made)
                dve.wait_ge(loaded, 16)
                ch(v.tensor_copy(rows_f[:], rows[:]))
                ch(v.tensor_tensor(above[:], rows_f[:, 0:TILES], rows_f[:, 1:TILES + 1], ALU.is_gt))
                ch(v.tensor_reduce(per_row[:], above[:], X, ALU.add))
                dve.wait_ge(summed, 1)
                ch(v.tensor_copy(g.unordered[:], total[0:1, 0:1]))

            @block.tensor
            def _(pe):
                pe.wait_ge(made, 3)
                nc.tensor.matmul(total[0:1, 0:1], g.ones[:, 0:1], per_row[:], start=True, stop=True).then_inc(summed, 1)


def digits(nc, g, word, name, and_with=None, shift=None):
    with Phase(nc, name) as p:
        a, b, made = p.sb("a", [P, TILES], I32), p.sb("b", [P, TILES], I32), p.sem("made")
        with p.block() as block:
            @block.vector
            def _(dve):
                ch = Chain(dve, made)
                ch(nc.vector.tensor_copy(a[:], g.rec[:, :, word]))
                if shift:
                    ch(nc.vector.tensor_single_scalar(b[:], a[:], shift, ALU.arith_shift_right))
                else:
                    ch(nc.vector.tensor_single_scalar(b[:], a[:], and_with, ALU.bitwise_and))
                ch(nc.vector.tensor_copy(g.keys[:], b[:]))


def count_keys(nc, g, groups, before, name):
    G = groups
    CT = 2 * CH if 2 * CH * G <= 512 else CH
    pairs = TILES // (2 * CT)
    with Phase(nc, name) as p:
        oh = p.sb("oh", [P, 2, CT, G], BF16)
        tot = [p.ps(f"tot{h}", [P, 512]) for h in range(2)]
        marked = [p.sem(f"marked{h}") for h in range(2)]
        summed = [p.sem(f"summed{h}") for h in range(2)]
        kept = [p.sem(f"kept{h}") for h in range(2)]
        done, zeroed, turn = p.sem("done"), p.sem("zeroed"), p.sem("turn")
        counts = before[:, 1:1 + G * TILES].rearrange("p (g t) -> p g t", t=TILES)
        with p.block() as block:
            @block.vector
            def _(dve):
                nc.vector.memset(before[:, 0:1], 0.0).then_inc(zeroed, 1)
                with dve.Fori(0, pairs) as i:
                    for h in range(2):
                        dve.wait_ge(summed[h], i)
                        nc.vector.tensor_tensor(oh[:, h], spread(g.keys[:, bass.ds((i * 2 + h) * CT, CT)], 2, G),
                                                spread(g.iota[:, 0:G], 1, CT), ALU.is_equal).then_inc(marked[h], 1)
                for h in range(2):
                    dve.wait_ge(kept[h], pairs)
                dve.wait_ge(zeroed, 1)
                flat = before[:, 1:1 + G * TILES]
                nc.vector.tensor_tensor_scan(out=flat, data0=flat, data1=flat, initial=0.0,
                                             op0=ALU.add, op1=ALU.max).then_inc(done, 1)
                dve.wait_ge(done, 1)

            @block.tensor
            def _(pe):
                with pe.Fori(0, pairs) as i:
                    for h in range(2):
                        pe.wait_ge(kept[h], i)
                        pe.wait_ge(marked[h], i + 1)
                        nc.tensor.matmul(tot[h][:, 0:CT * G], g.ones_bf[:], oh[:, h].rearrange("p t g -> p (t g)"),
                                         start=True, stop=True).then_inc(summed[h], 1)

            @block.scalar
            def _(act):
                with act.Fori(0, pairs) as i:
                    for h in range(2):
                        act.wait_ge(summed[h], i + 1)
                        act.sem_inc(turn, 1)
                        nc.scalar.copy(counts[:, :, bass.ds((i * 2 + h) * CT, CT)].rearrange("p g t -> p t g"),
                                       tot[h][:, 0:CT * G].rearrange("p (t g) -> p t g", g=G)).then_inc(kept[h], 1)


def place_keys(nc, g, groups, before, name, records_to=None, positions=None):
    G = groups
    CT = 2 * CH if 2 * CH * G <= 512 else CH
    pairs = TILES // (2 * CT)
    with Phase(nc, name) as p:
        oh = p.sb("oh", [P, 2, CT, G], BF16)
        pos = p.sb("pos", [P, 2, CT, G])
        posf = p.sb("posf", [P, 2, CT])
        idx = p.sb("idx", [P, 2, CT], I32)
        rec = p.sb("rec", [P, 2, CT, REC])
        above = [p.ps(f"above{h}", [P, 512]) for h in range(2)]
        marked = [p.sem(f"marked{h}") for h in range(2)]
        counted = [p.sem(f"counted{h}") for h in range(2)]
        indexed = [p.sem(f"indexed{h}") for h in range(2)]
        copied = [p.sem(f"copied{h}") for h in range(2)]
        scattered = [p.sem(f"scattered{h}") for h in range(2)]
        chain, turn = p.sem("chain"), p.sem("turn")
        base = before[:, 0:G * TILES].rearrange("p (g t) -> p t g", t=TILES)
        with p.block() as block:
            @block.vector
            def _(dve):
                v, ch = nc.vector, Chain(dve, chain)
                with dve.Fori(0, pairs) as i:
                    ch.enter(i, 6)
                    for h in range(2):
                        v.tensor_tensor(oh[:, h], spread(g.keys[:, bass.ds((i * 2 + h) * CT, CT)], 2, G),
                                        spread(g.iota[:, 0:G], 1, CT), ALU.is_equal).then_inc(marked[h], 1)
                    for h in range(2):
                        dve.wait_ge(counted[h], i + 1)
                        ch(v.tensor_tensor(pos[:, h], above[h][:, 0:CT * G].rearrange("p (t g) -> p t g", g=G),
                                           base[:, bass.ds((i * 2 + h) * CT, CT), :], ALU.add))
                        ch(v.tensor_tensor(pos[:, h], pos[:, h], oh[:, h], ALU.mult))
                        if records_to is not None:
                            dve.wait_ge(scattered[h], i * (16 * CT))
                        ch(v.tensor_reduce(posf[:, h], pos[:, h], X, ALU.add))
                        out = idx[:, h] if records_to is not None else positions[:, bass.ds((i * 2 + h) * CT, CT)]
                        dve.sem_inc(turn, 1)
                        v.tensor_copy(out, posf[:, h]).then_inc(indexed[h], 1)
                    dve.wait_ge(indexed[0], i + 1)
                    dve.wait_ge(indexed[1], i + 1)
                ch.leave(pairs)

            @block.tensor
            def _(pe):
                with pe.Fori(0, pairs) as i:
                    for h in range(2):
                        pe.wait_ge(indexed[h], i)
                        pe.wait_ge(marked[h], i + 1)
                        nc.tensor.matmul(above[h][:, 0:CT * G], g.tri_bf[:], oh[:, h].rearrange("p t g -> p (t g)"),
                                         start=True, stop=True).then_inc(counted[h], 1)

            if records_to is not None:
                @block.scalar
                def _(act):
                    with act.Fori(0, pairs) as i:
                        for h in range(2):
                            act.wait_ge(scattered[h], i * (16 * CT))
                            act.sem_inc(turn, 1)
                            nc.scalar.copy(rec[:, h], g.rec[:, bass.ds((i * 2 + h) * CT, CT), :]).then_inc(copied[h], 1)

                @block.gpsimd
                def _(pool):
                    with pool.Fori(0, pairs) as i:
                        for h in range(2):
                            pool.wait_ge(copied[h], i + 1)
                            pool.wait_ge(indexed[h], i + 1)
                            pool.sem_inc(turn, 1)
                            for k in range(CT):
                                nc.gpsimd.indirect_dma_start(
                                    out=records_to, out_offset=bass.IndirectOffsetOnAxis(ap=idx[:, h, k:k + 1], axis=0),
                                    in_=rec[:, h, k, :], in_offset=None).then_inc(scattered[h], 16)
                    for h in range(2):
                        pool.wait_ge(scattered[h], pairs * 16 * CT)


def read_records(nc, g, source, name):
    with Phase(nc, name) as p:
        landed = p.sem("landed")
        with p.block() as block:
            @block.sync
            def _(sp):
                sp.dma_start(g.rec[:], source.rearrange("(t p) w -> p t w", p=P)).then_inc(landed, 16)
                sp.wait_ge(landed, 16)


def path_table(nc, g, before, table, name):
    with Phase(nc, name) as p:
        made, counted = p.sem("made"), p.sem("counted")
        B, S = BLOCKS, STEPS
        R = max(B, SCANS)
        fi = p.sb("fi", [1, 2, B], I32)
        f = p.sb("f", [1, 2, B])
        one_row = p.sb("one_row", [1, R])
        cols = p.sb("cols", [R, 4])
        cmp = p.sb("cmp", [R, 3, S])
        tf = p.sb("tf", [1, S, 4])
        wraps = p.sb("wraps", [1, S])
        small, node, tiles = p.ps("small", [P, 512]), p.ps("node", [P, 512]), p.ps("tiles", [P, 512])
        wrap = [p.ps(f"wrap{a}", [P, 512]) for a in range(2)]
        widths = (RING * CH, SCAN_LEN)
        with p.block() as block:
            @block.vector
            def _(dve):
                v, ch = nc.vector, Chain(dve, made)
                starts = before[0:1, 0:B * TILES].rearrange("p (g t) -> p g t", t=TILES)[:, :, 0]
                ch(v.tensor_copy(fi[:, 0, :], starts))
                ch(v.tensor_single_scalar(fi[:, 1, :], fi[:, 0, :], 7, ALU.arith_shift_right))
                ch(v.tensor_copy(f[:, 0, :], fi[:, 1, :]))
                ch(v.tensor_scalar(f[:, 0, :], f[:, 0, :], float(TILES - 1), None, ALU.min))
                ch(v.memset(one_row[:], 1.0))
                ch(v.tensor_tensor(f[:, 1, :], f[:, 0, :], g.iota[0:1, 0:B], ALU.add))
                ch(v.memset(tf[:], 0.0))
                dve.wait_ge(counted, 1)
                ch(v.tensor_copy(cols[0:B, 0:1], small[0:B, 0:1]))
                ch(v.tensor_copy(cols[:, 1:2], small[0:R, 1:2]))
                for a, w in enumerate(widths):
                    ch(v.tensor_scalar(cols[:, 2 + a:3 + a], cols[:, 1:2], float(w), float(w), ALU.mult, ALU.add))
                ch(v.tensor_scalar(cmp[0:B, 0, :], g.steprow[0:B, :], cols[0:B, 0:1], None, ALU.is_ge))
                dve.wait_ge(counted, 2)
                ch(v.tensor_scalar(tf[:, :, 2], node[0:1, 0:S], 1.0, None, ALU.subtract))
                ch(v.tensor_tensor(tf[:, :, 0], g.steprow[0:1, :], tf[:, :, 2], ALU.subtract))
                dve.wait_ge(counted, 3)
                for a in range(2):
                    ch(v.tensor_scalar(cmp[:, 1 + a, :], tiles[0:R, 0:S], cols[:, 2 + a:3 + a], None, ALU.is_ge))
                dve.wait_ge(counted, 4)
                for a, w in enumerate(widths):
                    ch(v.tensor_copy(wraps[:], wrap[a][0:1, 0:S]))
                    ch(v.scalar_tensor_tensor(tf[:, :, 1 + 2 * a], wraps[:], -float(w), tf[:, :, 0], ALU.mult, ALU.add))
                ch(v.scalar_tensor_tensor(tf[:, :, 3], tf[:, :, 3], float(SCANS), wraps[:], ALU.mult, ALU.add))
                ch(v.tensor_copy(table[:], tf[:].rearrange("p s w -> p (s w)")))

            @block.tensor
            def _(pe):
                mm = nc.tensor.matmul
                pe.wait_ge(made, 6)
                mm(small[0:B, 0:1], f[:, 1, :], one_row[:, 0:1], start=True, stop=True)
                mm(small[0:R, 1:2], g.iota[0:1, 0:R], one_row[:, 0:1], start=True, stop=True).then_inc(counted, 1)
                pe.wait_ge(made, 12)
                mm(node[0:1, 0:S], g.ones[0:B, 0:1], cmp[0:B, 0, :], start=True, stop=True).then_inc(counted, 1)
                pe.wait_ge(made, 14)
                mm(tiles[0:R, 0:S], one_row[:], tf[:, :, 0], start=True, stop=True).then_inc(counted, 1)
                pe.wait_ge(made, 16)
                for a in range(2):
                    last = mm(wrap[a][0:1, 0:S], g.ones[0:R, 0:1], cmp[:, 1 + a, :], start=True, stop=True)
                last.then_inc(counted, 1)


def edge_indices(nc, g):
    with Phase(nc, "cols") as p:
        made = p.sem("made")
        f = p.sb("f", [P, TILES])
        with p.block() as block:
            @block.vector
            def _(dve):
                v, ch = nc.vector, Chain(dve, made)
                ch(v.scalar_tensor_tensor(f[:], g.rec[:, :, 0], float(RELS), g.rec[:, :, 2], ALU.mult, ALU.add))
                ch(v.tensor_copy(g.rel_idx[:], f[:]))
                ch(v.tensor_copy(g.src_idx[:], g.rec[:, :, 0]))
                ch(v.tensor_copy(g.dst[:], g.rec[:, :, 1]))
                ch(v.tensor_copy(g.src[:], g.rec[:, :, 0]))
                for q in range(2):
                    ch(v.tensor_copy(g.edge_sc[:, q], g.rec[:, :, 4 + q * HEADS0:4 + (q + 1) * HEADS0]
                                     .rearrange("p (c j) h -> p j c h", j=SCAN_LEN)))


class Norms:

    def __init__(self, nc, p, g):
        self.nc, self.g, self.n = nc, g, 0
        self.var_ready, self.std_ready = p.sem("var_ready"), p.sem("std_ready")
        self.sq = p.sb("sq", [P, BLOCKS, D])
        self.st = p.sb("st", [P, 5, BLOCKS])

    def vector(self, dve, ch, out, src, gain=None, bias=None, relu=False):
        v, st, sq = self.nc.vector, self.st, self.sq
        self.n += 1
        ch(v.tensor_reduce(st[:, 0, :], src[:], X, ALU.add))
        ch(v.tensor_scalar(st[:, 1, :], st[:, 0, :], 1.0 / D, None, ALU.mult))
        ch(v.tensor_tensor(out[:], src[:], spread(st[:, 1, :], 2, D), ALU.subtract))
        ch(v.tensor_tensor(sq[:], out[:], out[:], ALU.mult))
        ch(v.tensor_reduce(st[:, 2, :], sq[:], X, ALU.add))
        v.tensor_scalar(st[:, 3, :], st[:, 2, :], 1.0 / D, EPS, ALU.mult, ALU.add).then_inc(self.var_ready, 1)
        dve.wait_ge(self.std_ready, self.n)
        ch(v.reciprocal(st[:, 0, :], st[:, 4, :]))
        ch(v.tensor_tensor(out[:], out[:], spread(st[:, 0, :], 2, D), ALU.mult))
        if gain is not None:
            ch(v.tensor_tensor(out[:], out[:], spread(self.g.row(gain), 1, BLOCKS), ALU.mult))
            ch(v.tensor_tensor(out[:], out[:], spread(self.g.row(bias), 1, BLOCKS), ALU.add))
        if relu:
            ch(v.tensor_scalar_max(out[:], out[:], 0.0))

    def scalar(self, act, norms):
        for n in range(norms):
            act.wait_ge(self.var_ready, n + 1)
            self.nc.scalar.activation(self.st[:, 4, :], self.st[:, 3, :], ACT.Sqrt).then_inc(self.std_ready, 1)


def norm_phase(nc, g, name, work, norms):
    with Phase(nc, name) as p:
        made = p.sem("made")
        ln = Norms(nc, p, g)
        with p.block() as block:
            @block.vector
            def _(dve):
                work(dve, Chain(dve, made), ln)

            @block.scalar
            def _(act):
                ln.scalar(act, norms)


def split(nc, dve, ch, parts, at, src, rest):
    v = nc.vector

    def part(a):
        return parts[:, at, a, :]

    ch(v.tensor_scalar(part(0), src, 1.0, None, ALU.mult))
    ch(v.tensor_tensor(rest, src, part(0), ALU.subtract))
    ch(v.tensor_scalar(part(1), rest, 1.0, None, ALU.mult))
    ch(v.tensor_tensor(part(2), rest, part(1), ALU.subtract))


def typed_tables(nc, g, layer, x):
    with Phase(nc, f"tab{layer}") as p:
        xm = p.sb("xm", [P, TYPES, D])
        xt = p.sb("xt", [P, TYPES, D])
        kvq = p.sb("kvq", [P, 3, D])
        tab = p.sb("tab", [P, RELS, 2, D])
        pt, pk = p.ps("pt", [P, 512]), p.ps("pk", [P, 512])
        pr = [p.ps(f"pr{j}", [P, 512]) for j in range(4)]
        masked, turned, xt_ready, projected = p.sem("masked"), p.sem("turned"), p.sem("xt_ready"), p.sem("projected")
        kvq_ready, related, tab_ready = p.sem("kvq_ready"), p.sem("related"), p.sem("tab_ready")
        tab_out, chain = p.sem("tab_out"), p.sem("chain")
        rest = p.sb("rest", [P, 1, D])
        half = RELS - 4
        with p.block() as block:
            @block.vector
            def _(dve):
                v, ch = nc.vector, Chain(dve, chain)

                def mask(b):
                    wait(dve, turned, b)
                    for t in range(TYPES):
                        v.tensor_scalar(xm[:, t, :], flat(x[:, bass.ds(b, 1), :]), g.mask[:, t, bass.ds(b, 1)], None,
                                        ALU.mult).then_inc(masked, 1)

                def queries_and_keys(b):
                    dve.wait_ge(kvq_ready, b + 1)
                    split(nc, dve, ch, g.q_parts, bass.ds(b, 1), kvq[:, 2:3, :], rest[:])
                    wait(dve, tab_out, b * 16)
                    dve.wait_ge(related, b + 1)
                    v.tensor_copy(tab[:, 0:4, 0, :], pr[0][:].rearrange("p (r d) -> p r d", d=D)).then_inc(tab_ready, 1)
                    v.tensor_copy(tab[:, 4:RELS, 0, :], pr[1][:, 0:half * D].rearrange("p (r d) -> p r d", d=D)).then_inc(tab_ready, 1)

                mask(0)
                with dve.Fori(0, BLOCKS - 1) as b:
                    ch.enter(b, 4)
                    mask(b + 1)
                    queries_and_keys(b)
                ch.leave(BLOCKS - 1)
                queries_and_keys(BLOCKS - 1)

            @block.tensor
            def _(pe):
                t_ = nc.tensor

                def turn_rows(b):
                    wait(pe, xt_ready, b)
                    pe.wait_ge(masked, b * TYPES + TYPES)
                    for t in range(TYPES):
                        mm = t_.transpose(pt[:, t * D:(t + 1) * D], xm[:, t, :], g.ident[:])
                    mm.then_inc(turned, 1)

                def project(b):
                    wait(pe, kvq_ready, b)
                    pe.wait_ge(xt_ready, b + 1)
                    for a in range(3):
                        for t in range(TYPES):
                            w = g.typed(a, layer, t)
                            lhs, rhs = (w, xt[:, t, :]) if a < 2 else (xt[:, t, :], w)
                            mm = t_.matmul(pk[:, a * D:(a + 1) * D], lhs, rhs, start=(t == 0), stop=(t == TYPES - 1))
                    mm.then_inc(projected, 1)

                def relate(b):
                    wait(pe, tab_ready, b * 4)
                    pe.wait_ge(kvq_ready, b + 1)
                    for a in range(2):
                        w = g.relation(a, layer)
                        t_.matmul(pr[2 * a][:, 0:4 * D], kvq[:, a, :], w[:, 0:4 * D], start=True, stop=True)
                        mm = t_.matmul(pr[2 * a + 1][:, 0:half * D], kvq[:, a, :], w[:, 4 * D:RELS * D], start=True, stop=True)
                    mm.then_inc(related, 1)

                turn_rows(0)
                with pe.Fori(0, BLOCKS - 1) as b:
                    project(b)
                    turn_rows(b + 1)
                    relate(b)
                project(BLOCKS - 1)
                relate(BLOCKS - 1)

            @block.scalar
            def _(act):
                s = nc.scalar

                def keep_turned(b):
                    wait(act, projected, b)
                    act.wait_ge(turned, b + 1)
                    s.copy(xt[:].rearrange("p t d -> p (t d)"), pt[:, 0:TYPES * D]).then_inc(xt_ready, 1)

                def keep_projected(b):
                    wait(act, related, b)
                    wait(act, chain, b * 4)
                    act.wait_ge(projected, b + 1)
                    s.copy(kvq[:].rearrange("p a d -> p (a d)"), pk[:, 0:3 * D]).then_inc(kvq_ready, 1)

                def keep_values(b):
                    wait(act, tab_out, b * 16)
                    act.wait_ge(related, b + 1)
                    s.copy(tab[:, 0:4, 1, :], pr[2][:].rearrange("p (r d) -> p r d", d=D)).then_inc(tab_ready, 1)
                    s.copy(tab[:, 4:RELS, 1, :], pr[3][:, 0:half * D].rearrange("p (r d) -> p r d", d=D)).then_inc(tab_ready, 1)

                keep_turned(0)
                with act.Fori(0, BLOCKS - 1) as b:
                    keep_projected(b)
                    keep_turned(b + 1)
                    keep_values(b)
                keep_projected(BLOCKS - 1)
                keep_values(BLOCKS - 1)

            @block.sync
            def _(sp):
                with sp.Fori(0, BLOCKS) as b:
                    sp.wait_ge(tab_ready, b * 4 + 4)
                    sp.dma_start(g.rel_tab.rearrange("(n r) w -> n (r w)", r=RELS)[bass.ds(b * P, P), :],
                                 tab[:].rearrange("p r a d -> p (r a d)")).then_inc(tab_out, 16)
                sp.wait_ge(tab_out, BLOCKS * 16)


def one_hots(nc, g):
    with Phase(nc, "onehot") as p:
        node_row = p.sb("node_row", [P, NP])
        oh = p.sb("oh", [P, SLOTS, CH, P], BF16)
        oht = p.sb("oht", [P, SLOTS, CH, P], BF16)
        turned = [p.ps(f"turned{h}", [P, CH * P], BF16) for h in range(SLOTS)]
        loaded, made, flipped, copied = p.sem("loaded"), p.sem("made"), p.sem("flipped"), p.sem("copied")
        turn = p.sem("turn")
        oh_out = [p.sem(f"oh_out{h}") for h in range(SLOTS)]
        oht_out = [p.sem(f"oht_out{h}") for h in range(SLOTS)]
        blocks = node_row[:].rearrange("p (b n) -> p b n", n=P)
        with p.block() as block:
            @block.sync
            def _(sp):
                sp.dma_start(node_row[:], g.ins["c_node"]).then_inc(loaded, 16)

                def chunk(i, j, steps):
                    c, h = i * RING + j, j % SLOTS
                    wait(sp, made, c + 1)
                    sp.sem_inc(turn, 1)
                    sp.dma_start(g.oh[bass.ds(c, 1)].rearrange("c p w -> (c p) w")[:, 0:steps * P],
                                 oh[:, h, 0:steps].rearrange("p s n -> p (s n)")).then_inc(oh_out[h], 16)
                    wait(sp, copied, c + 1)
                    sp.sem_inc(turn, 1)
                    sp.dma_start(g.oht[bass.ds(c, 1)].rearrange("c p w -> (c p) w")[:, 0:steps * P],
                                 oht[:, h, 0:steps].rearrange("p s n -> p (s n)")).then_inc(oht_out[h], 16)

                laps(sp, chunk, peel=False)
                for h in range(SLOTS):
                    sp.wait_ge(oh_out[h], (CHUNKS + TAIL) * 16 // SLOTS)
                    sp.wait_ge(oht_out[h], (CHUNKS + TAIL) * 16 // SLOTS)

            @block.vector
            def _(dve):
                dve.wait_ge(loaded, 16)

                def chunk(i, j, steps):
                    c, h = i * RING + j, j % SLOTS
                    wait(dve, oh_out[h], i * (16 * RING // SLOTS) + 16 * (j // SLOTS))
                    wait(dve, flipped, c - SLOTS + 1)
                    dve.sem_inc(turn, 1)
                    for k, (tile, _, node, _) in enumerate(path_words(nc, dve, g.tab_dst, c, steps)):
                        ins = nc.vector.tensor_scalar(oh[:, h, k, :], flat(blocks[:, bass.ds(node, 1), :]),
                                                      g.dst[:, bass.ds(tile, 1)], None, ALU.is_equal)
                    ins.then_inc(made, 1)

                laps(dve, chunk)

            @block.tensor
            def _(pe):
                def chunk(i, j, steps):
                    c, h = i * RING + j, j % SLOTS
                    wait(pe, copied, c - SLOTS + 1)
                    wait(pe, made, c + 1)
                    for k in range(steps):
                        mm = nc.tensor.transpose(turned[h][:, k * P:(k + 1) * P], oh[:, h, k, :], g.ident_bf[:])
                    mm.then_inc(flipped, 1)

                laps(pe, chunk)

            @block.scalar
            def _(act):
                def chunk(i, j, steps):
                    c, h = i * RING + j, j % SLOTS
                    wait(act, oht_out[h], i * (16 * RING // SLOTS) + 16 * (j // SLOTS))
                    wait(act, flipped, c + 1)
                    nc.scalar.copy(oht[:, h, 0:steps].rearrange("p s n -> p (s n)"), turned[h][:, 0:steps * P]).then_inc(copied, 1)

                laps(act, chunk)


def expand(nc, pe, parts, node, onehot, out):
    for a in range(3):
        mm = nc.tensor.matmul(out, onehot, flat(parts[:, bass.ds(node, 1), a, :]), start=(a == 0), stop=(a == 2))
    return mm


def gather_scores(nc, g, heads, with_values, tab, idx, near, name):
    H = heads
    W = 2 * D if with_values else D
    Q = H // HEADS0
    with Phase(nc, name) as p:
        ring = p.sb("ring", [P, RING, CH, W])
        slots = ring[:].rearrange("p c t d -> p (c t) d")
        prod = p.sb("prod", [P, CH, D])
        sums = p.sb("sums", [P, CH, Q, HEADS0])
        oht = p.sb("oht", [P, SLOTS, CH * P], BF16)
        cur = p.sb("cur", [P, RING, CH], I32)
        near_rows = [p.ps(f"near{h}", [P, 1024]) for h in range(2)]
        indexed = p.sem("indexed")
        oht_in = [p.sem(f"oht_in{h}") for h in range(SLOTS)]
        gathered = [p.sem(f"gathered{j}") for j in range(RING)]
        values_out = [p.sem(f"values_out{j}") for j in range(RING)]
        made, multiplied, stepped, turn = p.sem("made"), p.sem("multiplied"), p.sem("stepped"), p.sem("turn")
        per = 16 * CH
        places = g.score[:].rearrange("p q j c h -> p q (j c) h")
        with p.block() as block:
            @block.scalar
            def _(act):
                def chunk(i, j, steps):
                    act.wait_ge(gathered[j], i * per)
                    act.sem_inc(turn, 1)
                    nc.scalar.copy(cur[:, j, :], idx[:, bass.ds((i * RING + j) * CH, CH)]).then_inc(indexed, 1)

                laps(act, chunk, tail=False, peel=False)

            @block.gpsimd
            def _(pool):
                def chunk(i, j, steps):
                    c = i * RING + j
                    pool.wait_ge(indexed, c + 1)
                    if not isinstance(i, int):
                        pool.wait_ge(stepped, c - RING + LAG + 1)
                        if with_values:
                            pool.wait_ge(values_out[j], i * 16)
                    pool.sem_inc(turn, 1)
                    for k in range(CH):
                        nc.gpsimd.indirect_dma_start(
                            out=ring[:, j, k, :], out_offset=None, in_=tab,
                            in_offset=bass.IndirectOffsetOnAxis(ap=cur[:, j, k:k + 1], axis=0)).then_inc(gathered[j], 16)

                laps(pool, chunk, tail=False)

            @block.sync
            def _(sp):
                def chunk(i, j, steps):
                    c = i * RING + j
                    wait(sp, multiplied, c - SLOTS + 1)
                    sp.sem_inc(turn, 1)
                    sp.dma_start(oht[:, j % SLOTS, 0:steps * P], g.oht[bass.ds(c, 1)].rearrange("c p w -> (c p) w")[:, 0:steps * P])\
                        .then_inc(oht_in[j % SLOTS], 16)
                    if with_values and not (isinstance(i, int) and i == LAPS):
                        sp.wait_ge(gathered[j], i * per + per)
                        sp.sem_inc(turn, 1)
                        sp.dma_start(g.values[bass.ds(c, 1)].rearrange("c p (t d) -> (c p) t d", d=D),
                                     ring[:, j, :, D:2 * D]).then_inc(values_out[j], 16)

                laps(sp, chunk)
                if with_values:
                    for j in range(RING):
                        sp.wait_ge(values_out[j], LAPS * 16)

            @block.tensor
            def _(pe):
                def chunk(i, j, steps):
                    c, h = i * RING + j, j % 2
                    pe.wait_ge(oht_in[j % SLOTS], i * (16 * RING // SLOTS) + 16 * (j // SLOTS) + 16)
                    wait(pe, stepped, c - 1)
                    pe.sem_inc(turn, 1)
                    for k, (_, _, node, _) in enumerate(path_words(nc, pe, g.tab_dst, c, steps)):
                        mm = expand(nc, pe, near, node, oht[:, j % SLOTS, k * P:(k + 1) * P], near_rows[h][:, k * P:(k + 1) * P])
                    mm.then_inc(multiplied, 1)

                laps(pe, chunk)

            @block.vector
            def _(dve):
                v = nc.vector
                v.memset(g.score[:], 0.0).then_inc(turn, 1)
                per_chunk = 2 * CH + 1
                zero = 1
                v.memset(sums[:], 0.0).then_inc(made, 1)

                def chunk(i, j, steps):
                    c, h = i * RING + j, j % 2
                    before = c * per_chunk + zero
                    if not (isinstance(i, int) and i == LAPS):
                        dve.wait_ge(gathered[j], i * per + per)
                    dve.wait_ge(multiplied, c + 1)
                    dve.sem_inc(turn, 1)
                    spots = []
                    for k, (_, slot, _, place) in enumerate(path_words(nc, dve, g.tab_dst, c, steps)):
                        spots.append(place)
                        v.tensor_tensor(prod[:, k, :], flat(slots[:, bass.ds(slot, 1), 0:D]),
                                        near_rows[h][:, k * P:(k + 1) * P], ALU.mult).then_inc(made, 1)
                    dve.wait_ge(made, before + steps)
                    v.tensor_reduce(sums[:, 0:steps].rearrange("p t q h -> p (t q h)"),
                                    prod[:, 0:steps].rearrange("p t (h d) -> p (t h) d", h=H), X, ALU.add).then_inc(made, 1)
                    for k, place in enumerate(spots):
                        at = places[:, 0:Q, bass.ds(place, 1), :].rearrange("p q a h -> p q (a h)")
                        dve.wait_ge(made, before + steps + 1 + k)
                        ins = v.tensor_tensor(at, at, sums[:, k], ALU.add)
                        ins.then_inc(made, 1)
                    dve.wait_ge(made, before + 2 * steps + 1)
                    dve.sem_inc(stepped, 1)

                laps(dve, chunk)


def segment_softmax(nc, g, group, name, scale=None):
    H = HEADS0
    J = SCAN_LEN
    G = 7
    JG = J // G
    L = J * P
    R = SCAN_ROWS
    with Phase(nc, name) as p:
        a = p.sb("a", [R, L])
        fw_all, bw = p.sb("fw", [P, L]), p.sb("bw", [R, L])
        fw = fw_all[0:R, :]
        seg = p.sb("seg", [R, L])
        cont = p.sb("cont", [R, L + 1], BF16)
        mark = p.sb("mark", [R, L + 1], BF16)
        dst1 = fw_all[:, 0:J * R].rearrange("p (j c h) -> p j c h", j=J, h=H)
        ends = p.sb("ends", [R, 6])
        erow = p.sb("erow", [1, 4, R])
        crow = p.sb("crow", [1, 2, R])
        carry = p.sb("carry", [R, 2])
        bank = [p.ps(f"bank{j}", [P, 512]) for j in range(G)]
        small = p.ps("small", [P, 512])
        made, pe_done, act_done = p.sem("made"), p.sem("pe_done"), p.sem("act_done")
        dve_note, pe_note = p.sem("dve_note"), p.sem("pe_note")
        shift_f, shift_b = g.shift[0:R, 0:R], g.shift[0:R, P:P + R]
        score = g.score[:, group].rearrange("p j c h -> p j (c h)")
        dstc = dst1.rearrange("p j c h -> p j (c h)")

        with p.block() as block:
            @block.vector
            def _(dve):
                v, ch = nc.vector, Chain(dve, made)
                if scale is not None:
                    ch(v.scalar_tensor_tensor(g.score[:, group], g.score[:, group], scale, g.edge_sc[:, group],
                                              ALU.mult, ALU.add))
                v.tensor_scalar_add(dst1, spread(g.dst[:].rearrange("p (c j) -> p j c", j=J), 3, H), 1.0).then_inc(dve_note, 1)
                dve.wait_ge(pe_done, 1)
                for j in range(G):
                    ch(v.tensor_copy(seg[:, j * JG * P:(j + 1) * JG * P], bank[j][0:R, 0:JG * P]))
                v.tensor_tensor(cont[:, 1:L], seg[:, 1:L], seg[:, 0:L - 1], ALU.is_equal).then_inc(dve_note, 1)
                dve.wait_ge(pe_done, 3)
                ch(v.tensor_tensor(cont[:, 0:1], seg[:, 0:1], small[0:R, 0:1], ALU.is_equal))
                ch(v.tensor_tensor(cont[:, L:L + 1], seg[:, L - 1:L], small[0:R, 1:2], ALU.is_equal))
                ch(v.tensor_scalar(mark[:], cont[:], 1.0, BIG, ALU.subtract, ALU.mult))
                ch(v.tensor_reduce(ends[:, 2:3], cont[:, 0:L], X, ALU.min))
                ch(v.tensor_reduce(ends[:, 3:4], cont[:, 1:L + 1], X, ALU.min))
                dve.wait_ge(act_done, 1)

                def scans(data0, data1, starts, op0, op1):
                    v.tensor_tensor_scan(out=fw, data0=data0[:, 0:L], data1=data1[:], initial=starts[0],
                                         op0=op0, op1=op1).then_inc(dve_note, 1)
                    v.tensor_tensor_scan(out=bw[:, ::-1], data0=data0[:, L:0:-1], data1=data1[:, ::-1], initial=starts[1],
                                         op0=op0, op1=op1).then_inc(dve_note, 1)

                def carries(note, op0, op1, first, of_mask):
                    dve.wait_ge(dve_note, note)
                    ch(v.tensor_copy(ends[:, 0:1], fw[:, L - 1:L]))
                    v.tensor_copy(ends[:, 1:2], bw[:, 0:1]).then_inc(dve_note, 1)
                    dve.wait_ge(pe_done, 4 if of_mask else 6)
                    ch(v.tensor_copy(erow[:].rearrange("p a r -> p (a r)"), small[0:1, 0:4 * R]))
                    if of_mask:
                        ch(v.tensor_scalar(erow[:, 2:4, :], erow[:, 2:4, :], 1.0, BIG, ALU.subtract, ALU.mult))
                    ch(v.memset(crow[:, 0, 0:H], first))
                    ch(v.memset(crow[:, 1, R - H:R], first))
                    for h in range(H):
                        ch(v.tensor_tensor_scan(out=crow[:, 0, H + h:R:H], data0=erow[:, 2, h:R - H:H],
                                                data1=erow[:, 0, h:R - H:H], initial=first, op0=op0, op1=op1))
                        ch(v.tensor_tensor_scan(out=crow[:, 1, h:R - H:H][:, ::-1], data0=erow[:, 3, H + h:R:H][:, ::-1],
                                                data1=erow[:, 1, H + h:R:H][:, ::-1], initial=first, op0=op0, op1=op1))
                    dve.sem_inc(dve_note, 1)
                    dve.wait_ge(pe_done, 5 if of_mask else 7)
                    ch(v.tensor_copy(carry[:], small[0:R, 0:2]))

                scans(mark, a, (-BIG, -BIG), ALU.add, ALU.max)
                carries(4, ALU.add, ALU.max, -BIG, True)
                scans(mark, a, (carry[:, 0:1], carry[:, 1:2]), ALU.add, ALU.max)
                dve.wait_ge(dve_note, 8)
                ch(v.tensor_tensor(fw, fw, bw[:], ALU.max))
                v.tensor_tensor(a[:], a[:], fw, ALU.subtract).then_inc(dve_note, 1)
                dve.wait_ge(act_done, 2)
                scans(cont, seg, (0.0, 0.0), ALU.mult, ALU.add)
                carries(11, ALU.mult, ALU.add, 0.0, False)
                scans(cont, seg, (carry[:, 0:1], carry[:, 1:2]), ALU.mult, ALU.add)
                dve.wait_ge(dve_note, 15)
                ch(v.tensor_tensor(fw, fw, bw[:], ALU.add))
                ch(v.tensor_tensor(fw, fw, seg[:], ALU.subtract))
                ch(v.reciprocal(bw[:], fw))
                v.tensor_tensor(a[:], seg[:], bw[:], ALU.mult).then_inc(dve_note, 1)
                dve.wait_ge(pe_done, 8)
                for j in range(G):
                    out = score[:, j * JG:(j + 1) * JG]
                    ch(v.tensor_copy(out, bank[j][:, 0:JG * R].rearrange("p (j r) -> p j r", j=JG)))

            @block.tensor
            def _(pe):
                t_ = nc.tensor
                pe.wait_ge(dve_note, 1)
                for j in range(J):
                    at = bank[j // JG][0:R, (j % JG) * P:(j % JG + 1) * P]
                    mm = t_.transpose(at, dstc[:, j], g.ident[:])
                mm.then_inc(pe_done, 1)
                pe.wait_ge(dve_note, 2)
                for j in range(J):
                    at = bank[j // JG][0:R, (j % JG) * P:(j % JG + 1) * P]
                    mm = t_.transpose(at, score[:, j], g.ident[:])
                mm.then_inc(pe_done, 1)
                t_.matmul(small[0:R, 0:1], shift_f, seg[:, L - 1:L], start=True, stop=True)
                t_.matmul(small[0:R, 1:2], shift_b, seg[:, 0:1], start=True, stop=True).then_inc(pe_done, 1)
                for note in (5, 12):
                    pe.wait_ge(dve_note, note)
                    for j in range(4):
                        mm = t_.matmul(small[0:1, j * R:(j + 1) * R], ends[:, j:j + 1], g.ident[0:R, 0:R], start=True, stop=True)
                    mm.then_inc(pe_done, 1)
                    pe.wait_ge(dve_note, note + 1)
                    for j in range(2):
                        mm = t_.matmul(small[0:R, j:j + 1], crow[:, j, :], g.ones[0:1, 0:1], start=True, stop=True)
                    mm.then_inc(pe_done, 1)
                pe.wait_ge(act_done, 1)
                pe.wait_ge(dve_note, 16)
                for j in range(J):
                    at = bank[j // JG][:, (j % JG) * R:(j % JG + 1) * R]
                    mm = t_.transpose(at, a[:, j * P:(j + 1) * P], g.ident[0:R, 0:R])
                mm.then_inc(pe_done, 1)

            @block.scalar
            def _(act):
                act.wait_ge(pe_done, 2)
                for j in range(G):
                    cp = nc.scalar.copy(a[:, j * JG * P:(j + 1) * JG * P], bank[j][0:R, 0:JG * P])
                cp.then_inc(act_done, 1)
                act.wait_ge(dve_note, 9)
                nc.scalar.activation(seg[:], a[:], ACT.Exp).then_inc(act_done, 1)


def aggregate(nc, g, table, name, weighted):
    width = D if weighted else MSG
    with Phase(nc, name) as p:
        ring = p.sb("ring", [P, RING, CH, width])
        slots = ring[:].rearrange("p c t d -> p (c t) d")
        oh = p.sb("oh", [P, 2, CH, P])
        zeros = p.sb("zeros", [P, 512], BF16)
        sums = p.ps("sums", [P, 7 * 512])
        blocks_of_sums = sums[:, 0:BLOCKS * D].rearrange("p (b d) -> p b d", d=D)
        landed = [p.sem(f"landed{j}") for j in range(RING)]
        cleared, zeroed, ready, marked, stepped = (p.sem(n) for n in ("cleared", "zeroed", "ready", "marked", "stepped"))
        turn, kept = p.sem("turn"), p.sem("kept")
        if weighted:
            oh_bf = p.sb("oh_bf", [P, SLOTS, CH * P], BF16)
            oh_in = [p.sem(f"oh_in{h}") for h in range(SLOTS)]
        else:
            node_row, loaded = p.sb("node_row", [P, NP]), p.sem("loaded")
            blocks = node_row[:].rearrange("p (b n) -> p b n", n=P)
        in_tail = lambda i: isinstance(i, int) and i == LAPS

        with p.block() as block:
            @block.sync
            def _(sp):
                if not weighted:
                    sp.dma_start(node_row[:], g.ins["c_node"]).then_inc(loaded, 16)

                def chunk(i, j, steps):
                    c = i * RING + j
                    if not in_tail(i):
                        if not isinstance(i, int):
                            sp.wait_ge(stepped, c - RING + LAG + 1)
                            sp.sem_inc(turn, 1)
                        src = g.values if weighted else g.messages
                        sp.dma_start(ring[:, j], src[bass.ds(c, 1)].rearrange("c p (t d) -> (c p) t d", d=width) if weighted else
                                     src.rearrange("(c t p) w -> c p t w", p=P, t=CH)[bass.ds(c, 1)].rearrange("c p t w -> (c p) t w"))\
                            .then_inc(landed[j], 16)
                    if weighted:
                        wait(sp, marked, c - SLOTS + 1)
                        sp.sem_inc(turn, 1)
                        sp.dma_start(oh_bf[:, j % SLOTS, 0:steps * P],
                                     g.oh[bass.ds(c, 1)].rearrange("c p w -> (c p) w")[:, 0:steps * P]).then_inc(oh_in[j % SLOTS], 16)

                laps(sp, chunk, tail=weighted)

            if weighted:
                @block.scalar
                def _(act):
                    def chunk(i, j, steps):
                        c, h = i * RING + j, j % 2
                        wait(act, stepped, c - 1)
                        act.wait_ge(oh_in[j % SLOTS], i * (16 * RING // SLOTS) + 16 * (j // SLOTS) + 16)
                        nc.scalar.copy(oh[:, h, 0:steps].rearrange("p s n -> p (s n)"), oh_bf[:, j % SLOTS, 0:steps * P]).then_inc(marked, 1)

                    laps(act, chunk)

            @block.vector
            def _(dve):
                v = nc.vector
                v.memset(zeros[:], 0.0).then_inc(cleared, 1)
                if not weighted:
                    dve.wait_ge(loaded, 16)

                def weigh(i, j, steps):
                    dve.wait_ge(landed[j], i * 16 + 16)
                    rows = ring[:, j].rearrange("p t (h d) -> p t h d", h=HEADS0)
                    w = g.score[:, 0, (j % 2) * CH:(j % 2 + 1) * CH, bass.ds(i * (RING // 2) + j // 2, 1), :]
                    v.tensor_tensor(rows, rows, spread(w.rearrange("p k c h -> p k (c h)"), 3, D // HEADS0), ALU.mult)\
                        .then_inc(ready, 1)

                def mark(i, j, steps):
                    c, h = i * RING + j, j % 2
                    wait(dve, stepped, c - 1)
                    if not in_tail(i):
                        dve.wait_ge(landed[j], i * 16 + 16)
                    dve.sem_inc(turn, 1)
                    for k, (_, slot, node, _) in enumerate(path_words(nc, dve, table, c, steps)):
                        ins = v.tensor_scalar(oh[:, h, k, :], flat(blocks[:, bass.ds(node, 1), :]),
                                              flat(slots[:, bass.ds(slot, 1), D:D + 1]), None, ALU.is_equal)
                    ins.then_inc(marked, 1)

                if weighted:
                    laps(dve, weigh, tail=False, peel=False)
                else:
                    laps(dve, mark)
                dve.wait_ge(stepped, CHUNKS + TAIL)
                v.tensor_copy(g.agg[:], blocks_of_sums).then_inc(kept, 1)
                dve.wait_ge(kept, 1)

            @block.tensor
            def _(pe):
                pe.wait_ge(cleared, 1)
                for j in range(7):
                    nc.tensor.matmul(sums[:, j * 512:(j + 1) * 512], zeros[:, 0:P], zeros[:], start=True, stop=True).then_inc(zeroed, 1)

                def chunk(i, j, steps):
                    c, h = i * RING + j, j % 2
                    pe.wait_ge(marked, c + 1)
                    if weighted and not in_tail(i):
                        pe.wait_ge(ready, c + 1)
                    pe.sem_inc(turn, 1)
                    for k, (_, slot, node, _) in enumerate(path_words(nc, pe, table, c, steps)):
                        mm = nc.tensor.matmul(flat(blocks_of_sums[:, bass.ds(node, 1), :]), oh[:, h, k, :],
                                              flat(slots[:, bass.ds(slot, 1), 0:D]), start=False, stop=True, skip_group_check=True)
                    mm.then_inc(stepped, 1)

                laps(pe, chunk)


def typed_update(nc, g, layer, x, y):
    with Phase(nc, f"upd{layer}") as p:
        xm = p.sb("xm", [P, TYPES, GROUP, D])
        xt = p.sb("xt", [P, GROUP, TYPES, D])
        rest, gated = p.sb("rest", [P, GROUP, D]), p.sb("gated", [P, GROUP, D])
        keep = p.sb("keep", [P, BLOCKS])
        pt, ph = p.ps("pt", [P, 2048]), p.ps("ph", [P, 1024])
        masked, turned, xt_ready, projected = p.sem("masked"), p.sem("turned"), p.sem("xt_ready"), p.sem("projected")
        chain, updated = p.sem("chain"), p.sem("updated")
        with p.block() as block:
            @block.vector
            def _(dve):
                v, ch = nc.vector, Chain(dve, chain)
                ch(v.tensor_scalar(keep[:], g.gate[:, layer, :], -1.0, 2.0, ALU.mult, ALU.add))
                with dve.Fori(0, GROUPS) as n:
                    ch.enter(n, 2)
                    at = bass.ds(n * GROUP, GROUP)
                    dve.wait_ge(turned, n)
                    for t in range(TYPES):
                        v.tensor_tensor(xm[:, t], g.agg[:, at, :], spread(g.mask[:, t, at], 2, D), ALU.mult).then_inc(masked, 1)
                    dve.wait_ge(updated, n)
                    ch(v.tensor_tensor(rest[:], x[:, at, :], spread(keep[:, at], 2, D), ALU.mult))
                    dve.wait_ge(projected, n + 1)
                    ch(v.tensor_tensor(gated[:], ph[:, 0:GROUP * D].rearrange("p (b d) -> p b d", d=D),
                                       spread(g.gate[:, layer, at], 2, D), ALU.mult))
                    v.tensor_tensor(y[:, at, :], gated[:], rest[:], ALU.add).then_inc(updated, 1)
                ch.leave(GROUPS)

            @block.tensor
            def _(pe):
                t_ = nc.tensor
                with pe.Fori(0, GROUPS) as n:
                    pe.wait_ge(xt_ready, n)
                    pe.wait_ge(masked, n * TYPES + TYPES)
                    for b in range(GROUP):
                        for t in range(TYPES):
                            mm = t_.transpose(pt[:, (b * TYPES + t) * D:(b * TYPES + t + 1) * D], xm[:, t, b, :], g.ident[:])
                    mm.then_inc(turned, 1)
                    pe.wait_ge(updated, n)
                    pe.wait_ge(xt_ready, n + 1)
                    for b in range(GROUP):
                        for t in range(TYPES):
                            mm = t_.matmul(ph[:, b * D:(b + 1) * D], xt[:, b, t, :], g.typed(3, layer, t), start=(t == 0), stop=(t == TYPES - 1))
                    mm.then_inc(projected, 1)

            @block.scalar
            def _(act):
                with act.Fori(0, GROUPS) as n:
                    act.wait_ge(projected, n)
                    act.wait_ge(turned, n + 1)
                    nc.scalar.copy(xt[:].rearrange("p b t d -> p (b t d)"), pt[:, 0:GROUP * TYPES * D]).then_inc(xt_ready, 1)


def plain_tables(nc, g, x):
    with Phase(nc, "tab2") as p:
        xs, xt = p.sb("xs", [P, GROUP, D]), p.sb("xt", [P, GROUP, D])
        qkv = p.sb("qkv", [P, GROUP, 3 * D])
        rest = p.sb("rest", [P, GROUP, D])
        pt, pk = p.ps("pt", [P, 1024]), p.ps("pk", [P, GROUP, 512])
        copied, turned, xt_ready, projected = p.sem("copied"), p.sem("turned"), p.sem("xt_ready"), p.sem("projected")
        qkv_ready, out, chain = p.sem("qkv_ready"), p.sem("out"), p.sem("chain")
        bias = g.rows[:, ROWS.index("bq") * D:(ROWS.index("bq") + 3) * D]
        with p.block() as block:
            @block.vector
            def _(dve):
                v, ch = nc.vector, Chain(dve, chain)
                with dve.Fori(0, GROUPS) as n:
                    ch.enter(n, 8)
                    at = bass.ds(n * GROUP, GROUP)
                    dve.wait_ge(turned, n)
                    v.tensor_scalar(xs[:], x[:, at, :], 1.0, None, ALU.mult).then_inc(copied, 1)
                    dve.wait_ge(out, n * 16)
                    dve.wait_ge(projected, n + 1)
                    v.tensor_tensor(qkv[:], pk[:, :, 0:3 * D], spread(bias, 1, GROUP), ALU.add).then_inc(qkv_ready, 1)
                    dve.wait_ge(qkv_ready, n + 1)
                    split(nc, dve, ch, g.q_parts, at, qkv[:, :, D:2 * D], rest[:])
                    split(nc, dve, ch, g.v_parts, at, qkv[:, :, 2 * D:3 * D], rest[:])
                ch.leave(GROUPS)

            @block.tensor
            def _(pe):
                with pe.Fori(0, GROUPS) as n:
                    pe.wait_ge(xt_ready, n)
                    pe.wait_ge(copied, n + 1)
                    for b in range(GROUP):
                        mm = nc.tensor.transpose(pt[:, b * D:(b + 1) * D], xs[:, b, :], g.ident[:])
                    mm.then_inc(turned, 1)
                    pe.wait_ge(qkv_ready, n)
                    pe.wait_ge(xt_ready, n + 1)
                    for b in range(GROUP):
                        mm = nc.tensor.matmul(pk[:, b, 0:3 * D], xt[:, b, :], g.wqkv[:], start=True, stop=True)
                    mm.then_inc(projected, 1)

            @block.scalar
            def _(act):
                with act.Fori(0, GROUPS) as n:
                    act.wait_ge(projected, n)
                    act.wait_ge(turned, n + 1)
                    nc.scalar.copy(flat(xt[:]), pt[:, 0:GROUP * D]).then_inc(xt_ready, 1)

            @block.sync
            def _(sp):
                with sp.Fori(0, GROUPS) as n:
                    sp.wait_ge(qkv_ready, n + 1)
                    sp.dma_start(g.q_tab[bass.ds(n * (GROUP * P), GROUP * P), :].rearrange("(b p) w -> p b w", p=P),
                                 qkv[:, :, 0:D]).then_inc(out, 16)
                sp.wait_ge(out, GROUPS * 16)


def scatter_messages(nc, g):
    with Phase(nc, "msg") as p:
        ring = p.sb("ring", [P, RING, CH, MSG])
        slots = ring[:].rearrange("p c t d -> p (c t) d")
        oht = p.sb("oht", [P, SLOTS, CH * P], BF16)
        idx = p.sb("idx", [P, RING, CH], I32)
        near_rows = [p.ps(f"near{h}", [P, 1024]) for h in range(2)]
        oht_in = [p.sem(f"oht_in{h}") for h in range(SLOTS)]
        scattered = [p.sem(f"scattered{j}") for j in range(RING)]
        made, multiplied, stepped, finished, named, cleared, turn = (
            p.sem(n) for n in ("made", "multiplied", "stepped", "finished", "named", "cleared", "turn"))
        per = 16 * CH
        with p.block() as block:
            @block.sync
            def _(sp):
                def chunk(i, j, steps):
                    c = i * RING + j
                    wait(sp, multiplied, c - SLOTS + 1)
                    sp.sem_inc(turn, 1)
                    sp.dma_start(oht[:, j % SLOTS, 0:steps * P], g.oht[bass.ds(c, 1)].rearrange("c p w -> (c p) w")[:, 0:steps * P])\
                        .then_inc(oht_in[j % SLOTS], 16)

                laps(sp, chunk)

            @block.tensor
            def _(pe):
                def chunk(i, j, steps):
                    c, h = i * RING + j, j % 2
                    pe.wait_ge(oht_in[j % SLOTS], i * (16 * RING // SLOTS) + 16 * (j // SLOTS) + 16)
                    wait(pe, stepped, c - 1)
                    pe.sem_inc(turn, 1)
                    for k, (_, _, node, _) in enumerate(path_words(nc, pe, g.tab_dst, c, steps)):
                        mm = expand(nc, pe, g.v_parts, node, oht[:, j % SLOTS, k * P:(k + 1) * P], near_rows[h][:, k * P:(k + 1) * P])
                    mm.then_inc(multiplied, 1)

                laps(pe, chunk)

            @block.vector
            def _(dve):
                v = nc.vector
                v.memset(ring[:], 0.0).then_inc(cleared, 1)
                dve.wait_ge(cleared, 1)

                def chunk(i, j, steps):
                    c, h = i * RING + j, j % 2
                    if not isinstance(i, int):
                        dve.wait_ge(scattered[j], i * per)
                        dve.sem_inc(turn, 1)
                        v.memset(ring[:, j, :, 0:D], 0.0).then_inc(cleared, 1)
                        dve.wait_ge(cleared, c - RING + 2)
                    dve.wait_ge(multiplied, c + 1)
                    dve.sem_inc(turn, 1)
                    for k, (_, slot, _, _) in enumerate(path_words(nc, dve, g.tab_dst, c, steps)):
                        row = flat(slots[:, bass.ds(slot, 1), 0:D])
                        wait(dve, made, c * CH + k)
                        v.tensor_tensor(row, row, near_rows[h][:, k * P:(k + 1) * P], ALU.add).then_inc(made, 1)
                    dve.wait_ge(made, c * CH + steps)
                    dve.sem_inc(stepped, 1)
                    if isinstance(i, int) and i == 0 and j < LAG:
                        return
                    jj = (j - LAG) % RING
                    scan = i * (RING // 2) + (j - LAG) // 2
                    for q in range(2):
                        row = ring[:, jj, :, q * D // 2:(q + 1) * D // 2].rearrange("p t (h d) -> p t h d", h=HEADS0)
                        w = g.score[:, q, (jj % 2) * CH:(jj % 2 + 1) * CH, bass.ds(scan, 1), :].rearrange("p k c h -> p k (c h)")
                        v.tensor_tensor(row, row, spread(w, 3, D // HEADS1), ALU.mult).then_inc(finished, 1)

                laps(dve, chunk)

            @block.scalar
            def _(act):
                act.wait_ge(cleared, 1)

                def chunk(i, j, steps):
                    act.wait_ge(scattered[j], i * per)
                    act.sem_inc(turn, 1)
                    at = bass.ds((i * RING + j) * CH, CH)
                    nc.scalar.copy(ring[:, j, :, D], g.src[:, at]).then_inc(named, 1)
                    nc.scalar.copy(idx[:, j, :], g.pos[:, at]).then_inc(named, 1)

                laps(act, chunk, tail=False, peel=False)

            @block.gpsimd
            def _(pool):
                def chunk(i, j, steps):
                    c = i * RING + j
                    pool.wait_ge(finished, c * 2 + 2)
                    pool.wait_ge(named, c * 2 + 2)
                    pool.sem_inc(turn, 1)
                    for k in range(CH):
                        nc.gpsimd.indirect_dma_start(
                            out=g.messages, out_offset=bass.IndirectOffsetOnAxis(ap=idx[:, j, k:k + 1], axis=0),
                            in_=ring[:, j, k, :], in_offset=None).then_inc(scattered[j], 16)

                laps(pool, chunk, tail=False, peel=False)
                for j in range(RING):
                    pool.wait_ge(scattered[j], LAPS * per)


def output_projection(nc, g, x, y):
    with Phase(nc, "proj") as p:
        xs, xt = p.sb("xs", [P, GROUP, D]), p.sb("xt", [P, GROUP, D])
        pt, ph = p.ps("pt", [P, 1024]), p.ps("ph", [P, 1024])
        copied, turned, xt_ready, projected, updated = (p.sem(n) for n in ("copied", "turned", "xt_ready", "projected", "updated"))
        made = p.sem("made")
        with p.block() as block:
            @block.vector
            def _(dve):
                with dve.Fori(0, GROUPS) as n:
                    at = bass.ds(n * GROUP, GROUP)
                    dve.wait_ge(turned, n)
                    nc.vector.tensor_scalar(xs[:], g.agg[:, at, :], 1.0, None, ALU.mult).then_inc(copied, 1)
                    dve.wait_ge(projected, n + 1)
                    nc.vector.tensor_tensor(y[:, at, :], ph[:, 0:GROUP * D].rearrange("p (b d) -> p b d", d=D),
                                            x[:, at, :], ALU.add).then_inc(updated, 1)
                dve.wait_ge(updated, GROUPS)
                nc.vector.tensor_tensor(y[:], y[:], spread(g.row("bo"), 1, BLOCKS), ALU.add).then_inc(made, 1)
                dve.wait_ge(made, 1)

            @block.tensor
            def _(pe):
                with pe.Fori(0, GROUPS) as n:
                    pe.wait_ge(xt_ready, n)
                    pe.wait_ge(copied, n + 1)
                    for b in range(GROUP):
                        mm = nc.tensor.transpose(pt[:, b * D:(b + 1) * D], xs[:, b, :], g.ident[:])
                    mm.then_inc(turned, 1)
                    pe.wait_ge(updated, n)
                    pe.wait_ge(xt_ready, n + 1)
                    for b in range(GROUP):
                        mm = nc.tensor.matmul(ph[:, b * D:(b + 1) * D], xt[:, b, :], g.wo[:], start=True, stop=True)
                    mm.then_inc(projected, 1)

            @block.scalar
            def _(act):
                with act.Fori(0, GROUPS) as n:
                    act.wait_ge(projected, n)
                    act.wait_ge(turned, n + 1)
                    nc.scalar.copy(flat(xt[:]), pt[:, 0:GROUP * D]).then_inc(xt_ready, 1)


def feed_forward(nc, g, xn, x2, x1, y, out):
    with Phase(nc, "ffn") as p:
        xs, xt = p.sb("xs", [P, GROUP, D]), p.sb("xt", [P, GROUP, D])
        hid = p.sb("hid", [P, GROUP, 4, P])
        pt, p1 = p.ps("pt", [P, 1024]), p.ps("p1", [P, GROUP, 4, P])
        copied, turned, xt_ready, opened, hid_ready, closed, updated = (
            p.sem(n) for n in ("copied", "turned", "xt_ready", "opened", "hid_ready", "closed", "updated"))
        made, stored = p.sem("made"), p.sem("stored")
        width = GROUP * P
        with p.block() as block:
            @block.vector
            def _(dve):
                ch = Chain(dve, made)
                ch(nc.vector.tensor_tensor(x2[:], x2[:], x1[:], ALU.add))
                ch(nc.vector.tensor_tensor(x2[:], x2[:], spread(g.row("b2"), 1, BLOCKS), ALU.add))
                nc.vector.tensor_scalar(xs[:], xn[:, 0:GROUP, :], 1.0, None, ALU.mult).then_inc(copied, 1)

                def add(n):
                    dve.wait_ge(closed, n + 1)
                    nc.vector.tensor_tensor(y[:, bass.ds(n * GROUP, GROUP), :],
                                            pt[:, 0:width].rearrange("p (b d) -> p b d", d=D),
                                            x2[:, bass.ds(n * GROUP, GROUP), :], ALU.add).then_inc(updated, 1)

                with dve.Fori(0, GROUPS - 1) as n:
                    dve.wait_ge(turned, n + 1)
                    nc.vector.tensor_scalar(xs[:], xn[:, bass.ds(n * GROUP + GROUP, GROUP), :], 1.0, None, ALU.mult).then_inc(copied, 1)
                    add(n)
                add(GROUPS - 1)

            @block.tensor
            def _(pe):
                t_ = nc.tensor
                with pe.Fori(0, GROUPS) as n:
                    pe.wait_ge(updated, n)
                    pe.wait_ge(copied, n + 1)
                    for b in range(GROUP):
                        mm = t_.transpose(pt[:, b * D:(b + 1) * D], xs[:, b, :], g.ident[:])
                    mm.then_inc(turned, 1)
                    pe.wait_ge(hid_ready, n * GROUP)
                    pe.wait_ge(xt_ready, n + 1)
                    for b in range(GROUP):
                        for j in range(4):
                            mm = t_.matmul(p1[:, b, j, :], g.w1[:, j * P:(j + 1) * P], xt[:, b, :], start=True, stop=True)
                        mm.then_inc(opened, 1)
                    for b in range(GROUP):
                        pe.wait_ge(hid_ready, n * GROUP + b + 1)
                        for j in range(4):
                            mm = t_.matmul(pt[:, b * D:(b + 1) * D], hid[:, b, j, :], g.w2[:, j * D:(j + 1) * D],
                                           start=(j == 0), stop=(j == 3))
                    mm.then_inc(closed, 1)

            @block.scalar
            def _(act):
                with act.Fori(0, GROUPS) as n:
                    act.wait_ge(opened, n * GROUP)
                    act.wait_ge(turned, n + 1)
                    nc.scalar.copy(flat(xt[:]), pt[:, 0:width]).then_inc(xt_ready, 1)
                    act.wait_ge(closed, n)
                    for b in range(GROUP):
                        act.wait_ge(opened, n * GROUP + b + 1)
                        for j in range(4):
                            relu = nc.scalar.activation(hid[:, b, j, :], p1[:, b, j, :], ACT.Relu, bias=g.b1[:, j:j + 1])
                        relu.then_inc(hid_ready, 1)

            @block.sync
            def _(sp):
                sp.wait_ge(updated, GROUPS)
                sp.dma_start(out, flat(y[:])).then_inc(stored, 16)
                sp.wait_ge(stored, 16)


class Graph:

    def __init__(self, nc, stack, ins):
        self.ins = ins

        def sb(name, shape, dt=F32):
            return stack.enter_context(nc.sbuf_tensor(name, shape, dt))

        self.ident, self.tri = sb("ident", [P, P]), sb("tri", [P, P])
        self.ident_bf = sb("ident_bf", [P, P], BF16)
        self.tri_bf, self.ones_bf = sb("tri_bf", [P, P], BF16), sb("ones_bf", [P, P], BF16)
        self.ones = sb("ones", [P, 2])
        self.iota = sb("iota", [P, LO])
        self.shift = sb("shift", [P, 2 * P])
        self.wtyped = sb("wtyped", [P, 4 * LAYERS * TYPES * D])
        self.wrel = sb("wrel", [P, 2 * LAYERS * RELS * D])
        self.wqkv, self.wo = sb("wqkv", [P, 3 * D]), sb("wo", [P, D])
        self.w1, self.w2 = sb("w1", [P, HID]), sb("w2", [P, HID])
        self.wc, self.b1, self.bc = sb("wc", [P, HEADS1]), sb("b1", [P, 4]), sb("bc", [P, HEADS1])
        self.rows = sb("rows", [P, len(ROWS) * D])
        self.mask, self.gate = sb("mask", [P, TYPES, BLOCKS]), sb("gate", [P, LAYERS, BLOCKS])
        self.mixw = sb("mixw", [P, 2])
        self.unordered = sb("unordered", [1, 1], I32)
        self.tab_dst = sb("tab_dst", [1, 4 * STEPS], I32)
        self.rel_idx, self.src_idx = (sb(n, [P, TILES], I32) for n in ("rel_idx", "src_idx"))
        self.pos = sb("pos", [P, TILES], I32)
        self.dst, self.src = (sb(n, [P, TILES]) for n in ("dst", "src"))
        self.edge_sc = sb("edge_sc", [P, 2, SCAN_LEN, SCANS, HEADS0])

        def dram(name, shape, dt=F32):
            return nc.dram_tensor(name, shape, dt, kind="Internal").ap()

        self.tab_src = dram("tab_src", [1, 4 * STEPS], I32)
        self.rec_a, self.rec_b = dram("rec_a", [EP, REC]), dram("rec_b", [EP, REC])
        self.rel_tab, self.q_tab = dram("rel_tab", [NP * RELS, 2 * D]), dram("q_tab", [NP, D])
        self.oh, self.oht = (dram(n, [CHUNKS + TAIL, P, CH * P], BF16) for n in ("oh", "oht"))
        self.values, self.messages = dram("values", [CHUNKS, P, CH * D]), dram("messages", [EP, MSG])

    def node_buffers(self, nc, stack):
        self.agg, self.xa, self.xb = (
            stack.enter_context(nc.sbuf_tensor(n, [P, BLOCKS, D], F32)) for n in ("agg", "xa", "xb"))
        self.q_parts = stack.enter_context(nc.sbuf_tensor("q_parts", [P, BLOCKS, 3, D], BF16))
        self.score = stack.enter_context(nc.sbuf_tensor("score", [P, 2, SCAN_LEN, SCANS, HEADS0], F32))

    def row(self, name):
        at = ROWS.index(name)
        return self.rows[:, at * D:(at + 1) * D]

    def typed(self, which, layer, t):
        at = (which * LAYERS + layer) * TYPES + t
        return self.wtyped[:, at * D:(at + 1) * D]

    def relation(self, which, layer):
        at = (2 * layer + which) * RELS
        return self.wrel[:, at * D:(at + RELS) * D]


def build_program(nc, ins, out):
    with ExitStack() as stack:
        g = Graph(nc, stack, ins)
        with ExitStack() as sorting:
            g.rec = sorting.enter_context(nc.sbuf_tensor("rec", [P, TILES, REC], F32))
            g.keys = sorting.enter_context(nc.sbuf_tensor("keys", [P, TILES], F32))
            g.steprow = sorting.enter_context(nc.sbuf_tensor("steprow", [BLOCKS, STEPS], F32))
            load_inputs(nc, g)
            edge_scores(nc, g)
            count_inversions(nc, g)
            unordered = nc.values_load(g.unordered[0:1, 0:1], min_val=0, max_val=EP,
                                       skip_runtime_bounds_check_because="a count of edges")
            with nc.If(unordered > 0):
                with nc.sbuf_tensor("before", [P, 1 + LO * TILES], F32) as before:
                    digits(nc, g, 1, "lo", and_with=LO - 1)
                    count_keys(nc, g, LO, before, "count_lo")
                    place_keys(nc, g, LO, before, "place_lo", records_to=g.rec_a)
                    read_records(nc, g, g.rec_a, "read_a")
                    digits(nc, g, 1, "hi", shift=6)
                    count_keys(nc, g, HI, before, "count_hi")
                    place_keys(nc, g, HI, before, "place_hi", records_to=g.rec_b)
                    read_records(nc, g, g.rec_b, "read_b")
            with nc.Else():
                nc.all_engine_barrier()
            nc.all_engine_barrier()
            with nc.sbuf_tensor("before_blocks", [P, 1 + BLOCKS * TILES], F32) as before:
                digits(nc, g, 1, "dst_block", shift=7)
                count_keys(nc, g, BLOCKS, before, "count_dst")
                path_table(nc, g, before, g.tab_dst, "path_dst")
                digits(nc, g, 0, "src_block", shift=7)
                count_keys(nc, g, BLOCKS, before, "count_src")
                place_keys(nc, g, BLOCKS, before, "place_src", positions=g.pos)
                with nc.sbuf_tensor("tab_src_sb", [1, 4 * STEPS], I32) as tab:
                    path_table(nc, g, before, tab, "path_src")
                    copy_over(nc, g.tab_src, tab[:], "tab_src_out")
            edge_indices(nc, g)
        g.node_buffers(nc, stack)
        one_hots(nc, g)
        v = nc.vector

        copy_over(nc, g.xb[:], g.ins["x"].rearrange("p (b d) -> p b d", d=D), "nodes_in")
        norm_phase(nc, g, "norm_in", lambda dve, ch, ln: ln.vector(dve, ch, g.xa, g.xb, relu=True), 1)
        x, y = g.xa, g.xb
        for l in range(LAYERS):
            typed_tables(nc, g, l, x)
            gather_scores(nc, g, HEADS0, True, g.rel_tab, g.rel_idx, g.q_parts, f"scores{l}")
            segment_softmax(nc, g, 0, f"softmax{l}")
            aggregate(nc, g, g.tab_dst, f"agg{l}", True)
            typed_update(nc, g, l, x, y)
            norm_phase(nc, g, f"norm{l}",
                       lambda dve, ch, ln, y=y, l=l: ln.vector(dve, ch, y, y, f"ln_g{l}", f"ln_b{l}"), 1)
            x, y = y, x

        g.x1 = stack.enter_context(nc.sbuf_tensor("x1", [P, BLOCKS, D], F32))
        copy_over(nc, g.x1[:], g.ins["x"].rearrange("p (b d) -> p b d", d=D), "nodes_again")

        def mix(dve, ch, ln):
            ch(v.tensor_scalar(g.xa[:], g.xa[:], g.mixw[:, 1:2], None, ALU.mult))
            ch(v.scalar_tensor_tensor(g.xa[:], g.xb[:], g.mixw[:, 0:1], g.xa[:], ALU.mult, ALU.add))
            ln.vector(dve, ch, g.xa, g.xa, "agg_g", "agg_b")
            ch(v.tensor_tensor(g.x1[:], g.x1[:], g.xa[:], ALU.add))
            ln.vector(dve, ch, g.xb, g.x1, relu=True)
            ln.vector(dve, ch, g.xa, g.xb, "g1", "be1")

        norm_phase(nc, g, "mix", mix, 3)
        with nc.sbuf_tensor("v_parts", [P, BLOCKS, 3, D], BF16) as g.v_parts:
            plain_tables(nc, g, g.xa)
            gather_scores(nc, g, HEADS1, False, g.q_tab, g.src_idx, g.q_parts, "scores2")
            for group in range(2):
                segment_softmax(nc, g, group, f"softmax2_{group}", scale=float(D // HEADS1) ** -0.5)
            scatter_messages(nc, g)
        with nc.sbuf_tensor("tab_src_in", [1, 4 * STEPS], I32) as tab:
            copy_over(nc, tab[:], g.tab_src, "tab_src_back")
            aggregate(nc, g, tab, "agg2", False)
        output_projection(nc, g, g.xb, g.xb)
        norm_phase(nc, g, "norm2", lambda dve, ch, ln: ln.vector(dve, ch, g.xa, g.xb, "g2", "be2"), 1)
        feed_forward(nc, g, g.xa, g.xb, g.x1, g.agg, out)



def constants():
    k = np.arange(P)
    h = HEADS0
    shift = np.zeros((P, 2 * P), np.float32)
    shift[:, 0:P] = k[None, :] == k[:, None] + h
    shift[:, P:] = k[None, :] == k[:, None] - h
    return {
        "c_ident": np.eye(P, dtype=np.float32),
        "c_tri": (k[:, None] < k[None, :]).astype(np.float32),
        "c_iota": np.tile(np.arange(LO, dtype=np.float32), (P, 1)),
        "c_shift": shift,
        "c_node": np.tile(np.arange(NP, dtype=np.float32), (P, 1)),
        "c_step": np.tile(np.arange(STEPS, dtype=np.float32), (BLOCKS, 1)),
    }


def lay_out(inp):
    f = np.float32
    a = {k: np.asarray(v) for k, v in inp.items()}
    arrays = constants()
    x = np.zeros((NP, D), f)
    x[:NODES] = a["x"]
    arrays["x"] = x.reshape(BLOCKS, P, D).transpose(1, 0, 2).reshape(P, BLOCKS * D)
    nt = np.zeros(NP, np.int32)
    nt[:NODES] = a["node_type_3"]
    arrays["ntype"] = nt.reshape(BLOCKS, P).T
    cols = np.zeros((3, EP), np.int32)
    cols[0:2] = NP - 1
    cols[0, :EDGES], cols[1, :EDGES], cols[2, :EDGES] = a["src"], a["dst"], a["edge_type_6"]
    arrays["edge_cols"] = cols.reshape(3, TILES, P).transpose(2, 0, 1).reshape(P, 3 * TILES)
    following = np.append(cols[1], cols[1, -1:])
    arrays["dst_rows"] = np.stack([following[r * TILES:(r + 1) * TILES + 1] for r in range(P)])
    ea = np.zeros((D, EP), f)
    ea[:, :EDGES] = a["edge_attr_128"].T
    arrays["edge_attr"] = ea
    typed = np.stack([a["L0_gnn_Wk"], a["L0_gnn_Wv"], a["L0_gnn_Wq"], a["L0_gnn_Wa"]])
    arrays["w_typed"] = typed.reshape(4 * LAYERS * TYPES, D, D).transpose(1, 0, 2).reshape(D, -1)
    dh = D // HEADS0
    rel = np.zeros((LAYERS, 2, RELS, D, D), f)
    for which, name in enumerate(("L0_gnn_W_att", "L0_gnn_W_msg")):
        for h in range(HEADS0):
            rel[:, which, :, h * dh:(h + 1) * dh, h * dh:(h + 1) * dh] = a[name][:, h]
    arrays["w_rel"] = rel.reshape(LAYERS * 2 * RELS, D, D).transpose(1, 0, 2).reshape(D, -1)
    arrays["b_pri"] = np.repeat(a["L0_gnn_pri"].transpose(1, 0, 2).reshape(HEADS0, LAYERS * RELS), dh, 0)
    arrays["w_qkv"] = np.concatenate([a["L1_gnn_Wq"], a["L1_gnn_Wk"], a["L1_gnn_Wv"]], 1)
    arrays["w_o"], arrays["w_1"], arrays["w_c"] = a["L1_gnn_Wo"], a["L1_gnn_W1"], a["L1_gnn_Wc"]
    arrays["w_2"] = a["L1_gnn_W2"].reshape(4, D, D).transpose(1, 0, 2).reshape(D, 4 * D)
    arrays["b_1"] = a["L1_gnn_b1"].reshape(4, D).T
    rows = dict(ln_g0=a["L0_gnn_ln_g"][0], ln_g1=a["L0_gnn_ln_g"][1], ln_b0=a["L0_gnn_ln_b"][0],
                ln_b1=a["L0_gnn_ln_b"][1], agg_g=a["L0_gnn_agg_g"], agg_b=a["L0_gnn_agg_b"])
    for n in ("bq", "bk", "bv", "bo", "b2", "g1", "be1", "g2", "be2"):
        rows[n] = a["L1_gnn_" + n]
    arrays["b_rows"] = np.tile(np.concatenate([rows[n] for n in ROWS])[None], (P, 1))
    arrays["b_c"] = np.tile(a["L1_gnn_bc"][None], (P, 1))
    arrays["b_skip"] = np.tile(a["L0_gnn_skip"].reshape(1, -1), (P, 1))
    arrays["b_aggw"] = np.tile(a["L0_gnn_agg_w"][None], (P, 1))
    return {k: np.ascontiguousarray(v) for k, v in arrays.items()}


def kernel(**inputs):
    import concourse.bacc as _bacc
    from concourse.bass_utils import run_bass_kernel_spmd as _run

    nc = _bacc.Bacc("TRN2", target_bir_lowering=False, num_devices=1)
    arrays = lay_out(inputs)
    ins = {n: nc.dram_tensor(n, v.shape, mybir.dt.from_np(v.dtype), kind="ExternalInput").ap() for n, v in arrays.items()}
    out = nc.dram_tensor("out", (P, BLOCKS * D), F32, kind="ExternalOutput").ap()
    build_program(nc, ins, out)
    r = _run(nc, [arrays], core_ids=[0])
    got = np.asarray(r.results[0]["out"])
    return got.reshape(P, BLOCKS, D).transpose(1, 0, 2).reshape(NP, D)[:NODES]
```

```python
from contextlib import ExitStack

import numpy as np

import concourse.bass as bass
from concourse import mybir
from concourse.alu_op_type import AluOpType as ALU

F32 = mybir.dt.float32
BF16 = mybir.dt.bfloat16
I32 = mybir.dt.int32
ACT = mybir.ActivationFunctionType
X = mybir.AxisListType.X

P = 128
D = 128
NODES, EDGES = 3125, 50000
BLOCKS = -(-NODES // P)
NP = BLOCKS * P
CH = 7
TILES = 392
EP = TILES * P
CHUNKS = TILES // CH
PAIRS = CHUNKS // 2
RING = 8
LAPS = CHUNKS // RING
STEPS = TILES + BLOCKS - 1
TAIL = -(-STEPS // CH) - CHUNKS
LAG = -(-(CH + BLOCKS - 1) // CH) - 1
GROUP = 5
GROUPS = BLOCKS // GROUP
QUAD = 4
QUADS = TILES // QUAD
QUAD_LAG = -(-(QUAD + BLOCKS - 1) // QUAD) - 1
BANKS = QUAD_LAG + 1
QUAD_LAPS = QUADS // BANKS
QUAD_TAIL = STEPS // QUAD - QUADS
REC = 4
TYPES, RELS, LAYERS = 3, 6, 2
HEADS0, HEADS1 = 4, 8
MSG = 132
LO, HI = 64, NP // 64
BIG = 1.0e30
EPS = 1e-5
HID = 4 * D
ROWS = ["ln_g0", "ln_g1", "ln_b0", "ln_b1", "agg_g", "agg_b", "bq", "bk", "bv", "bo", "b2", "g1", "be1", "g2", "be2"]
SCAN_LEN = 2 * CH
SCANS = TILES // SCAN_LEN
SCAN_ROWS = SCANS * HEADS0


def spread(ap, axis, n):
    shape = list(ap.shape)
    shape.insert(axis, n)
    return ap.unsqueeze(axis).to_broadcast(shape)


def wait(eng, sem, count):
    if not isinstance(count, int) or count > 0:
        eng.wait_ge(sem, count)


def laps(eng, chunk, tail=True, peel=True):
    if peel:
        for j in range(RING):
            chunk(0, j, CH)
    with eng.Fori(1 if peel else 0, LAPS) as i:
        for j in range(RING):
            chunk(i, j, CH)
    if tail:
        for j in range(TAIL):
            chunk(LAPS, j, min(CH, STEPS - (CHUNKS + j) * CH))


def quad_laps(eng, body, tail=True, peel=True):
    def two(i):
        for j in range(2 * BANKS):
            body(i + j // BANKS, j % BANKS, j % 2)

    if peel:
        two(0)
    with eng.Fori(1 if peel else 0, QUAD_LAPS // 2) as pair:
        two(pair * 2)
    if tail:
        for j in range(QUAD_TAIL):
            body(QUAD_LAPS, j, j % 2)


def finished_quad(i, j):
    slot = (j - QUAD_LAG) % BANKS
    return i * BANKS + j - QUAD_LAG, slot, i if j >= QUAD_LAG else i - 1


def path_words(nc, eng, table, c, steps, per=CH):
    why = "path_table builds the words within their ranges"
    _, words = nc.values_load_multi_w_load_instructions(
        table[0:1, bass.ds(c * (4 * per), 4 * steps)], engines=[eng.engine], min_val=0, max_val=TILES - 1,
        skip_runtime_bounds_check_because=why)
    tops = (TILES, RING * CH, BLOCKS, BANKS * QUAD)
    return [[nc.s_assert_within(w, 0, top - 1, skip_runtime_bounds_check_because=why)
             for w, top in zip(words[4 * k:4 * k + 4], tops)] for k in range(steps)]


def flat(ap):
    return ap.rearrange("p a d -> p (a d)")


class Chain:

    def __init__(self, eng, done):
        self.eng, self.done, self.base, self.n = eng, done, 0, 0

    def __call__(self, ins):
        self.n += 1
        ins.then_inc(self.done, 1)
        self.eng.wait_ge(self.done, self.base + self.n)

    def later(self, ins):
        self.n += 1
        ins.then_inc(self.done, 1)

    def sync(self):
        self.eng.wait_ge(self.done, self.base + self.n)

    def enter(self, i, per):
        if self.n or not isinstance(self.base, int):
            self.start = self.base + self.n
        else:
            self.start = self.base
        self.base, self.n, self.per = self.start + i * per, 0, per

    def leave(self, trips):
        assert self.n == self.per
        self.base, self.n = self.start + trips * self.per, 0


class Phase:

    def __init__(self, nc, name):
        self.nc, self.name, self.stack, self.sems = nc, name, ExitStack(), []

    def __enter__(self):
        return self

    def __exit__(self, *a):
        self.stack.close()
        self.nc.clear_and_free_semaphores(self.sems)
        self.nc.all_engine_barrier()

    def sb(self, name, shape, dt=F32):
        return self.stack.enter_context(self.nc.sbuf_tensor(f"{self.name}_{name}", shape, dt))

    def ps(self, name, shape, dt=F32):
        return self.stack.enter_context(self.nc.psum_tensor(f"{self.name}_{name}", shape, dt))

    def sem(self, name):
        self.sems.append(self.nc.alloc_semaphore(f"{self.name}_{name}"))
        return self.sems[-1]

    def block(self):
        return self.nc.Block()


def load_inputs(nc, g):
    with Phase(nc, "load") as p:
        loaded, made, expd = p.sem("loaded"), p.sem("made"), p.sem("expd")
        ntype = p.sb("ntype", [P, BLOCKS], I32)
        ecols = p.sb("ecols", [P, REC, TILES], I32)
        skip = p.sb("skip", [P, LAYERS * TYPES])
        skipe = p.sb("skipe", [P, LAYERS * TYPES])
        aggw = p.sb("aggw", [P, 2])
        small = p.sb("small", [P, 8])
        ntf = p.sb("ntf", [P, BLOCKS])
        weights = [
            (g.wtyped[:], g.ins["w_typed"]), (g.wrel[:], g.ins["w_rel"]), (g.wqkv[:], g.ins["w_qkv"]), (g.wo[:], g.ins["w_o"]),
            (g.w1[:], g.ins["w_1"]), (g.w2[:], g.ins["w_2"]), (g.rows[:], g.ins["b_rows"]), (g.b1[:], g.ins["b_1"]),
            (g.pri[:], g.ins["b_pri"])]
        items = [
            (ntype[:], g.ins["ntype"]),
            (ecols[:], g.ins["edge_cols"].rearrange("p (a t) -> p a t", a=REC)), (g.ident[:], g.ins["c_ident"]),
            (g.tri[:], g.ins["c_tri"]), (g.iota[:], g.ins["c_iota"]), (g.shift[:], g.ins["c_shift"]),
            (g.steprow[:], g.ins["c_step"]), (g.wc[:], g.ins["w_c"]), (g.dst_rows[:], g.ins["dst_rows"]),
            (g.bc[:], g.ins["b_c"]), (skip[:], g.ins["b_skip"]), (aggw[:], g.ins["b_aggw"]),
        ]
        g.weights_asked = len(weights)
        with p.block() as block:
            @block.sync
            def _(sp):
                for dst, src in items[0::2]:
                    sp.dma_start(dst, src).then_inc(loaded, 16)

            @block.scalar
            def _(act):
                for dst, src in items[1::2]:
                    act.dma_start(dst, src).then_inc(loaded, 16)
                for dst, src in weights:
                    act.dma_start(dst, src).then_inc(g.weights_in, 16)
                act.wait_ge(loaded, 16 * len(items))
                nc.scalar.activation(skipe[:], skip[:], ACT.Exp, scale=-1.0).then_inc(expd, 1)
                act.wait_ge(made, 2)
                nc.scalar.activation(small[:, 4:6], small[:, 2:4], ACT.Exp, accum_out=small[:, 6:7]).then_inc(expd, 1)

            @block.vector
            def _(dve):
                ch = Chain(dve, made)
                dve.wait_ge(loaded, 16 * len(items))
                v = nc.vector
                ch(v.tensor_tensor(small[:, 0:1], aggw[:, 0:1], aggw[:, 1:2], ALU.max))
                ch(v.tensor_scalar(small[:, 2:4], aggw[:], small[:, 0:1], None, ALU.subtract))
                ch(v.memset(g.ones_bf[:], 1.0))
                ch(v.memset(g.ones[:], 1.0))
                ch(v.tensor_copy(g.tri_bf[:], g.tri[:]))
                ch(v.tensor_copy(g.ident_bf[:], g.ident[:]))
                ch(v.tensor_copy(g.iota_bf[:], g.iota[:]))
                for a in range(REC):
                    ch(v.tensor_copy(g.rec[:, :, a], ecols[:, a, :]))
                ch(v.tensor_copy(ntf[:], ntype[:]))
                for t in range(TYPES):
                    ch(v.tensor_single_scalar(g.mask[:, t, :], ntf[:], float(t), ALU.is_equal))
                dve.wait_ge(expd, 1)
                ch(v.tensor_scalar_add(skip[:], skipe[:], 1.0))
                ch(v.reciprocal(skipe[:], skip[:]))
                for l in range(LAYERS):
                    a = l * TYPES
                    ch(v.tensor_scalar(g.gate[:, l, :], g.mask[:, 0, :], skipe[:, a:a + 1], None, ALU.mult))
                    for t in range(1, TYPES):
                        ch(v.scalar_tensor_tensor(g.gate[:, l, :], g.mask[:, t, :], skipe[:, a + t:a + t + 1],
                                                  g.gate[:, l, :], ALU.mult, ALU.add))
                dve.wait_ge(expd, 2)
                ch(v.reciprocal(small[:, 7:8], small[:, 6:7]))
                ch(v.tensor_scalar(g.mixw[:], small[:, 4:6], small[:, 7:8], None, ALU.mult))


def copy_over(nc, dst, src, name):
    with Phase(nc, name) as p:
        copied = p.sem("copied")
        with p.block() as block:
            @block.sync
            def _(sp):
                sp.dma_start(dst, src).then_inc(copied, 16)
                sp.wait_ge(copied, 16)


def count_inversions(nc, g):
    with Phase(nc, "order") as p:
        made, summed = p.sem("made"), p.sem("summed")
        rows_f = p.sb("rows_f", [P, TILES + 1])
        above = p.sb("above", [P, TILES])
        per_row = p.sb("per_row", [P, 1])
        total = p.ps("total", [P, 512])
        with p.block() as block:
            @block.vector
            def _(dve):
                v, ch = nc.vector, Chain(dve, made)
                ch(v.tensor_copy(rows_f[:], g.dst_rows[:]))
                ch(v.tensor_tensor(above[:], rows_f[:, 0:TILES], rows_f[:, 1:TILES + 1], ALU.is_gt))
                ch(v.tensor_reduce(per_row[:], above[:], X, ALU.add))
                dve.wait_ge(summed, 1)
                ch(v.tensor_copy(g.unordered[:], total[0:1, 0:1]))

            @block.tensor
            def _(pe):
                pe.wait_ge(made, 3)
                nc.tensor.matmul(total[0:1, 0:1], g.ones[:, 0:1], per_row[:], start=True, stop=True).then_inc(summed, 1)


def digits(nc, g, word, name, and_with=None, shift=None):
    with Phase(nc, name) as p:
        a, b, made = p.sb("a", [P, TILES], I32), p.sb("b", [P, TILES], I32), p.sem("made")
        with p.block() as block:
            @block.vector
            def _(dve):
                ch = Chain(dve, made)
                ch(nc.vector.tensor_copy(a[:], g.rec[:, :, word]))
                if shift:
                    ch(nc.vector.tensor_single_scalar(b[:], a[:], shift, ALU.arith_shift_right))
                else:
                    ch(nc.vector.tensor_single_scalar(b[:], a[:], and_with, ALU.bitwise_and))
                ch(nc.vector.tensor_copy(g.keys[:], b[:]))


def count_keys(nc, g, groups, before, name):
    G = groups
    CT = 2 * CH if 2 * CH * G <= 512 else CH
    pairs = TILES // (2 * CT)
    with Phase(nc, name) as p:
        oh = p.sb("oh", [P, 2, CT, G], BF16)
        tot = [p.ps(f"tot{h}", [P, 512]) for h in range(2)]
        marked = [p.sem(f"marked{h}") for h in range(2)]
        summed = [p.sem(f"summed{h}") for h in range(2)]
        kept = [p.sem(f"kept{h}") for h in range(2)]
        done, zeroed, turn = p.sem("done"), p.sem("zeroed"), p.sem("turn")
        counts = before[:, 1:1 + G * TILES].rearrange("p (g t) -> p g t", t=TILES)
        with p.block() as block:
            @block.vector
            def _(dve):
                nc.vector.memset(before[:, 0:1], 0.0).then_inc(zeroed, 1)
                with dve.Fori(0, pairs) as i:
                    for h in range(2):
                        dve.wait_ge(summed[h], i)
                        nc.vector.tensor_tensor(oh[:, h], spread(g.keys[:, bass.ds((i * 2 + h) * CT, CT)], 2, G),
                                                spread(g.iota[:, 0:G], 1, CT), ALU.is_equal).then_inc(marked[h], 1)
                for h in range(2):
                    dve.wait_ge(kept[h], pairs)
                dve.wait_ge(zeroed, 1)
                flat = before[:, 1:1 + G * TILES]
                nc.vector.tensor_tensor_scan(out=flat, data0=flat, data1=flat, initial=0.0,
                                             op0=ALU.add, op1=ALU.max).then_inc(done, 1)
                dve.wait_ge(done, 1)

            @block.tensor
            def _(pe):
                with pe.Fori(0, pairs) as i:
                    for h in range(2):
                        pe.wait_ge(kept[h], i)
                        pe.wait_ge(marked[h], i + 1)
                        nc.tensor.matmul(tot[h][:, 0:CT * G], g.ones_bf[:], oh[:, h].rearrange("p t g -> p (t g)"),
                                         start=True, stop=True).then_inc(summed[h], 1)

            @block.scalar
            def _(act):
                with act.Fori(0, pairs) as i:
                    for h in range(2):
                        act.wait_ge(summed[h], i + 1)
                        act.sem_inc(turn, 1)
                        nc.scalar.copy(counts[:, :, bass.ds((i * 2 + h) * CT, CT)].rearrange("p g t -> p t g"),
                                       tot[h][:, 0:CT * G].rearrange("p (t g) -> p t g", g=G)).then_inc(kept[h], 1)


def count_blocks(nc, g, starts, name):
    G, CT = BLOCKS, 2 * CH
    pairs = TILES // (2 * CT)
    with Phase(nc, name) as p:
        oh = p.sb("oh", [P, 2, CT, G], BF16)
        zeros = p.sb("zeros", [P, CT * G], BF16)
        totals = p.sb("totals", [1, G + 1])
        sums = p.ps("sums", [P, 512])
        marked = [p.sem(f"marked{h}") for h in range(2)]
        summed = [p.sem(f"summed{h}") for h in range(2)]
        made, cleared = p.sem("made"), p.sem("cleared")
        with p.block() as block:
            @block.vector
            def _(dve):
                v, ch = nc.vector, Chain(dve, made)
                v.memset(zeros[:], 0.0).then_inc(cleared, 1)
                with dve.Fori(0, pairs) as i:
                    for h in range(2):
                        dve.wait_ge(summed[h], i)
                        v.tensor_tensor(oh[:, h], spread(g.keys[:, bass.ds((i * 2 + h) * CT, CT)], 2, G),
                                        spread(g.iota[:, 0:G], 1, CT), ALU.is_equal).then_inc(marked[h], 1)
                for h in range(2):
                    dve.wait_ge(summed[h], pairs)
                ch(v.memset(totals[:], 0.0))
                ch(v.tensor_reduce(totals[:, 1:1 + G], sums[0:1, 0:CT * G].rearrange("p (t g) -> p g t", g=G), X, ALU.add))
                ch(v.tensor_tensor_scan(out=starts, data0=totals[:, 0:G], data1=totals[:, 0:G], initial=0.0,
                                        op0=ALU.add, op1=ALU.max))

            @block.tensor
            def _(pe):
                pe.wait_ge(cleared, 1)
                nc.tensor.matmul(sums[:, 0:CT * G], zeros[:, 0:P], zeros[:], start=True, stop=True)
                with pe.Fori(0, pairs) as i:
                    for h in range(2):
                        pe.wait_ge(marked[h], i + 1)
                        nc.tensor.matmul(sums[:, 0:CT * G], g.ones_bf[:], oh[:, h].rearrange("p t g -> p (t g)"),
                                         start=False, stop=True, skip_group_check=True).then_inc(summed[h], 1)


def place_keys(nc, g, groups, before, name, records_to=None, positions=None, edge_attributes=False):
    G = groups
    CT = 2 * CH if 2 * CH * G <= 512 else CH
    pairs = TILES // (2 * CT)
    with Phase(nc, name) as p:
        oh = p.sb("oh", [P, 2, CT, G], BF16)
        pos = p.sb("pos", [P, 2, CT, G])
        posf = p.sb("posf", [P, 2, CT])
        idx = p.sb("idx", [P, 2, CT], I32)
        rec = p.sb("rec", [P, 2, CT, REC])
        above = [p.ps(f"above{h}", [P, 512]) for h in range(2)]
        marked = [p.sem(f"marked{h}") for h in range(2)]
        counted = [p.sem(f"counted{h}") for h in range(2)]
        indexed = [p.sem(f"indexed{h}") for h in range(2)]
        copied = [p.sem(f"copied{h}") for h in range(2)]
        scattered = [p.sem(f"scattered{h}") for h in range(2)]
        chain, turn = p.sem("chain"), p.sem("turn")
        if edge_attributes:
            assert CT == SCAN_LEN
            pieces, piece = 4, CT * P // 4
            ea = p.sb("ea", [P, 2, CT * P])
            edge_row = p.sb("edge_row", [HEADS1, 2, CT * P])
            edge_sums = [p.ps(f"edge_sums{k}", [P, 512]) for k in range(pieces)]
            ea_kept, rows_out = ([p.sem(f"{n}{h}") for h in range(2)] for n in ("ea_kept", "rows_out"))
            ea_in, ea_used = ([[p.sem(f"{n}{h}_{u}") for u in range(2)] for h in range(2)] for n in ("ea_in", "ea_used"))
        base = before[:, 0:G * TILES].rearrange("p (g t) -> p t g", t=TILES)
        with p.block() as block:
            @block.vector
            def _(dve):
                v, ch = nc.vector, Chain(dve, chain)
                with dve.Fori(0, pairs) as i:
                    ch.enter(i, 6)
                    for h in range(2):
                        v.tensor_tensor(oh[:, h], spread(g.keys[:, bass.ds((i * 2 + h) * CT, CT)], 2, G),
                                        spread(g.iota[:, 0:G], 1, CT), ALU.is_equal).then_inc(marked[h], 1)
                    for h in range(2):
                        dve.wait_ge(counted[h], i + 1)
                        ch(v.tensor_tensor(pos[:, h], above[h][:, 0:CT * G].rearrange("p (t g) -> p t g", g=G),
                                           base[:, bass.ds((i * 2 + h) * CT, CT), :], ALU.add))
                        ch(v.tensor_tensor(pos[:, h], pos[:, h], oh[:, h], ALU.mult))
                        if records_to is not None:
                            dve.wait_ge(scattered[h], i * (16 * CT))
                        ch(v.tensor_reduce(posf[:, h], pos[:, h], X, ALU.add))
                        out = idx[:, h] if records_to is not None else positions[:, bass.ds((i * 2 + h) * CT, CT)]
                        dve.sem_inc(turn, 1)
                        v.tensor_copy(out, posf[:, h]).then_inc(indexed[h], 1)
                    dve.wait_ge(indexed[0], i + 1)
                    dve.wait_ge(indexed[1], i + 1)
                ch.leave(pairs)

            @block.tensor
            def _(pe):
                with pe.Fori(0, pairs) as i:
                    for h in range(2):
                        pe.wait_ge(indexed[h], i)
                        pe.wait_ge(marked[h], i + 1)
                        nc.tensor.matmul(above[h][:, 0:CT * G], g.tri_bf[:], oh[:, h].rearrange("p t g -> p (t g)"),
                                         start=True, stop=True).then_inc(counted[h], 1)
                        if edge_attributes:
                            for k in range(pieces):
                                pe.wait_ge(ea_in[h][k // 2], i * 16 + 16)
                                if h:
                                    pe.wait_ge(ea_kept[0], i * pieces + k + 1)
                                else:
                                    pe.wait_ge(ea_kept[1], i * pieces)
                                nc.tensor.matmul(edge_sums[k][0:HEADS1, 0:piece], g.wc[:], ea[:, h, k * piece:(k + 1) * piece],
                                                 start=True, stop=True).then_inc(ea_used[h][k // 2], 1)

            if edge_attributes:
                @block.sync
                def _(sp):
                    with sp.Fori(0, pairs) as i:
                        for h in range(2):
                            for u in range(2):
                                sp.wait_ge(ea_used[h][u], i * 2)
                                sp.dma_start(ea[:, h, u * 2 * piece:(u + 1) * 2 * piece],
                                             g.ins["edge_attr"][:, bass.ds((i * 2 + h) * (CT * P) + u * 2 * piece, 2 * piece)])\
                                    .then_inc(ea_in[h][u], 16)

                @block.scalar
                def _(act):
                    with act.Fori(0, pairs) as i:
                        for h in range(2):
                            act.wait_ge(rows_out[h], i * 32)
                            for k in range(pieces):
                                act.wait_ge(ea_used[h][k // 2], i * 2 + k % 2 + 1)
                                nc.scalar.activation(edge_row[:, h, k * piece:(k + 1) * piece], edge_sums[k][0:HEADS1, 0:piece],
                                                     ACT.Identity, bias=g.bc[:]).then_inc(ea_kept[h], 1)
                            act.wait_ge(ea_kept[h], i * pieces + pieces)
                            for q in range(2):
                                act.dma_start(g.edge_rows[q, bass.ds(i * 2 + h, 1)].rearrange("c h l -> (c h) l"),
                                              edge_row[q * HEADS0:(q + 1) * HEADS0, h, :]).then_inc(rows_out[h], 16)
                    for h in range(2):
                        act.wait_ge(rows_out[h], pairs * 32)

            if records_to is not None:
                @block.scalar
                def _(act):
                    with act.Fori(0, pairs) as i:
                        for h in range(2):
                            act.wait_ge(scattered[h], i * (16 * CT))
                            act.sem_inc(turn, 1)
                            nc.scalar.copy(rec[:, h], g.rec[:, bass.ds((i * 2 + h) * CT, CT), :]).then_inc(copied[h], 1)

                @block.gpsimd
                def _(pool):
                    with pool.Fori(0, pairs) as i:
                        for h in range(2):
                            pool.wait_ge(copied[h], i + 1)
                            pool.wait_ge(indexed[h], i + 1)
                            pool.sem_inc(turn, 1)
                            for k in range(CT):
                                nc.gpsimd.indirect_dma_start(
                                    out=records_to, out_offset=bass.IndirectOffsetOnAxis(ap=idx[:, h, k:k + 1], axis=0),
                                    in_=rec[:, h, k, :], in_offset=None).then_inc(scattered[h], 16)
                    for h in range(2):
                        pool.wait_ge(scattered[h], pairs * 16 * CT)


def read_records(nc, g, source, name):
    with Phase(nc, name) as p:
        landed = p.sem("landed")
        with p.block() as block:
            @block.sync
            def _(sp):
                sp.dma_start(g.rec[:], source.rearrange("(t p) w -> p t w", p=P)).then_inc(landed, 16)
                sp.wait_ge(landed, 16)


def path_table(nc, g, starts, table, name):
    with Phase(nc, name) as p:
        made, counted = p.sem("made"), p.sem("counted")
        B, S = BLOCKS, STEPS
        R = max(B, SCANS)
        fi = p.sb("fi", [1, 2, B], I32)
        f = p.sb("f", [1, 2, B])
        one_row = p.sb("one_row", [1, R])
        cols = p.sb("cols", [R, 4])
        cmp = p.sb("cmp", [R, 3, S])
        tf = p.sb("tf", [1, S, 4])
        wraps = p.sb("wraps", [1, S])
        small, node, tiles = p.ps("small", [P, 512]), p.ps("node", [P, 512]), p.ps("tiles", [P, 512])
        wrap = [p.ps(f"wrap{a}", [P, 512]) for a in range(2)]
        widths = (RING * CH, BANKS * QUAD)
        with p.block() as block:
            @block.vector
            def _(dve):
                v, ch = nc.vector, Chain(dve, made)
                ch(v.tensor_copy(fi[:, 0, :], starts))
                ch(v.tensor_single_scalar(fi[:, 1, :], fi[:, 0, :], 7, ALU.arith_shift_right))
                ch(v.tensor_copy(f[:, 0, :], fi[:, 1, :]))
                ch(v.tensor_scalar(f[:, 0, :], f[:, 0, :], float(TILES - 1), None, ALU.min))
                ch(v.memset(one_row[:], 1.0))
                ch(v.tensor_tensor(f[:, 1, :], f[:, 0, :], g.iota[0:1, 0:B], ALU.add))
                ch(v.memset(tf[:], 0.0))
                dve.wait_ge(counted, 1)
                ch(v.tensor_copy(cols[0:B, 0:1], small[0:B, 0:1]))
                ch(v.tensor_copy(cols[:, 1:2], small[0:R, 1:2]))
                for a, w in enumerate(widths):
                    ch(v.tensor_scalar(cols[:, 2 + a:3 + a], cols[:, 1:2], float(w), float(w), ALU.mult, ALU.add))
                ch(v.tensor_scalar(cmp[0:B, 0, :], g.steprow[0:B, :], cols[0:B, 0:1], None, ALU.is_ge))
                dve.wait_ge(counted, 2)
                ch(v.tensor_scalar(tf[:, :, 2], node[0:1, 0:S], 1.0, None, ALU.subtract))
                ch(v.tensor_tensor(tf[:, :, 0], g.steprow[0:1, :], tf[:, :, 2], ALU.subtract))
                dve.wait_ge(counted, 3)
                for a in range(2):
                    ch(v.tensor_scalar(cmp[:, 1 + a, :], tiles[0:R, 0:S], cols[:, 2 + a:3 + a], None, ALU.is_ge))
                dve.wait_ge(counted, 4)
                for a, w in enumerate(widths):
                    ch(v.tensor_copy(wraps[:], wrap[a][0:1, 0:S]))
                    ch(v.scalar_tensor_tensor(tf[:, :, 1 + 2 * a], wraps[:], -float(w), tf[:, :, 0], ALU.mult, ALU.add))
                ch(v.tensor_copy(table[:], tf[:].rearrange("p s w -> p (s w)")))

            @block.tensor
            def _(pe):
                mm = nc.tensor.matmul
                pe.wait_ge(made, 6)
                mm(small[0:B, 0:1], f[:, 1, :], one_row[:, 0:1], start=True, stop=True)
                mm(small[0:R, 1:2], g.iota[0:1, 0:R], one_row[:, 0:1], start=True, stop=True).then_inc(counted, 1)
                pe.wait_ge(made, 12)
                mm(node[0:1, 0:S], g.ones[0:B, 0:1], cmp[0:B, 0, :], start=True, stop=True).then_inc(counted, 1)
                pe.wait_ge(made, 14)
                mm(tiles[0:R, 0:S], one_row[:], tf[:, :, 0], start=True, stop=True).then_inc(counted, 1)
                pe.wait_ge(made, 16)
                for a in range(2):
                    last = mm(wrap[a][0:1, 0:S], g.ones[0:R, 0:1], cmp[:, 1 + a, :], start=True, stop=True)
                last.then_inc(counted, 1)


def edge_indices(nc, g):
    with Phase(nc, "cols") as p:
        p.sems.append(g.weights_in)
        made = p.sem("made")
        f = p.sb("f", [P, TILES])
        with p.block() as block:
            @block.vector
            def _(dve):
                v, ch = nc.vector, Chain(dve, made)
                ch(v.scalar_tensor_tensor(f[:], g.rec[:, :, 0], float(RELS), g.rec[:, :, 2], ALU.mult, ALU.add))
                ch(v.tensor_copy(g.rel_idx[:], f[:]))
                ch(v.tensor_copy(g.src_idx[:], g.rec[:, :, 0]))
                ch(v.tensor_copy(g.dst[:], g.rec[:, :, 1]))
                ch(v.tensor_copy(g.src[:], g.rec[:, :, 0]))
                ch(v.tensor_copy(g.number[:], g.rec[:, :, 3]))
                dve.wait_ge(g.weights_in, 16 * g.weights_asked)
                ch(v.tensor_scalar(g.pri[:], g.pri[:], float(D // HEADS0) ** -0.5, None, ALU.mult))
                for l in range(LAYERS):
                    w = g.relation(0, l).rearrange("p (r d) -> p r d", d=D)
                    ch(v.tensor_tensor(w, w, spread(g.pri[:, l * RELS:(l + 1) * RELS], 2, D), ALU.mult))


class Norms:

    def __init__(self, nc, p, g):
        self.nc, self.g, self.n = nc, g, 0
        self.var_ready, self.std_ready = p.sem("var_ready"), p.sem("std_ready")
        self.measured = p.sem("measured")
        self.parts = p.sb("parts", [P, BLOCKS, 6])
        self.st = p.sb("st", [P, 5, BLOCKS])

    def vector(self, dve, ch, out, src, gain=None, bias=None, relu=False):
        v, st, parts, n = self.nc.vector, self.st, self.parts, self.n
        self.n += 1
        for b in range(BLOCKS):
            v.bn_stats(parts[:, b, :], src[:, b, :]).then_inc(self.measured, 1)
        dve.wait_ge(self.measured, (n + 1) * BLOCKS)
        half = D // 2
        ch(v.tensor_tensor(st[:, 0, :], parts[:, :, 1], parts[:, :, 4], ALU.add))
        ch(v.tensor_tensor(st[:, 1, :], parts[:, :, 1], parts[:, :, 4], ALU.subtract))
        ch(v.tensor_tensor(st[:, 2, :], parts[:, :, 2], parts[:, :, 5], ALU.add))
        ch(v.tensor_scalar(st[:, 0, :], st[:, 0, :], 0.5, None, ALU.mult))
        ch(v.tensor_tensor(st[:, 1, :], st[:, 1, :], st[:, 1, :], ALU.mult))
        ch(v.scalar_tensor_tensor(st[:, 2, :], st[:, 1, :], half / 2, st[:, 2, :], ALU.mult, ALU.add))
        v.tensor_scalar(st[:, 3, :], st[:, 2, :], 1.0 / D, EPS, ALU.mult, ALU.add).then_inc(self.var_ready, 1)
        dve.wait_ge(self.std_ready, n + 1)
        ch(v.reciprocal(st[:, 1, :], st[:, 4, :]))
        for b in range(BLOCKS):
            mean, rstd = st[:, 0, b:b + 1], st[:, 1, b:b + 1]
            if gain is None:
                ch.later(v.tensor_scalar(out[:, b, :], src[:, b, :], mean, rstd, ALU.subtract, ALU.mult))
            else:
                ch.later(v.scalar_tensor_tensor(out[:, b, :], src[:, b, :], mean, self.g.row(gain), ALU.subtract, ALU.mult))
        ch.sync()
        if gain is not None:
            for b in range(BLOCKS):
                ch.later(v.scalar_tensor_tensor(out[:, b, :], out[:, b, :], st[:, 1, b:b + 1], self.g.row(bias), ALU.mult, ALU.add))
            ch.sync()
        if relu:
            ch(v.tensor_scalar_max(out[:], out[:], 0.0))

    def scalar(self, act, norms):
        for n in range(norms):
            act.wait_ge(self.var_ready, n + 1)
            self.nc.scalar.activation(self.st[:, 4, :], self.st[:, 3, :], ACT.Sqrt).then_inc(self.std_ready, 1)


def norm_phase(nc, g, name, work, norms, load=None):
    with Phase(nc, name) as p:
        made = p.sem("made")
        ln = Norms(nc, p, g)
        ln.loaded = p.sem("loaded")
        with p.block() as block:
            if load:
                @block.sync
                def _(sp):
                    sp.dma_start(*load).then_inc(ln.loaded, 16)

            @block.vector
            def _(dve):
                work(dve, Chain(dve, made), ln)

            @block.scalar
            def _(act):
                ln.scalar(act, norms)


def split(nc, dve, ch, parts, at, src, rest):
    v = nc.vector

    def part(a):
        return parts[:, at, a, :]

    ch(v.tensor_scalar(part(0), src, 1.0, None, ALU.mult))
    ch(v.tensor_tensor(rest, src, part(0), ALU.subtract))
    ch(v.tensor_scalar(part(1), rest, 1.0, None, ALU.mult))
    ch(v.tensor_tensor(part(2), rest, part(1), ALU.subtract))


def typed_tables(nc, g, layer, x):
    with Phase(nc, f"tab{layer}") as p:
        xm = p.sb("xm", [P, TYPES, D])
        xt = p.sb("xt", [P, TYPES, D])
        kvq = p.sb("kvq", [P, 3, D])
        tab = p.sb("tab", [P, RELS, 2, D])
        pt, pk, pvq = p.ps("pt", [P, 512]), p.ps("pk", [P, 512]), p.ps("pvq", [P, 512])
        pr = [p.ps(f"pr{j}", [P, 512]) for j in range(4)]
        masked, turned, xt_ready, projected = p.sem("masked"), p.sem("turned"), p.sem("xt_ready"), p.sem("projected")
        kvq_ready, related, tab_ready = p.sem("kvq_ready"), p.sem("related"), p.sem("tab_ready")
        tab_out, chain = p.sem("tab_out"), p.sem("chain")
        rest = p.sb("rest", [P, 1, D])
        half = RELS - 4
        with p.block() as block:
            @block.vector
            def _(dve):
                v, ch = nc.vector, Chain(dve, chain)

                def mask(b):
                    wait(dve, turned, b)
                    for t in range(TYPES):
                        v.tensor_scalar(xm[:, t, :], flat(x[:, bass.ds(b, 1), :]), g.mask[:, t, bass.ds(b, 1)], None,
                                        ALU.mult).then_inc(masked, 1)

                def queries_and_keys(b):
                    dve.wait_ge(kvq_ready, b * 2 + 2)
                    split(nc, dve, ch, g.q_parts, bass.ds(b, 1), kvq[:, 2:3, :], rest[:])
                    wait(dve, tab_out, b * 16)
                    dve.wait_ge(related, b + 1)
                    v.tensor_copy(tab[:, 0:4, 0, :], pr[0][:].rearrange("p (r d) -> p r d", d=D)).then_inc(tab_ready, 1)
                    v.tensor_copy(tab[:, 4:RELS, 0, :], pr[1][:, 0:half * D].rearrange("p (r d) -> p r d", d=D)).then_inc(tab_ready, 1)

                mask(0)
                with dve.Fori(0, BLOCKS - 1) as b:
                    ch.enter(b, 4)
                    mask(b + 1)
                    queries_and_keys(b)
                ch.leave(BLOCKS - 1)
                queries_and_keys(BLOCKS - 1)

            @block.tensor
            def _(pe):
                t_ = nc.tensor

                def turn_rows(b):
                    wait(pe, xt_ready, b)
                    pe.wait_ge(masked, b * TYPES + TYPES)
                    for t in range(TYPES):
                        mm = t_.transpose(pt[:, t * D:(t + 1) * D], xm[:, t, :], g.ident[:])
                    mm.then_inc(turned, 1)

                def project(b):
                    wait(pe, kvq_ready, b * 2)
                    pe.wait_ge(xt_ready, b + 1)
                    for a, to in enumerate((pk[:, 0:D], pvq[:, 0:D], pvq[:, D:2 * D])):
                        for t in range(TYPES):
                            w = g.typed(a, layer, t)
                            lhs, rhs = (w, xt[:, t, :]) if a < 2 else (xt[:, t, :], w)
                            mm = t_.matmul(to, lhs, rhs, start=(t == 0), stop=(t == TYPES - 1))
                        if a != 1:
                            mm.then_inc(projected, 1)

                def relate(b):
                    wait(pe, tab_ready, b * 4)
                    for a in range(2):
                        pe.wait_ge(kvq_ready, b * 2 + 1 + a)
                        w = g.relation(a, layer)
                        t_.matmul(pr[2 * a][:, 0:4 * D], kvq[:, a, :], w[:, 0:4 * D], start=True, stop=True)
                        mm = t_.matmul(pr[2 * a + 1][:, 0:half * D], kvq[:, a, :], w[:, 4 * D:RELS * D], start=True, stop=True)
                    mm.then_inc(related, 1)

                turn_rows(0)
                with pe.Fori(0, BLOCKS - 1) as b:
                    project(b)
                    turn_rows(b + 1)
                    relate(b)
                project(BLOCKS - 1)
                relate(BLOCKS - 1)

            @block.scalar
            def _(act):
                s = nc.scalar

                def keep_turned(b):
                    wait(act, projected, b * 2)
                    act.wait_ge(turned, b + 1)
                    s.copy(xt[:].rearrange("p t d -> p (t d)"), pt[:, 0:TYPES * D]).then_inc(xt_ready, 1)

                def keep_projected(b):
                    wait(act, related, b)
                    act.wait_ge(projected, b * 2 + 1)
                    s.copy(kvq[:, 0, :], pk[:, 0:D]).then_inc(kvq_ready, 1)
                    wait(act, chain, b * 4)
                    act.wait_ge(projected, b * 2 + 2)
                    s.copy(kvq[:, 1:3, :].rearrange("p a d -> p (a d)"), pvq[:, 0:2 * D]).then_inc(kvq_ready, 1)

                def keep_values(b):
                    wait(act, tab_out, b * 16)
                    act.wait_ge(related, b + 1)
                    s.copy(tab[:, 0:4, 1, :], pr[2][:].rearrange("p (r d) -> p r d", d=D)).then_inc(tab_ready, 1)
                    s.copy(tab[:, 4:RELS, 1, :], pr[3][:, 0:half * D].rearrange("p (r d) -> p r d", d=D)).then_inc(tab_ready, 1)

                keep_turned(0)
                with act.Fori(0, BLOCKS - 1) as b:
                    keep_projected(b)
                    keep_turned(b + 1)
                    keep_values(b)
                keep_projected(BLOCKS - 1)
                keep_values(BLOCKS - 1)

            @block.sync
            def _(sp):
                with sp.Fori(0, BLOCKS) as b:
                    sp.wait_ge(tab_ready, b * 4 + 4)
                    sp.dma_start(g.rel_tab.rearrange("(n r) w -> n (r w)", r=RELS)[bass.ds(b * P, P), :],
                                 tab[:].rearrange("p r a d -> p (r a d)")).then_inc(tab_out, 16)
                sp.wait_ge(tab_out, BLOCKS * 16)


def local_targets(nc, g):
    T = TILES // 4
    with Phase(nc, "near") as p:
        rows = p.sb("rows", [1, 2, STEPS])
        one_row = p.sb("one_row", [1, P])
        column = p.sb("column", [P, 4])
        dst_t = p.sb("dst_t", [T, 4, P])
        pick = p.sb("pick", [T, 4, STEPS])
        tile_b, node_b, turned, picked, count = (p.ps(n, [P, 512]) for n in ("tile_b", "node_b", "turned", "picked", "count"))
        base = p.sb("base", [P, STEPS])
        made, done, nodes_in = p.sem("made"), p.sem("done"), p.sem("nodes_in")
        words = g.tab_dst[:].rearrange("p (s w) -> p s w", w=4)
        with p.block() as block:
            @block.sync
            def _(sp):
                sp.dma_start(g.xb[:], g.ins["x"].rearrange("p (b d) -> p b d", d=D)).then_inc(nodes_in, 16)
                sp.wait_ge(nodes_in, 16)

            @block.vector
            def _(dve):
                v, ch = nc.vector, Chain(dve, made)
                ch(v.memset(one_row[:], 1.0))
                ch(v.tensor_copy(rows[:, 0, :], words[:, :, 0]))
                ch(v.tensor_copy(rows[:, 1, :], words[:, :, 2]))
                dve.wait_ge(done, 1)
                for a in range(4):
                    ch(v.tensor_scalar(column[:, a:a + 1], count[:, 0:1], float(a * T), None, ALU.add))
                ch(v.tensor_copy(dst_t[:], turned[0:T, :].rearrange("p (a e) -> p a e", e=P)))
                for a in range(4):
                    ch(v.tensor_scalar(pick[:, a, :], tile_b[0:T, 0:STEPS], column[0:T, a:a + 1], None, ALU.is_equal))
                ch(v.tensor_scalar(base[:], node_b[:, 0:STEPS], float(P), None, ALU.mult))
                dve.wait_ge(done, 2)
                ch(v.tensor_tensor(g.near_dst[:], picked[:, 0:STEPS], base[:], ALU.subtract))

            @block.tensor
            def _(pe):
                t_ = nc.tensor
                t_.matmul(count[:, 0:1], g.tri_bf[:], g.ones_bf[:, 0:1], start=True, stop=True)
                for a in range(4):
                    t_.transpose(turned[0:T, a * P:(a + 1) * P], g.dst[:, a * T:(a + 1) * T], g.ident[:])
                pe.wait_ge(made, 3)
                t_.matmul(tile_b[:, 0:STEPS], one_row[:], rows[:, 0, :], start=True, stop=True)
                t_.matmul(node_b[:, 0:STEPS], one_row[:], rows[:, 1, :], start=True, stop=True).then_inc(done, 1)
                pe.wait_ge(made, 12)
                for a in range(4):
                    mm = t_.matmul(picked[:, 0:STEPS], dst_t[:, a, :], pick[:, a, :], start=(a == 0), stop=(a == 3))
                mm.then_inc(done, 1)


def turn_edge_scores(nc, g, name, to_columns):
    J, G, R, L = SCAN_LEN, 7, SCAN_ROWS, SCAN_LEN * P
    JG = J // G
    with Phase(nc, name) as p:
        rows = p.sb("rows", [R, L])
        columns = p.sb("columns", [P, J, SCANS, HEADS0])
        bank = [p.ps(f"bank{j}", [P, 512]) for j in range(G)]
        moved, turned, made = p.sem("moved"), p.sem("turned"), p.sem("made")
        for_each = g.edge_sc[:].rearrange("p (c j) (q h) -> p q j c h", j=J, q=2)
        in_dram = [g.edge_rows[q].rearrange("c h l -> (c h) l") for q in range(2)]
        with p.block() as block:
            @block.sync
            def _(sp):
                for q in range(2):
                    if to_columns:
                        wait(sp, turned, q)
                        sp.dma_start(rows[:], in_dram[q]).then_inc(moved, 16)
                    else:
                        sp.wait_ge(made, (q + 1) * (1 + G))
                        sp.dma_start(in_dram[q], rows[:]).then_inc(moved, 16)
                sp.wait_ge(moved, 32)

            @block.tensor
            def _(pe):
                for q in range(2):
                    if to_columns:
                        pe.wait_ge(moved, 16 * q + 16)
                        wait(pe, made, q * G)
                        for j in range(J):
                            mm = nc.tensor.transpose(bank[j // JG][:, (j % JG) * R:(j % JG + 1) * R], rows[:, j * P:(j + 1) * P],
                                                     g.ident[0:R, 0:R])
                    else:
                        pe.wait_ge(made, q * (1 + G) + 1)
                        for j in range(J):
                            mm = nc.tensor.transpose(bank[j // JG][0:R, (j % JG) * P:(j % JG + 1) * P],
                                                     columns[:, j].rearrange("p c h -> p (c h)"), g.ident[:])
                    mm.then_inc(turned, 1)

            @block.vector
            def _(dve):
                v, ch = nc.vector, Chain(dve, made)
                for q in range(2):
                    if not to_columns:
                        ch(v.tensor_copy(columns[:], for_each[:, q]))
                        wait(dve, moved, 16 * q)
                    dve.wait_ge(turned, q + 1)
                    for j in range(G):
                        if to_columns:
                            ch(v.tensor_copy(for_each[:, q, j * JG:(j + 1) * JG],
                                             bank[j][:, 0:JG * R].rearrange("p (j c h) -> p j c h", j=JG, h=HEADS0)))
                        else:
                            ch(v.tensor_copy(rows[:, j * JG * P:(j + 1) * JG * P], bank[j][0:R, 0:JG * P]))


def sort_edge_scores(nc, g):
    copy_over(nc, g.by_edge.rearrange("(t p) w -> p t w", p=P), g.edge_sc[:], "by_edge_out")
    with Phase(nc, "by_edge_in") as p:
        idx, rows = p.sb("idx", [P, 2, CH], I32), p.sb("rows", [P, 2, CH, HEADS1])
        indexed, turn = p.sem("indexed"), p.sem("turn")
        gathered, kept = [p.sem(f"gathered{h}") for h in range(2)], [p.sem(f"kept{h}") for h in range(2)]
        with p.block() as block:
            @block.scalar
            def _(act):
                with act.Fori(0, PAIRS) as i:
                    for h in range(2):
                        act.wait_ge(gathered[h], i * (16 * CH))
                        act.sem_inc(turn, 1)
                        nc.scalar.copy(idx[:, h, :], g.number[:, bass.ds((i * 2 + h) * CH, CH)]).then_inc(indexed, 1)

            @block.gpsimd
            def _(pool):
                with pool.Fori(0, PAIRS) as i:
                    for h in range(2):
                        pool.wait_ge(kept[h], i)
                        pool.wait_ge(indexed, i * 2 + h + 1)
                        pool.sem_inc(turn, 1)
                        for k in range(CH):
                            nc.gpsimd.indirect_dma_start(
                                out=rows[:, h, k, :], out_offset=None, in_=g.by_edge,
                                in_offset=bass.IndirectOffsetOnAxis(ap=idx[:, h, k:k + 1], axis=0)).then_inc(gathered[h], 16)

            @block.vector
            def _(dve):
                with dve.Fori(0, PAIRS) as i:
                    for h in range(2):
                        dve.wait_ge(gathered[h], i * (16 * CH) + 16 * CH)
                        dve.sem_inc(turn, 1)
                        nc.vector.tensor_copy(g.edge_sc[:, bass.ds((i * 2 + h) * CH, CH), :], rows[:, h]).then_inc(kept[h], 1)
                for h in range(2):
                    dve.wait_ge(kept[h], PAIRS)


class OneHots:

    def __init__(self, nc, g, p):
        self.nc, self.g = nc, g
        self.oh = p.sb("oh", [P, 2, QUAD, P], BF16)
        self.oht = p.sb("oht", [P, 2, QUAD * P], BF16)
        self.turned = p.ps("turned", [P, QUAD * P], BF16)
        self.marked, self.flipped, self.copied = p.sem("marked"), p.sem("flipped"), p.sem("copied")

    def mark(self, dve, n, h):
        wait(dve, self.flipped, n - 1)
        mark_steps(self.nc, self.g, self.oh[:, h], n * QUAD, QUAD).then_inc(self.marked, 1)

    def turn(self, pe, n, h):
        wait(pe, self.marked, n + 1)
        wait(pe, self.copied, n)
        for k in range(QUAD):
            mm = self.nc.tensor.transpose(self.turned[:, k * P:(k + 1) * P], self.oh[:, h, k, :], self.g.ident_bf[:])
        return mm

    def keep(self, act, multiplied, n, h):
        wait(act, self.flipped, n + 1)
        wait(act, multiplied, n - 1)
        return self.nc.scalar.copy(self.oht[:, h], self.turned[:])

    def expand(self, pe, n, h, banks, parts):
        words = path_words(self.nc, pe, self.g.tab_dst, n, QUAD, QUAD)
        for k, (_, _, node, slot) in enumerate(words):
            for a in range(3):
                mm = self.nc.tensor.matmul(flat(banks[:, bass.ds(slot, 1), :]), self.oht[:, h, k * P:(k + 1) * P],
                                           flat(parts[:, bass.ds(node, 1), a, :]), start=False, stop=True, skip_group_check=True)
        return mm


def mark_steps(nc, g, out, first, steps):
    return nc.vector.tensor_tensor(out, spread(g.near_dst[:, bass.ds(first, steps)], 2, P), spread(g.iota_bf[:], 1, steps),
                                   ALU.is_equal)


def gather_scores(nc, g, heads, with_values, tab, idx, near, name):
    H = heads
    W = 2 * D if with_values else D
    with Phase(nc, name) as p:
        ring = p.sb("ring", [P, BANKS, QUAD, W])
        prod = p.sb("prod", [P, 2, QUAD, D])
        cur = p.sb("cur", [P, BANKS, QUAD], I32)
        zeros = p.sb("zeros", [P, 512], BF16)
        near_rows = p.ps("near_rows", [P, BANKS * QUAD, P])
        ones = OneHots(nc, g, p)
        gathered = [p.sem(f"gathered{j}") for j in range(BANKS)]
        values_out = [p.sem(f"values_out{j}") for j in range(BANKS)]
        indexed, multiplied, scored, summed, cleared, turn = (
            p.sem(n) for n in ("indexed", "multiplied", "scored", "summed", "cleared", "turn"))
        per = 16 * QUAD
        in_tail = lambda i: isinstance(i, int) and i == QUAD_LAPS
        last = lambda i, j: in_tail(i) and j == QUAD_TAIL - 1
        near_end = lambda i, j: in_tail(i) and j >= QUAD_TAIL - 2
        with p.block() as block:
            @block.scalar
            def _(act):
                def quad(i, j, parity):
                    n = i * BANKS + j
                    ones.keep(act, multiplied, n, parity).then_inc(ones.copied, 1)
                    if not in_tail(i):
                        wait(act, gathered[j], i * per)
                        act.sem_inc(turn, 1)
                        nc.scalar.copy(cur[:, j, :], idx[:, bass.ds(n * QUAD, QUAD)]).then_inc(indexed, 1)

                quad_laps(act, quad)

            @block.gpsimd
            def _(pool):
                def quad(i, j, parity):
                    n = i * BANKS + j
                    pool.wait_ge(indexed, n + 1)
                    if not isinstance(i, int) or i > 0:
                        pool.wait_ge(scored, n - BANKS + 1)
                        if with_values:
                            pool.wait_ge(values_out[j], i * 16)
                    pool.sem_inc(turn, 1)
                    for k in range(QUAD):
                        nc.gpsimd.indirect_dma_start(
                            out=ring[:, j, k, :], out_offset=None, in_=tab,
                            in_offset=bass.IndirectOffsetOnAxis(ap=cur[:, j, k:k + 1], axis=0)).then_inc(gathered[j], 16)

                quad_laps(pool, quad, tail=False)

            @block.sync
            def _(sp):
                def quad(i, j, parity):
                    n = i * BANKS + j
                    if with_values:
                        sp.wait_ge(gathered[j], i * per + per)
                        sp.sem_inc(turn, 1)
                        sp.dma_start(g.values[:, bass.ds(n * QUAD, QUAD), :], ring[:, j, :, D:2 * D]).then_inc(values_out[j], 16)

                if with_values:
                    quad_laps(sp, quad, tail=False)
                    for j in range(BANKS):
                        sp.wait_ge(values_out[j], QUAD_LAPS * 16)

            @block.tensor
            def _(pe):
                pe.wait_ge(cleared, 1)
                ones.turn(pe, 0, 0).then_inc(ones.flipped, 1)

                def quad(i, j, parity):
                    n = i * BANKS + j
                    if not in_tail(i):
                        if not isinstance(i, int) or i > 0:
                            pe.wait_ge(scored, n - BANKS + 1)
                        nc.tensor.matmul(near_rows[:, j * QUAD:(j + 1) * QUAD, :].rearrange("p t d -> p (t d)"), zeros[:, 0:P],
                                         zeros[:], start=True, stop=True)
                    pe.wait_ge(ones.copied, n + 1)
                    pe.sem_inc(turn, 1)
                    ones.expand(pe, n, parity, near_rows, near).then_inc(multiplied, 1)
                    if not last(i, j):
                        ones.turn(pe, n + 1, 1 - parity).then_inc(ones.flipped, 1)

                quad_laps(pe, quad)

            @block.vector
            def _(dve):
                v = nc.vector
                v.memset(zeros[:], 0.0).then_inc(cleared, 1)
                ones.mark(dve, 0, 0)
                ones.mark(dve, 1, 1)

                def quad(i, j, parity):
                    n = i * BANKS + j
                    if isinstance(i, int) and n < QUAD_LAG:
                        ones.mark(dve, n + 2, parity)
                        return
                    m, slot, lap = finished_quad(i, j)
                    dve.wait_ge(multiplied, n + 1)
                    dve.wait_ge(gathered[slot], lap * per + per)
                    wait(dve, summed, m - 1)
                    half = parity
                    v.tensor_tensor(prod[:, half], ring[:, slot, :, 0:D], near_rows[:, slot * QUAD:(slot + 1) * QUAD, :],
                                    ALU.mult).then_inc(scored, 1)
                    if not near_end(i, j):
                        ones.mark(dve, n + 2, parity)
                    dve.wait_ge(scored, m + 1)
                    dve.sem_inc(turn, 1)
                    v.tensor_reduce(g.score[:, bass.ds(m * QUAD, QUAD), 0:H],
                                    prod[:, half].rearrange("p t (h d) -> p t h d", h=H), X, ALU.add).then_inc(summed, 1)

                quad_laps(dve, quad)
                dve.wait_ge(summed, QUADS)


def segment_bounds(nc, g):
    H, J, G, R = HEADS0, SCAN_LEN, 7, SCAN_ROWS
    JG, L = J // G, J * P
    with Phase(nc, "bounds") as p:
        seg = p.sb("seg", [R, L])
        columns = p.sb("columns", [P, J, SCANS, H])
        bank = [p.ps(f"bank{j}", [P, 512]) for j in range(G)]
        small = p.ps("small", [P, 512])
        made, done = p.sem("made"), p.sem("done")
        cont = g.cont
        with p.block() as block:
            @block.vector
            def _(dve):
                v, ch = nc.vector, Chain(dve, made)
                ch(v.tensor_scalar_add(columns[:], spread(g.dst[:].rearrange("p (c j) -> p j c", j=J), 3, H), 1.0))
                dve.wait_ge(done, 1)
                for j in range(G):
                    keep = ch.later if j < G - 1 else ch
                    keep(v.tensor_copy(seg[:, j * JG * P:(j + 1) * JG * P], bank[j][0:R, 0:JG * P]))
                ch(v.tensor_tensor(cont[:, 1:L], seg[:, 1:L], seg[:, 0:L - 1], ALU.is_equal))
                dve.wait_ge(done, 2)
                ch(v.tensor_tensor(cont[:, 0:1], seg[:, 0:1], small[0:R, 0:1], ALU.is_equal))
                ch(v.tensor_tensor(cont[:, L:L + 1], seg[:, L - 1:L], small[0:R, 1:2], ALU.is_equal))
                ch(v.tensor_reduce(g.all_cont[:, 0:1], cont[:, 0:L], X, ALU.min))
                ch(v.tensor_reduce(g.all_cont[:, 1:2], cont[:, 1:L + 1], X, ALU.min))

            @block.tensor
            def _(pe):
                t_ = nc.tensor
                pe.wait_ge(made, 1)
                for j in range(J):
                    at = bank[j // JG][0:R, (j % JG) * P:(j % JG + 1) * P]
                    mm = t_.transpose(at, columns[:, j].rearrange("p c h -> p (c h)"), g.ident[:])
                mm.then_inc(done, 1)
                pe.wait_ge(made, 1 + G)
                t_.matmul(small[0:R, 0:1], g.shift[0:R, 0:R], seg[:, L - 1:L], start=True, stop=True)
                t_.matmul(small[0:R, 1:2], g.shift[0:R, P:P + R], seg[:, 0:1], start=True, stop=True).then_inc(done, 1)


def segment_softmax(nc, g, group, name, scale=None):
    H = HEADS0
    J = SCAN_LEN
    G = 7
    JG = J // G
    L = J * P
    R = SCAN_ROWS
    with Phase(nc, name) as p:
        a = p.sb("a", [R, L])
        fw_buf, bw = p.sb("fw", [R, L]), p.sb("bw", [R, L])
        fw = fw_buf[:]
        seg = p.sb("seg", [R, L])
        cont = g.cont
        mark = p.sb("mark", [R, L + 1], BF16)
        ends = p.sb("ends", [R, 6])
        erow = p.sb("erow", [1, 4, R])
        crow = p.sb("crow", [1, 2, R])
        carry = p.sb("carry", [R, 2])
        bank = [p.ps(f"bank{j}", [P, 512]) for j in range(G)]
        small = p.ps("small", [P, 512])
        made, pe_done, act_done = p.sem("made"), p.sem("pe_done"), p.sem("act_done")
        dve_note, banked = p.sem("dve_note"), p.sem("banked")
        heads = g.score[:].rearrange("p (c j) (q h) -> p q j c h", j=J, q=2)[:, group]
        by_scan = p.sb("by_scan", [P, J, SCANS, H])
        score = by_scan[:].rearrange("p j c h -> p j (c h)")

        if scale is not None:
            extra, extra_in = p.sb("extra", [R, L]), p.sem("extra_in")

        with p.block() as block:
            if scale is not None:
                @block.sync
                def _(sp):
                    sp.dma_start(extra[:], g.edge_rows[group].rearrange("c h l -> (c h) l")).then_inc(extra_in, 16)

            @block.vector
            def _(dve):
                v, ch = nc.vector, Chain(dve, made)
                if scale is not None:
                    v.tensor_scalar(by_scan[:], heads, scale, None, ALU.mult).then_inc(dve_note, 1)
                else:
                    v.tensor_copy(by_scan[:], heads).then_inc(dve_note, 1)
                ch(v.tensor_scalar(mark[:], cont[:], 1.0, BIG, ALU.subtract, ALU.mult))
                ch(v.tensor_copy(ends[:, 2:4], g.all_cont[:]))
                dve.wait_ge(act_done, 1)
                if scale is not None:
                    dve.wait_ge(extra_in, 16)
                    ch(v.tensor_tensor(a[:], a[:], extra[:], ALU.add))

                def scans(data0, data1, starts, op0, op1):
                    v.tensor_tensor_scan(out=fw, data0=data0[:, 0:L], data1=data1[:], initial=starts[0],
                                         op0=op0, op1=op1).then_inc(dve_note, 1)
                    v.tensor_tensor_scan(out=bw[:, ::-1], data0=data0[:, L:0:-1], data1=data1[:, ::-1], initial=starts[1],
                                         op0=op0, op1=op1).then_inc(dve_note, 1)

                def carries(note, op0, op1, first, of_mask):
                    dve.wait_ge(dve_note, note)
                    ch(v.tensor_copy(ends[:, 0:1], fw[:, L - 1:L]))
                    v.tensor_copy(ends[:, 1:2], bw[:, 0:1]).then_inc(dve_note, 1)
                    dve.wait_ge(pe_done, 1 if of_mask else 3)
                    ch(v.tensor_copy(erow[:].rearrange("p a r -> p (a r)"), small[0:1, 0:4 * R]))
                    if of_mask:
                        ch(v.tensor_scalar(erow[:, 2:4, :], erow[:, 2:4, :], 1.0, BIG, ALU.subtract, ALU.mult))
                    ch.later(v.memset(crow[:, 0, 0:H], first))
                    ch.later(v.memset(crow[:, 1, R - H:R], first))
                    for h in range(H):
                        scan = ch.later if h < H - 1 else ch
                        ch.later(v.tensor_tensor_scan(out=crow[:, 0, H + h:R:H], data0=erow[:, 2, h:R - H:H],
                                                data1=erow[:, 0, h:R - H:H], initial=first, op0=op0, op1=op1))
                        scan(v.tensor_tensor_scan(out=crow[:, 1, h:R - H:H][:, ::-1], data0=erow[:, 3, H + h:R:H][:, ::-1],
                                                data1=erow[:, 1, H + h:R:H][:, ::-1], initial=first, op0=op0, op1=op1))
                    dve.sem_inc(dve_note, 1)
                    dve.wait_ge(pe_done, 2 if of_mask else 4)
                    ch(v.tensor_copy(carry[:], small[0:R, 0:2]))

                scans(mark, a, (-BIG, -BIG), ALU.add, ALU.max)
                carries(3, ALU.add, ALU.max, -BIG, True)
                scans(mark, a, (carry[:, 0:1], carry[:, 1:2]), ALU.add, ALU.max)
                dve.wait_ge(dve_note, 7)
                ch(v.tensor_tensor(fw, fw, bw[:], ALU.max))
                v.tensor_tensor(a[:], a[:], fw, ALU.subtract).then_inc(dve_note, 1)
                dve.wait_ge(act_done, 2)
                scans(cont, seg, (0.0, 0.0), ALU.mult, ALU.add)
                carries(10, ALU.mult, ALU.add, 0.0, False)
                scans(cont, seg, (carry[:, 0:1], carry[:, 1:2]), ALU.mult, ALU.add)
                dve.wait_ge(dve_note, 14)
                ch(v.tensor_tensor(fw, fw, bw[:], ALU.add))
                ch(v.tensor_tensor(fw, fw, seg[:], ALU.subtract))
                for j in range(G + 1):
                    if j < G:
                        at = slice(j * JG * P, (j + 1) * JG * P)
                        ch.later(v.reciprocal(bw[:, at], fw[:, at]))
                    if j:
                        dve.wait_ge(made, ch.base + ch.n - (1 if j < G else 0))
                        before = slice((j - 1) * JG * P, j * JG * P)
                        v.tensor_tensor(a[:, before], seg[:, before], bw[:, before], ALU.mult).then_inc(dve_note, 1)

            @block.tensor
            def _(pe):
                t_ = nc.tensor
                pe.wait_ge(dve_note, 1)
                for j in range(J):
                    at = bank[j // JG][0:R, (j % JG) * P:(j % JG + 1) * P]
                    mm = t_.transpose(at, score[:, j], g.ident[:])
                    if j % JG == JG - 1:
                        mm.then_inc(banked, 1)
                for note in (4, 11):
                    pe.wait_ge(dve_note, note)
                    for j in range(4):
                        mm = t_.matmul(small[0:1, j * R:(j + 1) * R], ends[:, j:j + 1], g.ident[0:R, 0:R], start=True, stop=True)
                    mm.then_inc(pe_done, 1)
                    pe.wait_ge(dve_note, note + 1)
                    for j in range(2):
                        mm = t_.matmul(small[0:R, j:j + 1], crow[:, j, :], g.ones[0:1, 0:1], start=True, stop=True)
                    mm.then_inc(pe_done, 1)
                pe.wait_ge(act_done, 1)
                for j in range(J):
                    if j % JG == 0:
                        pe.wait_ge(dve_note, 15 + j // JG)
                    at = bank[j // JG][:, (j % JG) * R:(j % JG + 1) * R]
                    mm = t_.transpose(at, a[:, j * P:(j + 1) * P], g.ident[0:R, 0:R])
                    if j % JG == JG - 1:
                        mm.then_inc(banked, 1)

            @block.scalar
            def _(act):
                for j in range(G):
                    act.wait_ge(banked, j + 1)
                    cp = nc.scalar.copy(a[:, j * JG * P:(j + 1) * JG * P], bank[j][0:R, 0:JG * P])
                cp.then_inc(act_done, 1)
                act.wait_ge(dve_note, 8)
                nc.scalar.activation(seg[:], a[:], ACT.Exp).then_inc(act_done, 1)
                for j in range(G):
                    act.wait_ge(banked, G + j + 1)
                    nc.scalar.copy(heads[:, j * JG:(j + 1) * JG], bank[j][:, 0:JG * R].rearrange("p (j c h) -> p j c h", j=JG, h=H))\
                        .then_inc(act_done, 1)
                act.wait_ge(act_done, 2 + G)


def aggregate(nc, g, table, name, weighted):
    width = D if weighted else MSG
    with Phase(nc, name) as p:
        ring = p.sb("ring", [P, RING, CH, width])
        slots = ring[:].rearrange("p c t d -> p (c t) d")
        slots_of_ones = 4
        oh = p.sb("oh", [P, slots_of_ones, CH, P])
        zeros = p.sb("zeros", [P, 512], BF16)
        sums = p.ps("sums", [P, 7 * 512])
        blocks_of_sums = sums[:, 0:BLOCKS * D].rearrange("p (b d) -> p b d", d=D)
        landed = [p.sem(f"landed{j}") for j in range(RING)]
        cleared, zeroed, ready, marked, stepped = (p.sem(n) for n in ("cleared", "zeroed", "ready", "marked", "stepped"))
        turn, kept = p.sem("turn"), p.sem("kept")
        if not weighted:
            node_row, loaded = p.sb("node_row", [P, NP]), p.sem("loaded")
            blocks = node_row[:].rearrange("p (b n) -> p b n", n=P)
        in_tail = lambda i: isinstance(i, int) and i == LAPS
        VECTOR_STEPS = 4
        subtracted = p.sem("subtracted")

        with p.block() as block:
            @block.sync
            def _(sp):
                if not weighted:
                    sp.dma_start(node_row[:], g.ins["c_node"]).then_inc(loaded, 16)

                def chunk(i, j, steps):
                    c = i * RING + j
                    if not in_tail(i):
                        if not isinstance(i, int):
                            sp.wait_ge(stepped, c - RING + LAG + 1)
                            sp.sem_inc(turn, 1)
                        sp.dma_start(ring[:, j], g.values[:, bass.ds(c * CH, CH), :] if weighted else
                                     g.messages.rearrange("(c t p) w -> c p t w", p=P, t=CH)[bass.ds(c, 1)].rearrange("c p t w -> (c p) t w"))\
                            .then_inc(landed[j], 16)

                laps(sp, chunk, tail=False)

            if not weighted:
                @block.gpsimd
                def _(pool):
                    pool.wait_ge(loaded, 16)

                    def mark(i, j, steps):
                        c, h = i * RING + j, j % slots_of_ones
                        wait(pool, stepped, c - slots_of_ones + 1)
                        if not in_tail(i):
                            pool.wait_ge(landed[j], i * 16 + 16)
                        pool.sem_inc(turn, 1)
                        for k, (_, slot, node, _) in enumerate(path_words(nc, pool, table, c, steps)):
                            if k >= VECTOR_STEPS:
                                ins = nc.gpsimd.tensor_tensor(
                                    oh[:, h, k, :], flat(blocks[:, bass.ds(node, 1), :]),
                                    flat(slots[:, bass.ds(slot, 1), D:D + 1]).to_broadcast((P, P)), ALU.subtract)
                        if steps > VECTOR_STEPS:
                            ins.then_inc(subtracted, 1)

                    laps(pool, mark)
            else:
                @block.gpsimd
                def _(pool):
                    def weigh(i, j, steps):
                        pool.wait_ge(landed[j], i * 16 + 16)
                        rows = ring[:, j].rearrange("p t (h d) -> p t h d", h=HEADS0)
                        w = g.score[:, bass.ds((i * RING + j) * CH, CH), 0:HEADS0]
                        nc.gpsimd.tensor_tensor(rows, rows, spread(w, 3, D // HEADS0), ALU.mult)\
                            .then_inc(ready, 1)

                    laps(pool, weigh, tail=False, peel=False)

            @block.vector
            def _(dve):
                v = nc.vector
                v.memset(zeros[:], 0.0).then_inc(cleared, 1)
                if not weighted:
                    dve.wait_ge(loaded, 16)

                def mark(i, j, steps):
                    c, h = i * RING + j, j % slots_of_ones
                    wait(dve, stepped, c - slots_of_ones + 1)
                    if weighted:
                        mark_steps(nc, g, oh[:, h, 0:steps], c * CH, steps).then_inc(marked, 1)
                        return
                    if not in_tail(i):
                        dve.wait_ge(landed[j], i * 16 + 16)
                    dve.sem_inc(turn, 1)
                    for k, (_, slot, node, _) in enumerate(path_words(nc, dve, table, c, steps)):
                        if k < VECTOR_STEPS:
                            ins = v.tensor_scalar(oh[:, h, k, :], flat(blocks[:, bass.ds(node, 1), :]),
                                                  flat(slots[:, bass.ds(slot, 1), D:D + 1]), None, ALU.is_equal)
                    if steps > VECTOR_STEPS:
                        dve.wait_ge(subtracted, c + 1)
                        rest = oh[:, h, VECTOR_STEPS:steps, :]
                        ins = v.tensor_single_scalar(rest, rest, 0.0, ALU.is_equal)
                    ins.then_inc(marked, 1)

                laps(dve, mark)
                dve.wait_ge(stepped, CHUNKS + TAIL)
                v.tensor_copy(g.agg[:], blocks_of_sums).then_inc(kept, 1)
                dve.wait_ge(kept, 1)

            @block.tensor
            def _(pe):
                pe.wait_ge(cleared, 1)
                for j in range(7):
                    nc.tensor.matmul(sums[:, j * 512:(j + 1) * 512], zeros[:, 0:P], zeros[:], start=True, stop=True).then_inc(zeroed, 1)

                def chunk(i, j, steps):
                    c, h = i * RING + j, j % slots_of_ones
                    pe.wait_ge(marked, c + 1)
                    if weighted and not in_tail(i):
                        pe.wait_ge(ready, c + 1)
                    pe.sem_inc(turn, 1)
                    for k, (_, slot, node, _) in enumerate(path_words(nc, pe, table, c, steps)):
                        mm = nc.tensor.matmul(flat(blocks_of_sums[:, bass.ds(node, 1), :]), oh[:, h, k, :],
                                              flat(slots[:, bass.ds(slot, 1), 0:D]), start=False, stop=True, skip_group_check=True)
                    mm.then_inc(stepped, 1)

                laps(pe, chunk)


def typed_update(nc, g, layer, x, y):
    with Phase(nc, f"upd{layer}") as p:
        xm = p.sb("xm", [P, TYPES, GROUP, D])
        xt = p.sb("xt", [P, GROUP, TYPES, D])
        rest, gated = p.sb("rest", [P, GROUP, D]), p.sb("gated", [P, GROUP, D])
        keep = p.sb("keep", [P, BLOCKS])
        pt, ph = p.ps("pt", [P, 2048]), p.ps("ph", [P, 1024])
        masked, turned, xt_ready, projected = p.sem("masked"), p.sem("turned"), p.sem("xt_ready"), p.sem("projected")
        chain, updated = p.sem("chain"), p.sem("updated")
        with p.block() as block:
            @block.vector
            def _(dve):
                v, ch = nc.vector, Chain(dve, chain)
                ch(v.tensor_scalar(keep[:], g.gate[:, layer, :], -1.0, 2.0, ALU.mult, ALU.add))

                def mask(n):
                    wait(dve, turned, n)
                    for t in range(TYPES):
                        v.tensor_tensor(xm[:, t], g.agg[:, bass.ds(n * GROUP, GROUP), :],
                                        spread(g.mask[:, t, bass.ds(n * GROUP, GROUP)], 2, D), ALU.mult).then_inc(masked, 1)

                def update(n):
                    at = bass.ds(n * GROUP, GROUP)
                    wait(dve, updated, n)
                    ch(v.tensor_tensor(rest[:], x[:, at, :], spread(keep[:, at], 2, D), ALU.mult))
                    dve.wait_ge(projected, n + 1)
                    ch(v.tensor_tensor(gated[:], ph[:, 0:GROUP * D].rearrange("p (b d) -> p b d", d=D),
                                       spread(g.gate[:, layer, at], 2, D), ALU.mult))
                    v.tensor_tensor(y[:, at, :], gated[:], rest[:], ALU.add).then_inc(updated, 1)

                mask(0)
                with dve.Fori(0, GROUPS - 1) as n:
                    ch.enter(n, 2)
                    mask(n + 1)
                    update(n)
                ch.leave(GROUPS - 1)
                update(GROUPS - 1)

            @block.tensor
            def _(pe):
                t_ = nc.tensor

                def turn_rows(n):
                    wait(pe, xt_ready, n)
                    pe.wait_ge(masked, n * TYPES + TYPES)
                    for b in range(GROUP):
                        for t in range(TYPES):
                            mm = t_.transpose(pt[:, (b * TYPES + t) * D:(b * TYPES + t + 1) * D], xm[:, t, b, :], g.ident[:])
                    mm.then_inc(turned, 1)

                def project(n):
                    wait(pe, updated, n)
                    pe.wait_ge(xt_ready, n + 1)
                    for b in range(GROUP):
                        for t in range(TYPES):
                            mm = t_.matmul(ph[:, b * D:(b + 1) * D], xt[:, b, t, :], g.typed(3, layer, t), start=(t == 0), stop=(t == TYPES - 1))
                    mm.then_inc(projected, 1)

                turn_rows(0)
                with pe.Fori(0, GROUPS - 1) as n:
                    project(n)
                    turn_rows(n + 1)
                project(GROUPS - 1)

            @block.scalar
            def _(act):
                with act.Fori(0, GROUPS) as n:
                    act.wait_ge(projected, n)
                    act.wait_ge(turned, n + 1)
                    nc.scalar.copy(xt[:].rearrange("p b t d -> p (b t d)"), pt[:, 0:GROUP * TYPES * D]).then_inc(xt_ready, 1)


def plain_tables(nc, g, x):
    with Phase(nc, "tab2") as p:
        xs, xt = p.sb("xs", [P, GROUP, D]), p.sb("xt", [P, GROUP, D])
        qkv = p.sb("qkv", [P, GROUP, 3 * D])
        rest = p.sb("rest", [P, GROUP, D])
        pt, pk = p.ps("pt", [P, 1024]), p.ps("pk", [P, GROUP, 512])
        copied, turned, xt_ready, projected = p.sem("copied"), p.sem("turned"), p.sem("xt_ready"), p.sem("projected")
        qkv_ready, out, chain = p.sem("qkv_ready"), p.sem("out"), p.sem("chain")
        bias = g.rows[:, ROWS.index("bq") * D:(ROWS.index("bq") + 3) * D]
        with p.block() as block:
            @block.vector
            def _(dve):
                v, ch = nc.vector, Chain(dve, chain)

                def take(n):
                    wait(dve, turned, n)
                    v.tensor_scalar(xs[:], x[:, bass.ds(n * GROUP, GROUP), :], 1.0, None, ALU.mult).then_inc(copied, 1)

                def keep(n):
                    at = bass.ds(n * GROUP, GROUP)
                    wait(dve, out, n * 16)
                    dve.wait_ge(projected, n + 1)
                    v.tensor_tensor(qkv[:], pk[:, :, 0:3 * D], spread(bias, 1, GROUP), ALU.add).then_inc(qkv_ready, 1)
                    dve.wait_ge(qkv_ready, n + 1)
                    split(nc, dve, ch, g.q_parts, at, qkv[:, :, D:2 * D], rest[:])
                    split(nc, dve, ch, g.v_parts, at, qkv[:, :, 2 * D:3 * D], rest[:])

                take(0)
                with dve.Fori(0, GROUPS - 1) as n:
                    ch.enter(n, 8)
                    take(n + 1)
                    keep(n)
                ch.leave(GROUPS - 1)
                keep(GROUPS - 1)

            @block.tensor
            def _(pe):
                def turn_rows(n):
                    wait(pe, xt_ready, n)
                    pe.wait_ge(copied, n + 1)
                    for b in range(GROUP):
                        mm = nc.tensor.transpose(pt[:, b * D:(b + 1) * D], xs[:, b, :], g.ident[:])
                    mm.then_inc(turned, 1)

                def project(n):
                    wait(pe, qkv_ready, n)
                    pe.wait_ge(xt_ready, n + 1)
                    for b in range(GROUP):
                        mm = nc.tensor.matmul(pk[:, b, 0:3 * D], xt[:, b, :], g.wqkv[:], start=True, stop=True)
                    mm.then_inc(projected, 1)

                turn_rows(0)
                with pe.Fori(0, GROUPS - 1) as n:
                    project(n)
                    turn_rows(n + 1)
                project(GROUPS - 1)

            @block.scalar
            def _(act):
                with act.Fori(0, GROUPS) as n:
                    act.wait_ge(projected, n)
                    act.wait_ge(turned, n + 1)
                    nc.scalar.copy(flat(xt[:]), pt[:, 0:GROUP * D]).then_inc(xt_ready, 1)

            @block.sync
            def _(sp):
                with sp.Fori(0, GROUPS) as n:
                    sp.wait_ge(qkv_ready, n + 1)
                    sp.dma_start(g.q_tab[bass.ds(n * (GROUP * P), GROUP * P), :].rearrange("(b p) w -> p b w", p=P),
                                 qkv[:, :, 0:D]).then_inc(out, 16)
                sp.wait_ge(out, GROUPS * 16)


def scatter_messages(nc, g):
    with Phase(nc, "msg") as p:
        ring = p.sb("ring", [P, BANKS, QUAD, MSG])
        idx = p.sb("idx", [P, BANKS, QUAD], I32)
        zeros = p.sb("zeros", [P, 512], BF16)
        value_rows = p.ps("value_rows", [P, BANKS * QUAD, P])
        ones = OneHots(nc, g, p)
        scattered = [p.sem(f"scattered{j}") for j in range(BANKS)]
        multiplied, weighed, named, cleared, turn = (p.sem(n) for n in ("multiplied", "weighed", "named", "cleared", "turn"))
        per = 16 * QUAD
        in_tail = lambda i: isinstance(i, int) and i == QUAD_LAPS
        last = lambda i, j: in_tail(i) and j == QUAD_TAIL - 1
        near_end = lambda i, j: in_tail(i) and j >= QUAD_TAIL - 2
        with p.block() as block:
            @block.tensor
            def _(pe):
                pe.wait_ge(cleared, 1)
                ones.turn(pe, 0, 0).then_inc(ones.flipped, 1)

                def quad(i, j, parity):
                    n = i * BANKS + j
                    if not in_tail(i):
                        if not isinstance(i, int) or i > 0:
                            pe.wait_ge(weighed, n - BANKS + 1)
                        nc.tensor.matmul(value_rows[:, j * QUAD:(j + 1) * QUAD, :].rearrange("p t d -> p (t d)"), zeros[:, 0:P],
                                         zeros[:], start=True, stop=True)
                    pe.wait_ge(ones.copied, n + 1)
                    pe.sem_inc(turn, 1)
                    ones.expand(pe, n, parity, value_rows, g.v_parts).then_inc(multiplied, 1)
                    if not last(i, j):
                        ones.turn(pe, n + 1, 1 - parity).then_inc(ones.flipped, 1)

                quad_laps(pe, quad)

            @block.vector
            def _(dve):
                v = nc.vector
                v.memset(zeros[:], 0.0).then_inc(cleared, 1)
                v.memset(ring[:, :, :, D + 1:MSG], 0.0).then_inc(cleared, 1)
                ones.mark(dve, 0, 0)
                ones.mark(dve, 1, 1)
                dve.wait_ge(cleared, 2)

                def quad(i, j, parity):
                    n = i * BANKS + j
                    if isinstance(i, int) and n < QUAD_LAG:
                        ones.mark(dve, n + 2, parity)
                        return
                    m, slot, lap = finished_quad(i, j)
                    dve.wait_ge(multiplied, n + 1)
                    wait(dve, scattered[slot], lap * per)
                    dve.sem_inc(turn, 1)
                    v.tensor_tensor(ring[:, slot, :, 0:D].rearrange("p t (h d) -> p t h d", h=HEADS1),
                                    value_rows[:, slot * QUAD:(slot + 1) * QUAD, :].rearrange("p t (h d) -> p t h d", h=HEADS1),
                                    spread(g.score[:, bass.ds(m * QUAD, QUAD), :], 3, D // HEADS1), ALU.mult).then_inc(weighed, 1)
                    if not near_end(i, j):
                        ones.mark(dve, n + 2, parity)

                quad_laps(dve, quad)

            @block.scalar
            def _(act):
                act.wait_ge(cleared, 2)

                def quad(i, j, parity):
                    n = i * BANKS + j
                    ones.keep(act, multiplied, n, parity).then_inc(ones.copied, 1)
                    if isinstance(i, int) and n < QUAD_LAG:
                        return
                    m, slot, lap = finished_quad(i, j)
                    wait(act, scattered[slot], lap * per)
                    act.sem_inc(turn, 1)
                    nc.scalar.copy(ring[:, slot, :, D], g.src[:, bass.ds(m * QUAD, QUAD)]).then_inc(named, 1)
                    nc.scalar.copy(idx[:, slot, :], g.pos[:, bass.ds(m * QUAD, QUAD)]).then_inc(named, 1)

                quad_laps(act, quad)

            @block.gpsimd
            def _(pool):
                def quad(i, j, parity):
                    n = i * BANKS + j
                    pool.wait_ge(weighed, n + 1)
                    pool.wait_ge(named, n * 2 + 2)
                    pool.sem_inc(turn, 1)
                    for k in range(QUAD):
                        nc.gpsimd.indirect_dma_start(
                            out=g.messages, out_offset=bass.IndirectOffsetOnAxis(ap=idx[:, j, k:k + 1], axis=0),
                            in_=ring[:, j, k, :], in_offset=None).then_inc(scattered[j], 16)

                quad_laps(pool, quad, tail=False, peel=False)
                for j in range(BANKS):
                    pool.wait_ge(scattered[j], QUAD_LAPS * per)


def output_projection(nc, g, x, y):
    with Phase(nc, "proj") as p:
        xs, xt = p.sb("xs", [P, GROUP, D]), p.sb("xt", [P, GROUP, D])
        pt, ph = p.ps("pt", [P, 1024]), p.ps("ph", [P, 1024])
        copied, turned, xt_ready, projected, updated = (p.sem(n) for n in ("copied", "turned", "xt_ready", "projected", "updated"))
        made = p.sem("made")
        with p.block() as block:
            @block.vector
            def _(dve):
                with dve.Fori(0, GROUPS) as n:
                    at = bass.ds(n * GROUP, GROUP)
                    dve.wait_ge(turned, n)
                    nc.vector.tensor_scalar(xs[:], g.agg[:, at, :], 1.0, None, ALU.mult).then_inc(copied, 1)
                    dve.wait_ge(projected, n + 1)
                    nc.vector.tensor_tensor(y[:, at, :], ph[:, 0:GROUP * D].rearrange("p (b d) -> p b d", d=D),
                                            x[:, at, :], ALU.add).then_inc(updated, 1)
                dve.wait_ge(updated, GROUPS)
                nc.vector.tensor_tensor(y[:], y[:], spread(g.row("bo"), 1, BLOCKS), ALU.add).then_inc(made, 1)
                dve.wait_ge(made, 1)

            @block.tensor
            def _(pe):
                with pe.Fori(0, GROUPS) as n:
                    pe.wait_ge(xt_ready, n)
                    pe.wait_ge(copied, n + 1)
                    for b in range(GROUP):
                        mm = nc.tensor.transpose(pt[:, b * D:(b + 1) * D], xs[:, b, :], g.ident[:])
                    mm.then_inc(turned, 1)
                    pe.wait_ge(updated, n)
                    pe.wait_ge(xt_ready, n + 1)
                    for b in range(GROUP):
                        mm = nc.tensor.matmul(ph[:, b * D:(b + 1) * D], xt[:, b, :], g.wo[:], start=True, stop=True)
                    mm.then_inc(projected, 1)

            @block.scalar
            def _(act):
                with act.Fori(0, GROUPS) as n:
                    act.wait_ge(projected, n)
                    act.wait_ge(turned, n + 1)
                    nc.scalar.copy(flat(xt[:]), pt[:, 0:GROUP * D]).then_inc(xt_ready, 1)


def feed_forward(nc, g, xn, x2, x1, y, out):
    with Phase(nc, "ffn") as p:
        xs, xt = p.sb("xs", [P, GROUP, D]), p.sb("xt", [P, GROUP, D])
        hid = p.sb("hid", [P, GROUP, 4, P])
        pt, p1 = p.ps("pt", [P, 1024]), p.ps("p1", [P, GROUP, 4, P])
        copied, turned, xt_ready, opened, hid_ready, closed, updated = (
            p.sem(n) for n in ("copied", "turned", "xt_ready", "opened", "hid_ready", "closed", "updated"))
        made, stored = p.sem("made"), p.sem("stored")
        width = GROUP * P
        with p.block() as block:
            @block.vector
            def _(dve):
                ch = Chain(dve, made)
                ch(nc.vector.tensor_tensor(x2[:], x2[:], x1[:], ALU.add))
                ch(nc.vector.tensor_tensor(x2[:], x2[:], spread(g.row("b2"), 1, BLOCKS), ALU.add))
                nc.vector.tensor_scalar(xs[:], xn[:, 0:GROUP, :], 1.0, None, ALU.mult).then_inc(copied, 1)

                def add(n):
                    dve.wait_ge(closed, n + 1)
                    nc.vector.tensor_tensor(y[:, bass.ds(n * GROUP, GROUP), :],
                                            pt[:, 0:width].rearrange("p (b d) -> p b d", d=D),
                                            x2[:, bass.ds(n * GROUP, GROUP), :], ALU.add).then_inc(updated, 1)

                with dve.Fori(0, GROUPS - 1) as n:
                    dve.wait_ge(turned, n + 1)
                    nc.vector.tensor_scalar(xs[:], xn[:, bass.ds(n * GROUP + GROUP, GROUP), :], 1.0, None, ALU.mult).then_inc(copied, 1)
                    add(n)
                add(GROUPS - 1)

            @block.tensor
            def _(pe):
                t_ = nc.tensor
                with pe.Fori(0, GROUPS) as n:
                    pe.wait_ge(updated, n)
                    pe.wait_ge(copied, n + 1)
                    for b in range(GROUP):
                        mm = t_.transpose(pt[:, b * D:(b + 1) * D], xs[:, b, :], g.ident[:])
                    mm.then_inc(turned, 1)
                    pe.wait_ge(hid_ready, n * GROUP)
                    pe.wait_ge(xt_ready, n + 1)
                    for b in range(GROUP):
                        for j in range(4):
                            mm = t_.matmul(p1[:, b, j, :], g.w1[:, j * P:(j + 1) * P], xt[:, b, :], start=True, stop=True)
                        mm.then_inc(opened, 1)
                    for b in range(GROUP):
                        pe.wait_ge(hid_ready, n * GROUP + b + 1)
                        for j in range(4):
                            mm = t_.matmul(pt[:, b * D:(b + 1) * D], hid[:, b, j, :], g.w2[:, j * D:(j + 1) * D],
                                           start=(j == 0), stop=(j == 3))
                    mm.then_inc(closed, 1)

            @block.scalar
            def _(act):
                with act.Fori(0, GROUPS) as n:
                    act.wait_ge(opened, n * GROUP)
                    act.wait_ge(turned, n + 1)
                    nc.scalar.copy(flat(xt[:]), pt[:, 0:width]).then_inc(xt_ready, 1)
                    act.wait_ge(closed, n)
                    for b in range(GROUP):
                        act.wait_ge(opened, n * GROUP + b + 1)
                        for j in range(4):
                            relu = nc.scalar.activation(hid[:, b, j, :], p1[:, b, j, :], ACT.Relu, bias=g.b1[:, j:j + 1])
                        relu.then_inc(hid_ready, 1)

            @block.sync
            def _(sp):
                sp.wait_ge(updated, GROUPS)
                sp.dma_start(out, flat(y[:])).then_inc(stored, 16)
                sp.wait_ge(stored, 16)


class Graph:

    def __init__(self, nc, stack, ins):
        self.ins = ins

        def sb(name, shape, dt=F32):
            return stack.enter_context(nc.sbuf_tensor(name, shape, dt))

        self.ident, self.tri = sb("ident", [P, P]), sb("tri", [P, P])
        self.ident_bf = sb("ident_bf", [P, P], BF16)
        self.tri_bf, self.ones_bf = sb("tri_bf", [P, P], BF16), sb("ones_bf", [P, P], BF16)
        self.ones = sb("ones", [P, 2])
        self.iota = sb("iota", [P, P])
        self.iota_bf = sb("iota_bf", [P, P], BF16)
        self.shift = sb("shift", [P, 2 * P])
        typed, rels = 4 * LAYERS * TYPES * D, 2 * LAYERS * RELS * D
        self.layer_weights = sb("layer_weights", [P, typed + rels])
        self.wtyped, self.wrel = self.layer_weights[:, 0:typed], self.layer_weights[:, typed:typed + rels]
        self.wqkv, self.wo = sb("wqkv", [P, 3 * D]), sb("wo", [P, D])
        self.w1, self.w2 = sb("w1", [P, HID]), sb("w2", [P, HID])
        self.wc, self.b1, self.bc = sb("wc", [P, HEADS1]), sb("b1", [P, 4]), sb("bc", [HEADS1, 1])
        self.rows = sb("rows", [P, len(ROWS) * D])
        self.mask, self.gate = sb("mask", [P, TYPES, BLOCKS]), sb("gate", [P, LAYERS, BLOCKS])
        self.mixw = sb("mixw", [P, 2])
        self.pri = sb("pri", [P, LAYERS * RELS])
        self.weights_in = nc.alloc_semaphore("weights_in")
        self.unordered = sb("unordered", [1, 1], I32)
        self.tab_dst = sb("tab_dst", [1, 4 * STEPS], I32)
        self.rel_idx, self.src_idx = (sb(n, [P, TILES], I32) for n in ("rel_idx", "src_idx"))
        self.pos = sb("pos", [P, TILES], I32)
        self.dst, self.src = (sb(n, [P, TILES]) for n in ("dst", "src"))
        self.near_dst = sb("near_dst", [P, STEPS], BF16)
        self.number = sb("number", [P, TILES], I32)
        self.cont = sb("cont", [SCAN_ROWS, SCAN_LEN * P + 1], BF16)
        self.all_cont = sb("all_cont", [SCAN_ROWS, 2])

        def dram(name, shape, dt=F32):
            return nc.dram_tensor(name, shape, dt, kind="Internal").ap()

        self.tab_src = dram("tab_src", [1, 4 * STEPS], I32)
        self.rec_a, self.rec_b = dram("rec_a", [EP, REC]), dram("rec_b", [EP, REC])
        self.rel_tab, self.q_tab = dram("rel_tab", [NP * RELS, 2 * D]), dram("q_tab", [NP, D])
        self.edge_rows = dram("edge_rows", [2, SCANS, HEADS0, SCAN_LEN * P])
        self.by_edge = dram("by_edge", [EP, HEADS1])
        self.values, self.messages = dram("values", [P, TILES, D]), dram("messages", [EP, MSG])

    def node_buffers(self, nc, stack):
        self.agg, self.xa, self.xb = (
            stack.enter_context(nc.sbuf_tensor(n, [P, BLOCKS, D], F32)) for n in ("agg", "xa", "xb"))
        self.q_parts = stack.enter_context(nc.sbuf_tensor("q_parts", [P, BLOCKS, 3, D], BF16))
        self.score = stack.enter_context(nc.sbuf_tensor("score", [P, TILES, HEADS1], F32))

    def row(self, name):
        at = ROWS.index(name)
        return self.rows[:, at * D:(at + 1) * D]

    def typed(self, which, layer, t):
        at = (which * LAYERS + layer) * TYPES + t
        return self.wtyped[:, at * D:(at + 1) * D]

    def relation(self, which, layer):
        at = (2 * layer + which) * RELS
        return self.wrel[:, at * D:(at + RELS) * D]


def build_program(nc, ins, out):
    with ExitStack() as stack:
        g = Graph(nc, stack, ins)
        with ExitStack() as sorting:
            g.rec = sorting.enter_context(nc.sbuf_tensor("rec", [P, TILES, REC], F32))
            g.keys = sorting.enter_context(nc.sbuf_tensor("keys", [P, TILES], F32))
            g.dst_rows = sorting.enter_context(nc.sbuf_tensor("dst_rows_sb", [P, TILES + 1], I32))
            g.steprow = sorting.enter_context(nc.sbuf_tensor("steprow", [BLOCKS, STEPS], F32))
            load_inputs(nc, g)
            count_inversions(nc, g)
            unordered = nc.values_load(g.unordered[0:1, 0:1], min_val=0, max_val=EP,
                                       skip_runtime_bounds_check_because="a count of edges")
            with nc.If(unordered > 0):
                with nc.sbuf_tensor("before", [P, 1 + LO * TILES], F32) as before:
                    digits(nc, g, 1, "lo", and_with=LO - 1)
                    count_keys(nc, g, LO, before, "count_lo")
                    place_keys(nc, g, LO, before, "place_lo", records_to=g.rec_a)
                    read_records(nc, g, g.rec_a, "read_a")
                    digits(nc, g, 1, "hi", shift=6)
                    count_keys(nc, g, HI, before, "count_hi")
                    place_keys(nc, g, HI, before, "place_hi", records_to=g.rec_b)
                    read_records(nc, g, g.rec_b, "read_b")
            with nc.Else():
                nc.all_engine_barrier()
            nc.all_engine_barrier()
            with nc.sbuf_tensor("before_blocks", [P, 1 + BLOCKS * TILES], F32) as before:
                digits(nc, g, 1, "dst_block", shift=7)
                with nc.sbuf_tensor("starts", [1, BLOCKS], F32) as starts:
                    count_blocks(nc, g, starts[:], "count_dst")
                    path_table(nc, g, starts[:], g.tab_dst, "path_dst")
                digits(nc, g, 0, "src_block", shift=7)
                count_keys(nc, g, BLOCKS, before, "count_src")
                place_keys(nc, g, BLOCKS, before, "place_src", positions=g.pos, edge_attributes=True)
                with nc.sbuf_tensor("tab_src_sb", [1, 4 * STEPS], I32) as tab:
                    starts = before[0:1, 0:BLOCKS * TILES].rearrange("p (g t) -> p g t", t=TILES)[:, :, 0]
                    path_table(nc, g, starts, tab, "path_src")
                    copy_over(nc, g.tab_src, tab[:], "tab_src_out")
            edge_indices(nc, g)
        with nc.If(unordered > 0):
            with nc.sbuf_tensor("edge_sc", [P, TILES, HEADS1], F32) as g.edge_sc:
                turn_edge_scores(nc, g, "to_columns", True)
                sort_edge_scores(nc, g)
                turn_edge_scores(nc, g, "to_rows", False)
        with nc.Else():
            nc.all_engine_barrier()
        nc.all_engine_barrier()
        g.node_buffers(nc, stack)
        local_targets(nc, g)
        segment_bounds(nc, g)
        v = nc.vector

        norm_phase(nc, g, "norm_in", lambda dve, ch, ln: ln.vector(dve, ch, g.xa, g.xb, relu=True), 1)
        x, y = g.xa, g.xb
        for l in range(LAYERS):
            typed_tables(nc, g, l, x)
            gather_scores(nc, g, HEADS0, True, g.rel_tab, g.rel_idx, g.q_parts, f"scores{l}")
            segment_softmax(nc, g, 0, f"softmax{l}")
            aggregate(nc, g, g.tab_dst, f"agg{l}", True)
            typed_update(nc, g, l, x, y)
            norm_phase(nc, g, f"norm{l}",
                       lambda dve, ch, ln, y=y, l=l: ln.vector(dve, ch, y, y, f"ln_g{l}", f"ln_b{l}"), 1)
            x, y = y, x

        g.x1 = g.layer_weights[:, 0:BLOCKS * D].rearrange("p (b d) -> p b d", d=D)

        def mix(dve, ch, ln):
            ch(v.tensor_scalar(g.xa[:], g.xa[:], g.mixw[:, 1:2], None, ALU.mult))
            ch(v.scalar_tensor_tensor(g.xa[:], g.xb[:], g.mixw[:, 0:1], g.xa[:], ALU.mult, ALU.add))
            ln.vector(dve, ch, g.xa, g.xa, "agg_g", "agg_b")
            dve.wait_ge(ln.loaded, 16)
            ch(v.tensor_tensor(g.x1[:], g.x1[:], g.xa[:], ALU.add))
            ln.vector(dve, ch, g.xb, g.x1, relu=True)
            ln.vector(dve, ch, g.xa, g.xb, "g1", "be1")

        norm_phase(nc, g, "mix", mix, 3, load=(g.x1[:], g.ins["x"].rearrange("p (b d) -> p b d", d=D)))
        with nc.sbuf_tensor("v_parts", [P, BLOCKS, 3, D], BF16) as g.v_parts:
            plain_tables(nc, g, g.xa)
            gather_scores(nc, g, HEADS1, False, g.q_tab, g.src_idx, g.q_parts, "scores2")
            for group in range(2):
                segment_softmax(nc, g, group, f"softmax2_{group}", scale=float(D // HEADS1) ** -0.5)
            scatter_messages(nc, g)
        with nc.sbuf_tensor("tab_src_in", [1, 4 * STEPS], I32) as tab:
            copy_over(nc, tab[:], g.tab_src, "tab_src_back")
            aggregate(nc, g, tab, "agg2", False)
        output_projection(nc, g, g.xb, g.xb)
        norm_phase(nc, g, "norm2", lambda dve, ch, ln: ln.vector(dve, ch, g.xa, g.xb, "g2", "be2"), 1)
        feed_forward(nc, g, g.xa, g.xb, g.x1, g.agg, out)



def constants():
    k = np.arange(P)
    h = HEADS0
    shift = np.zeros((P, 2 * P), np.float32)
    shift[:, 0:P] = k[None, :] == k[:, None] + h
    shift[:, P:] = k[None, :] == k[:, None] - h
    return {
        "c_ident": np.eye(P, dtype=np.float32),
        "c_tri": (k[:, None] < k[None, :]).astype(np.float32),
        "c_iota": np.tile(np.arange(P, dtype=np.float32), (P, 1)),
        "c_shift": shift,
        "c_node": np.tile(np.arange(NP, dtype=np.float32), (P, 1)),
        "c_step": np.tile(np.arange(STEPS, dtype=np.float32), (BLOCKS, 1)),
    }


def lay_out(inp):
    f = np.float32
    a = {k: np.asarray(v) for k, v in inp.items()}
    arrays = constants()
    x = np.zeros((NP, D), f)
    x[:NODES] = a["x"]
    arrays["x"] = x.reshape(BLOCKS, P, D).transpose(1, 0, 2).reshape(P, BLOCKS * D)
    nt = np.zeros(NP, np.int32)
    nt[:NODES] = a["node_type_3"]
    arrays["ntype"] = nt.reshape(BLOCKS, P).T
    cols = np.zeros((REC, EP), np.int32)
    cols[3] = np.arange(EP)
    cols[0:2] = NP - 1
    cols[0, :EDGES], cols[1, :EDGES], cols[2, :EDGES] = a["src"], a["dst"], a["edge_type_6"]
    arrays["edge_cols"] = cols.reshape(REC, TILES, P).transpose(2, 0, 1).reshape(P, REC * TILES)
    following = np.append(cols[1], cols[1, -1:])
    arrays["dst_rows"] = np.stack([following[r * TILES:(r + 1) * TILES + 1] for r in range(P)])
    ea = np.zeros((D, EP), f)
    ea[:, :EDGES] = a["edge_attr_128"].T
    arrays["edge_attr"] = ea
    typed = np.stack([a["L0_gnn_Wk"], a["L0_gnn_Wv"], a["L0_gnn_Wq"], a["L0_gnn_Wa"]])
    arrays["w_typed"] = typed.reshape(4 * LAYERS * TYPES, D, D).transpose(1, 0, 2).reshape(D, -1)
    dh = D // HEADS0
    rel = np.zeros((LAYERS, 2, RELS, D, D), f)
    for which, name in enumerate(("L0_gnn_W_att", "L0_gnn_W_msg")):
        for h in range(HEADS0):
            rel[:, which, :, h * dh:(h + 1) * dh, h * dh:(h + 1) * dh] = a[name][:, h]
    arrays["w_rel"] = rel.reshape(LAYERS * 2 * RELS, D, D).transpose(1, 0, 2).reshape(D, -1)
    arrays["b_pri"] = np.repeat(a["L0_gnn_pri"].transpose(1, 0, 2).reshape(HEADS0, LAYERS * RELS), dh, 0)
    arrays["w_qkv"] = np.concatenate([a["L1_gnn_Wq"], a["L1_gnn_Wk"], a["L1_gnn_Wv"]], 1)
    arrays["w_o"], arrays["w_1"], arrays["w_c"] = a["L1_gnn_Wo"], a["L1_gnn_W1"], a["L1_gnn_Wc"]
    arrays["w_2"] = a["L1_gnn_W2"].reshape(4, D, D).transpose(1, 0, 2).reshape(D, 4 * D)
    arrays["b_1"] = a["L1_gnn_b1"].reshape(4, D).T
    rows = dict(ln_g0=a["L0_gnn_ln_g"][0], ln_g1=a["L0_gnn_ln_g"][1], ln_b0=a["L0_gnn_ln_b"][0],
                ln_b1=a["L0_gnn_ln_b"][1], agg_g=a["L0_gnn_agg_g"], agg_b=a["L0_gnn_agg_b"])
    for n in ("bq", "bk", "bv", "bo", "b2", "g1", "be1", "g2", "be2"):
        rows[n] = a["L1_gnn_" + n]
    arrays["b_rows"] = np.tile(np.concatenate([rows[n] for n in ROWS])[None], (P, 1))
    arrays["b_c"] = a["L1_gnn_bc"][:, None]
    arrays["b_skip"] = np.tile(a["L0_gnn_skip"].reshape(1, -1), (P, 1))
    arrays["b_aggw"] = np.tile(a["L0_gnn_agg_w"][None], (P, 1))
    return {k: np.ascontiguousarray(v) for k, v in arrays.items()}


def kernel(**inputs):
    import concourse.bacc as _bacc
    from concourse.bass_utils import run_bass_kernel_spmd as _run

    nc = _bacc.Bacc("TRN2", target_bir_lowering=False, num_devices=1)
    arrays = lay_out(inputs)
    ins = {n: nc.dram_tensor(n, v.shape, mybir.dt.from_np(v.dtype), kind="ExternalInput").ap() for n, v in arrays.items()}
    out = nc.dram_tensor("out", (P, BLOCKS * D), F32, kind="ExternalOutput").ap()
    build_program(nc, ins, out)
    r = _run(nc, [arrays], core_ids=[0])
    got = np.asarray(r.results[0]["out"])
    return got.reshape(P, BLOCKS, D).transpose(1, 0, 2).reshape(NP, D)[:NODES]
```
